# Optimizing a Trainium2 kernel written in Bass

```python
import numpy as np
import jax
import jax.numpy as jnp

def _softmax(x, axis=-1):
    return jax.nn.softmax(x, axis=axis)
def _gelu(x):
    return jax.nn.gelu(x, approximate=True)
def _silu(x):
    return jax.nn.silu(x)
def _sigmoid(x):
    return jax.nn.sigmoid(x)
def _layernorm(x, axis=-1, eps=1e-5):
    m = jnp.mean(x, axis=axis, keepdims=True)
    v = jnp.var(x, axis=axis, keepdims=True)
    return (x - m) / jnp.sqrt(v + eps)
def _scatter_add(tgt, idx, src, axis=0):
    return tgt.at[idx].add(src)
def _segment_sum(src, seg, n):
    return jax.ops.segment_sum(src, seg, n)

kernel_name = 'mk_adj_preln_d4_adj_256_09f4ef'

def setup_inputs(seed: int = 0):
    np.random.seed(seed)
    _w = jnp.asarray
    def _rec_inputs():
        import jax
        import jax.numpy as jnp
        _gk = jax.random.key(seed)
        x = -0.000929 + 1 * jax.random.normal(jax.random.fold_in(_gk, 1), (2708, 256), jnp.float32)
        _w = (1.0 + jnp.arange(2708, dtype=jnp.float32)) ** -0.5
        _w = _w / _w.mean()
        _pij = jnp.clip(0.0014771 * _w[:, None] * _w[None, :], 0.0, 1.0)
        _a = jax.random.uniform(jax.random.fold_in(_gk, 2), (2708, 2708)) < _pij
        _a = jnp.logical_or(_a, jnp.eye(2708, dtype=bool))
        _af = _a.astype(jnp.float32)
        adj = _af
        return x, adj
    x, adj = _rec_inputs()
    def _L0_gnn_setup():
        import jax, jax.numpy as jnp
        import numpy as np
        N = 4096
        IN = 256
        F = 64
        H = 4
        key = jax.random.key(seed)
        k1, k2, k3, k4, k5 = jax.random.split(key, 5)
        h = jax.random.normal(k1, (N, IN), jnp.float32)
        adj = jax.random.randint(k2, (N, N), 0, 2).astype(jnp.float32)
        adj = jnp.maximum(adj, jnp.eye(N, dtype=jnp.float32))
        Wm = (jax.random.normal(k3, (IN, H * F), jnp.float32) / np.sqrt(IN)).astype(jnp.float32)
        al = (jax.random.normal(k4, (F,), jnp.float32) / np.sqrt(2 * F)).astype(jnp.float32)
        ar = (jax.random.normal(k5, (F,), jnp.float32) / np.sqrt(2 * F)).astype(jnp.float32)
        return {'h': h, 'adj': adj, 'Wm': Wm, 'al': al, 'ar': ar}
    _L0_gnn_all = _L0_gnn_setup()
    _L0_gnn_in = {k: v for k, v in _L0_gnn_all.items() if k in ('Wm', 'al', 'ar', )}
    del _L0_gnn_all

    def _L1_gnn_setup():
        import jax, jax.numpy as jnp
        import numpy as np
        N, H, HEADS = (4096, 256, 3)
        ALPHA = 0.2
        NEG_INF = -9000000000000000.0

        def _sign_adj(key, n, density):
            k1, k2 = jax.random.split(key)
            mask = jax.random.uniform(k1, (n, n)) < density
            sign = jnp.where(jax.random.uniform(k2, (n, n)) < 0.5, -1.0, 1.0)
            adj = jnp.where(mask, sign, 0.0).astype(jnp.float32)
            idx = jnp.arange(n)
            return adj.at[idx, idx].set(1.0)

        def _gru_cell(x, hstate, Wih, Whh, bih, bhh):
            gi = x @ Wih.T + bih
            gh = hstate @ Whh.T + bhh
            ir, iz, inn = jnp.split(gi, 3, axis=1)
            hr, hz, hn = jnp.split(gh, 3, axis=1)
            r = jax.nn.sigmoid(ir + hr)
            z = jax.nn.sigmoid(iz + hz)
            n = jnp.tanh(inn + r * hn)
            return (1.0 - z) * n + z * hstate

        def _gat_head(h, node_adj, edge_adj, W, a):
            hW = h @ W
            hp = (node_adj > 0).astype(hW.dtype) @ hW
            hm = (node_adj < 0).astype(hW.dtype) @ hW
            e_plus = jax.nn.leaky_relu(jnp.concatenate([hp, hm], axis=1) @ a, ALPHA)[:, 0]
            e_minus = jax.nn.leaky_relu(jnp.concatenate([hm, hp], axis=1) @ a, ALPHA)[:, 0]
            att = jnp.where(edge_adj > 0, e_plus[None, :], NEG_INF)
            att = jnp.where(edge_adj < 0, e_minus[None, :], att)
            att = jax.nn.softmax(att, axis=1)
            return att * edge_adj @ hW
        key = jax.random.key(seed)
        ks = jax.random.split(key, 16)
        std = 0.01
        gain = 1.414
        return {'h': jax.random.normal(ks[0], (N, H), jnp.float32), 'node_adj': _sign_adj(ks[1], N, 0.005), 'edge_adj': _sign_adj(ks[2], N, 0.005), 'gat_W': jax.random.normal(ks[3], (HEADS, H, H), jnp.float32) * (gain / np.sqrt(H, dtype=np.float32)), 'gat_a': jax.random.normal(ks[4], (HEADS, 2 * H, 1), jnp.float32) * 0.1, 'edge_Wih': jax.random.normal(ks[5], (3 * H, H), jnp.float32) * std, 'edge_Whh': jax.random.normal(ks[6], (3 * H, H), jnp.float32) * std, 'edge_bih': jnp.zeros((3 * H,), jnp.float32), 'edge_bhh': jnp.zeros((3 * H,), jnp.float32), 'node_Wih': jax.random.normal(ks[7], (3 * H, H), jnp.float32) * std, 'node_Whh': jax.random.normal(ks[8], (3 * H, H), jnp.float32) * std, 'node_bih': jnp.zeros((3 * H,), jnp.float32), 'node_bhh': jnp.zeros((3 * H,), jnp.float32)}
    _L1_gnn_all = _L1_gnn_setup()
    _L1_gnn_in = {k: v for k, v in _L1_gnn_all.items() if k in ('gat_W', 'gat_a', 'edge_Wih', 'edge_Whh', 'edge_bih', 'edge_bhh', 'node_Wih', 'node_Whh', 'node_bih', 'node_bhh', )}
    del _L1_gnn_all

    def _L2_gnn_setup():
        import jax, jax.numpy as jnp
        import numpy as np
        N = 16384
        D = 256
        OUT = 256
        key = jax.random.key(seed)
        k1, k2, k3 = jax.random.split(key, 3)
        features = jax.random.normal(k1, (N, D), dtype=jnp.float32)
        adj = jax.random.uniform(k2, (N, N), dtype=jnp.float32)
        W = jax.random.normal(k3, (OUT, 2 * D), dtype=jnp.float32)
        return {'features': features, 'adj': adj, 'W': W}
    _L2_gnn_all = _L2_gnn_setup()
    _L2_gnn_in = {k: v for k, v in _L2_gnn_all.items() if k in ('W', )}
    del _L2_gnn_all

    def _L3_gnn_setup():
        import jax, jax.numpy as jnp
        import numpy as np
        N = 8192
        D = 256
        CUTOFF = 1.0
        MU = 1.0
        SIGMA = 0.5

        def sensitivity(r, mu, sigma):
            return jnp.exp(-(1.0 / r - 1.0 / mu) ** 2 / (2.0 * sigma * sigma))
        key = jax.random.key(seed)
        k_z, k_d, k_w = jax.random.split(key, 3)
        z = jax.random.normal(k_z, (N, D), dtype=jnp.float32)
        dist_matrix = jax.random.uniform(k_d, (N, N), dtype=jnp.float32) * 2.0 + 0.05
        W = jax.random.normal(k_w, (D, D), dtype=jnp.float32)
        B = jnp.zeros((D,), dtype=jnp.float32)
        return {'z': z, 'dist_matrix': dist_matrix, 'W': W, 'B': B}
    _L3_gnn_all = _L3_gnn_setup()
    _L3_gnn_in = {k: v for k, v in _L3_gnn_all.items() if k in ('W', 'B', )}
    del _L3_gnn_all

    return {
        "x": x,
        "adj": adj,
        "L0_gnn_Wm": _L0_gnn_in["Wm"],
        "L0_gnn_al": _L0_gnn_in["al"],
        "L0_gnn_ar": _L0_gnn_in["ar"],
        "L1_gnn_gat_W": _L1_gnn_in["gat_W"],
        "L1_gnn_gat_a": _L1_gnn_in["gat_a"],
        "L1_gnn_edge_Wih": _L1_gnn_in["edge_Wih"],
        "L1_gnn_edge_Whh": _L1_gnn_in["edge_Whh"],
        "L1_gnn_edge_bih": _L1_gnn_in["edge_bih"],
        "L1_gnn_edge_bhh": _L1_gnn_in["edge_bhh"],
        "L1_gnn_node_Wih": _L1_gnn_in["node_Wih"],
        "L1_gnn_node_Whh": _L1_gnn_in["node_Whh"],
        "L1_gnn_node_bih": _L1_gnn_in["node_bih"],
        "L1_gnn_node_bhh": _L1_gnn_in["node_bhh"],
        "L2_gnn_W": _L2_gnn_in["W"],
        "L3_gnn_W": _L3_gnn_in["W"],
        "L3_gnn_B": _L3_gnn_in["B"],
    }

def reference(x, adj, L0_gnn_Wm, L0_gnn_al, L0_gnn_ar, L1_gnn_gat_W, L1_gnn_gat_a, L1_gnn_edge_Wih, L1_gnn_edge_Whh, L1_gnn_edge_bih, L1_gnn_edge_bhh, L1_gnn_node_Wih, L1_gnn_node_Whh, L1_gnn_node_bih, L1_gnn_node_bhh, L2_gnn_W, L3_gnn_W, L3_gnn_B):
    import jax
    import jax.numpy as jnp
    def _L0_gnn_ref(h, adj, Wm, al, ar):
        import jax, jax.numpy as jnp
        import numpy as np
        N = 4096
        IN = 256
        F = 64
        H = 4
        n = h.shape[0]
        ht = (h @ Wm).reshape(n, H, F)
        el = jnp.einsum('nhf,f->nh', ht, al)
        er = jnp.einsum('nhf,f->nh', ht, ar)
        scores = jax.nn.leaky_relu(el[:, :, None] + er.T[None, :, :], 0.2)
        scores = jnp.where(adj[:, None, :] == 0, -jnp.inf, scores)
        attn = jax.nn.softmax(scores, axis=-1)
        out = jnp.einsum('nhj,jhf->nhf', attn, ht)
        return out.reshape(n, H * F)

    def _L1_gnn_ref(h, node_adj, edge_adj, gat_W, gat_a, edge_Wih, edge_Whh, edge_bih, edge_bhh, node_Wih, node_Whh, node_bih, node_bhh):
        import jax, jax.numpy as jnp
        import numpy as np
        N, H, HEADS = (4096, 256, 3)
        ALPHA = 0.2
        NEG_INF = -9000000000000000.0

        def _sign_adj(key, n, density):
            k1, k2 = jax.random.split(key)
            mask = jax.random.uniform(k1, (n, n)) < density
            sign = jnp.where(jax.random.uniform(k2, (n, n)) < 0.5, -1.0, 1.0)
            adj = jnp.where(mask, sign, 0.0).astype(jnp.float32)
            idx = jnp.arange(n)
            return adj.at[idx, idx].set(1.0)

        def _gru_cell(x, hstate, Wih, Whh, bih, bhh):
            gi = x @ Wih.T + bih
            gh = hstate @ Whh.T + bhh
            ir, iz, inn = jnp.split(gi, 3, axis=1)
            hr, hz, hn = jnp.split(gh, 3, axis=1)
            r = jax.nn.sigmoid(ir + hr)
            z = jax.nn.sigmoid(iz + hz)
            n = jnp.tanh(inn + r * hn)
            return (1.0 - z) * n + z * hstate

        def _gat_head(h, node_adj, edge_adj, W, a):
            hW = h @ W
            hp = (node_adj > 0).astype(hW.dtype) @ hW
            hm = (node_adj < 0).astype(hW.dtype) @ hW
            e_plus = jax.nn.leaky_relu(jnp.concatenate([hp, hm], axis=1) @ a, ALPHA)[:, 0]
            e_minus = jax.nn.leaky_relu(jnp.concatenate([hm, hp], axis=1) @ a, ALPHA)[:, 0]
            att = jnp.where(edge_adj > 0, e_plus[None, :], NEG_INF)
            att = jnp.where(edge_adj < 0, e_minus[None, :], att)
            att = jax.nn.softmax(att, axis=1)
            return att * edge_adj @ hW
        dn = jnp.diag(node_adj)
        de = jnp.diag(edge_adj)
        idx = jnp.arange(node_adj.shape[0])
        node_adj_norm = node_adj.at[idx, idx].add(-dn)
        edge_adj_norm = edge_adj.at[idx, idx].add(-de)
        node_support = node_adj_norm @ h
        edge_output = _gru_cell(node_support, h, edge_Wih, edge_Whh, edge_bih, edge_bhh)
        edge_support = _gat_head(h, node_adj_norm, edge_adj_norm, gat_W[0], gat_a[0])
        for i in range(1, HEADS):
            edge_support = edge_support + _gat_head(h, node_adj_norm, edge_adj_norm, gat_W[i], gat_a[i])
        edge_support = edge_support / HEADS
        node_output = _gru_cell(edge_support, h, node_Wih, node_Whh, node_bih, node_bhh)
        return de[:, None] * edge_output + dn[:, None] * node_output

    def _L2_gnn_ref(features, adj, W):
        import jax, jax.numpy as jnp
        import numpy as np
        N = 16384
        D = 256
        OUT = 256
        deg = adj.sum(axis=1, keepdims=True) + 1.0
        neigh = adj @ features / deg
        data = jnp.concatenate([features, neigh], axis=-1)
        return data @ W.T

    def _L3_gnn_ref(z, dist_matrix, W, B):
        import jax, jax.numpy as jnp
        import numpy as np
        N = 8192
        D = 256
        CUTOFF = 1.0
        MU = 1.0
        SIGMA = 0.5

        def sensitivity(r, mu, sigma):
            return jnp.exp(-(1.0 / r - 1.0 / mu) ** 2 / (2.0 * sigma * sigma))
        msg = z @ W + B
        sens = sensitivity(dist_matrix, MU, SIGMA)
        weights = jnp.where(dist_matrix < CUTOFF, sens, 0.0)
        return weights @ msg

    h = jnp.maximum(_layernorm(x, axis=-1), 0.0)
    x = x + _L0_gnn_ref(h, adj, L0_gnn_Wm, L0_gnn_al, L0_gnn_ar)
    h = jnp.maximum(_layernorm(x, axis=-1), 0.0)
    x = x + _L1_gnn_ref(h, adj, adj, L1_gnn_gat_W, L1_gnn_gat_a, L1_gnn_edge_Wih, L1_gnn_edge_Whh, L1_gnn_edge_bih, L1_gnn_edge_bhh, L1_gnn_node_Wih, L1_gnn_node_Whh, L1_gnn_node_bih, L1_gnn_node_bhh)
    h = jnp.maximum(_layernorm(x, axis=-1), 0.0)
    x = x + _L2_gnn_ref(h, adj, L2_gnn_W)
    h = jnp.maximum(_layernorm(x, axis=-1), 0.0)
    x = x + _L3_gnn_ref(h, adj, L3_gnn_W, L3_gnn_B)
    return x


_drawn_inputs = setup_inputs


def setup_inputs(seed=0):
    import zlib

    import numpy as np

    out = dict(_drawn_inputs(seed))
    spreads = {'L1_gnn_edge_bih': (0.0, 0.305),
     'L1_gnn_edge_bhh': (0.0, 0.48),
     'L1_gnn_node_bih': (0.0, 0.301),
     'L1_gnn_node_bhh': (0.0, 0.434),
     'L3_gnn_B': (0.0, 0.1)}
    factors = {'L1_gnn_gat_a': 34.35,
     'L1_gnn_edge_Whh': 3.215,
     'L1_gnn_node_Whh': 3.127,
     'L1_gnn_node_Wih': 2.683}
    for name, (base, spread) in spreads.items():
        noise = np.random.default_rng([zlib.crc32(name.encode()), seed]).standard_normal(out[name].shape)
        drawn = base * np.exp(spread * noise) if base else spread * noise
        out[name] = jnp.asarray(drawn.astype(out[name].dtype))
    for name, factor in factors.items():
        out[name] = (out[name] * factor).astype(out[name].dtype)
    return out
```

```python
from contextlib import ExitStack

import numpy as np
import concourse.bass as bass
from concourse import mybir

F32 = mybir.dt.float32
F16 = mybir.dt.float16
BF16 = mybir.dt.bfloat16
FP8 = mybir.dt.float8e4
ALU = mybir.AluOpType
ACT = mybir.ActivationFunctionType
AX = mybir.AxisListType
RMAX = bass.bass_isa.ReduceOp.max

P = 128


def gnn_stack_kernel(nc, t_in, out):
    N, D = t_in["x"].shape[0], 256
    NREAL = out.shape[0]
    NT = N // P
    DC = D // P
    H0, F0 = 4, 64
    C0 = F0 + 1
    H1 = 3
    EPS = 1e-5
    TINY = 1e-30
    NEAR_ZERO = 1e-12
    SLOPE = 0.2
    G0 = [(0, 8), (8, 7), (15, 7)]
    G1 = [(0, 6), (6, 6), (12, 5), (17, 5)]
    LOG2E = 1.0 / float(np.log(2.0))
    LN2 = float(np.log(2.0))
    LN2_HIGH = 0.693359375
    LN2_LOW = LN2 - LN2_HIGH
    ROUND = 1.5 * 2.0 ** 23
    NRING = 5
    NMASK = 29
    MASKED = -240.0
    QUARTER = NT * P // 2
    assert N == NT * P and DC == 2

    with ExitStack() as ctx:
        def sb(name, shape, dt=F32):
            return ctx.enter_context(nc.sbuf_tensor(name, shape, dt))

        sems = {}

        def sem(name):
            if name not in sems:
                sems[name] = ctx.enter_context(nc.semaphore(name))
            return sems[name]

        AT = sb("AT", [P, NT, N], FP8)
        X = sb("X", [P, NT, D])
        ident = sb("ident", [P, P])
        scratch = sb("scratch", [P, QUARTER // 2])
        stats = scratch[:, 0:NT * 6].rearrange("p (t c) -> p t c", c=6)
        E3 = scratch[:, NT * 6:NT * 15].rearrange("p (t c) -> p t c", c=9)
        junk = scratch[:].bitcast(BF16)
        mv = sb("mv", [P, NT, 2])
        ln = sb("ln", [P, 6, NT])
        small = sb("small", [P, 32])
        sens_count = sb("sens_count", [P, len(G0) * NT])
        sens_any = sb("sens_any", [P, 1], mybir.dt.int32)
        AR = 30298
        arena = sb("arena", [P, AR])
        PS = ctx.enter_context(nc.psum_tensor("PS", [P, 8, 512], F32))

        class Arena:
            def __init__(self):
                self.at = 0

            def take(self, *dims, dt=F32, size=4):
                n = int(np.prod(dims))
                words = -(-n * size // 4)
                words += words % 2
                v = arena[:, self.at:self.at + words]
                self.at += words
                assert self.at <= AR, (self.at, AR)
                if dt != F32:
                    v = v.bitcast(dt)
                v = v[:, 0:n]
                if len(dims) == 2:
                    v = v.rearrange("p (a b) -> p a b", a=dims[0])
                if len(dims) == 3:
                    v = v.rearrange("p (a b c) -> p a b c", a=dims[0], b=dims[1])
                if len(dims) == 4:
                    v = v.rearrange("p (a b c d) -> p a b c d", a=dims[0], b=dims[1], c=dims[2])
                return v

        a0 = Arena()
        MOV = a0.take(NT, H0, 2, 2 * C0, dt=F16, size=2)
        mask_at = a0.at
        MASK = a0.take(NMASK, 1024, dt=FP8, size=1)
        a0m = Arena()
        a0m.at = mask_at
        HTF = a0m.take(NT, H0 * C0)
        assert a0m.at <= a0.at
        ELB = a0.take(2, 1024)
        STG = a0.take(4, 1024)
        e_at = a0.at
        E = a0.take(8, 4 * C0)
        DA = a0.take(8, 4 * C0)
        a0w = Arena()
        a0w.at = e_at
        WM = a0w.take(DC, D)
        WMT = a0w.take(DC, D)
        TS = a0w.take(3, 4 * 2 * C0)
        HS = a0w.take(2, D)
        HTS = a0w.take(2, D)
        assert a0w.at <= a0.at
        ALR = a0.take(DC, 2 * H0)
        WAL = a0.take(DC, 2 * H0)
        ELR = a0.take(NT, 2 * H0)
        ELC = a0.take(NT * H0)
        NER = a0.take(NT, H0)
        COEF = a0.take(4, NT * H0)
        MX = a0.take(NT * H0)
        ELT = a0.take(P)
        RD = a0.take(8, H0)

        a1 = Arena()
        H32 = a1.take(NT, D)
        HHL = a1.take(NT, 2, D + 2, dt=F16, size=2)
        EB = a1.take(H1, N)
        ab = Arena()
        ab.at = a1.at - H1 * N
        GWT = ab.take(H1 * DC, D)
        AROW = a1.take(2, QUARTER)
        WIH = a1.take(DC, 3 * D)
        WHH = a1.take(DC, 3 * D)
        GW = a1.take(H1 * DC, D)
        gru_at = a1.at
        SH = a1.take(4 * P)
        NSS = a1.take(D)
        au = Arena()
        au.at = a1.at - D
        UP = au.take(NT, 3 * H1 + 1, dt=F16, size=2)
        HWS = a1.take(H1, 2, D + 2, dt=F16, size=2)
        TRZ = a1.take(2 * D)
        GT = a1.take(D)
        GN = a1.take(D)
        GD = TRZ[:, 0:D]
        BIAS = a1.take(4 * D, dt=BF16, size=2)
        tmp = Arena()
        tmp.at = gru_at
        BR = tmp.take(4 * D)
        BRB = tmp.take(2 * D)
        BP = tmp.take(4 * D, dt=BF16, size=2)
        assert tmp.at <= a1.at
        a2 = Arena()
        HW = a2.take(2, NT, 2 * (D + 2), dt=F16, size=2)
        ES = a2.take(NT, D)
        MB = a2.take(2, N)
        a2t_at = a2.at
        T = a2.take(NRING, 1024, dt=BF16, size=2)
        PW = a2.take(NRING, 1024, dt=BF16, size=2)
        a2t = Arena()
        a2t.at = a2t_at
        SH2 = a2t.take(4 * P)
        TRZ2 = a2t.take(2 * D)
        GT2 = a2t.take(D)
        GN2 = a2t.take(D)
        GD2 = TRZ2[:, 0:D]
        SH2B = a2t.take(4 * P)
        BIAS2 = a2t.take(4 * D, dt=BF16, size=2)
        BR2 = a2t.take(4 * D)
        BRB2 = a2t.take(2 * D)
        BP2 = a2t.take(4 * D, dt=BF16, size=2)
        assert a2t.at <= a2.at
        WIH2 = a2.take(DC, 3 * D)
        a2h = Arena()
        a2h.at = NT * (D + 2)
        H32B = a2h.take(NT, D)
        a2m = Arena()
        a2m.at = 2 * NT * (D + 2) + NT * D + N
        WHH2 = a2m.take(DC, 3 * D)
        a3 = Arena()
        HHL2 = a3.take(NT, 2, D + 2, dt=F16, size=2)
        H2 = a3.take(NT, D)
        NEI = a3.take(D)
        SH3 = a3.take(4 * P)
        W2 = a3.take(2 * DC, D)
        a4 = Arena()
        MSG = a4.take(NT, D)
        H3 = a4.take(NT, D)
        W3 = a4.take(DC, D)
        B3 = a4.take(D)
        SH4 = a4.take(2, DC * P)
        DIST = a4.take(4, 1024)
        RCP = a4.take(2, 1024)
        WT = a4.take(3, 1024)
        DN = sb("DN", [P, NT])
        NOTI = sb("NOTI", [P, P])
        E1 = sb("E1", [P, NT, H1])
        E2 = sb("E2", [P, NT * H1])
        FR = ln[:, 0:H1, :].rearrange("p a b -> p (a b)")
        M2 = sb("M2", [P, NT, 2, H1])
        A1 = sb("A1", [P, DC, H1])
        U1 = sb("U1", [P, DC, H1])
        ET = sb("ET", [P, P])
        ones3 = sb("ones3", [4, P], BF16)
        EP_D = nc.dram_tensor("e_rows", [NT, H1, P], F32, kind="Internal").ap()
        MN_D = nc.dram_tensor("m_rows", [NT, H1, P], F32, kind="Internal").ap()
        H_D = nc.dram_tensor("h_saved", [P, NT, D], F32, kind="Internal").ap()
        HW_D = nc.dram_tensor("hw_saved", [H1, P, NT, 2 * (D + 2)], F16, kind="Internal").ap()

        EL_D = nc.dram_tensor("el_rows", [NT, H0, P], F32, kind="Internal").ap()

        block = ctx.enter_context(nc.Block())
        adjT = t_in["adjT"].rearrange("(j p) i -> j p i", p=P)
        units0 = [(g, h) for g in range(len(G0)) for h in range(H0)]
        chunk0 = [(g, j) for g in range(len(G0)) for j in range(NT)]
        banks_before = {}
        cnt = 0
        for g, (b0, nb) in enumerate(G0):
            for u in range(H0 + 1):
                banks_before[(g, u)] = cnt
                cnt += nb
        stg_before = [16 * len(range(q, len(chunk0), 4)) for q in range(4)]

        units1 = [(h, g) for h in range(H1) for g in range(len(G0))]

        def layer3_needed(eng):
            eng.wait_ge(sem("flag"), 1)
            return eng.value_load(sens_any[0:1, 0:1], min_val=0, max_val=1)

        def link_on(eng, name):
            s = sem(name)
            state = [0]

            def link(ins):
                state[0] += 1
                ins.then_inc(s, 1)
                eng.wait_ge(s, state[0])
            return link

        @block.sync
        def _(sp):
            for c in range(2):
                sp.dma_start(X[:, c * 11:(c + 1) * 11, :],
                             t_in["x"][c * 11 * P:(c + 1) * 11 * P, :].rearrange("(t p) d -> p t d", p=P)
                             ).then_inc(sem("x_in"), 16)

            def load_chunk(n):
                g, j = chunk0[n]
                b0, nb = G0[g]
                if n >= 4:
                    sp.wait_ge(sem("stg_used"), n - 3)
                    sp.wait_ge(sem("checked"), n - 3)
                sp.dma_start(STG[:, n % 4, 0:nb * P], adjT[j, :, b0 * P:(b0 + nb) * P]
                             ).then_inc(sem(f"stg{n % 4}"), 16)

            def load_el(n):
                g, h = units0[n]
                b0, nb = G0[g]
                if n >= 2:
                    sp.wait_ge(sem("masks_built"), (n - 1) * NT)
                sp.dma_start(ELB[:, n % 2, 0:nb * P].rearrange("p (k q) -> p k q", q=P),
                             EL_D[b0:b0 + nb, h, :].partition_broadcast(P)).then_inc(sem(f"elb{n % 2}"), 16)

            for n in range(NT):
                load_chunk(n)
            sp.wait_ge(sem("el_t"), 1)
            sp.dma_start(EL_D.rearrange("t h q -> (t h) q"), ELT[0:NT * H0, :]).then_inc(sem("el_rows"), 16)
            sp.wait_ge(sem("el_rows"), 16)
            load_el(0)
            load_el(1)
            for q in range(4):
                for n in range(NT + 11 * q, NT + 11 * (q + 1)):
                    load_chunk(n)
                load_el(2 + q)
            for n in range(6, len(units0)):
                load_el(n)
            sp.wait_ge(sem("x_l0"), 1)
            sp.dma_start(GWT.rearrange("p (h c) d -> p h c d", h=H1),
                         t_in["gatWT"].rearrange("h (c p) k -> p h c k", p=P)).then_inc(sem("w1"), 16)
            sp.dma_start(A1[:], t_in["gat_a"]).then_inc(sem("w1"), 16)
            sp.dma_start(DN[:], t_in["diag"]).then_inc(sem("dn"), 16)
            sp.dma_start(WIH, t_in["edge_WihT"].rearrange("(c p) n -> p c n", p=P)).then_inc(sem("we"), 16)
            sp.dma_start(WHH, t_in["edge_WhhT"].rearrange("(c p) n -> p c n", p=P)).then_inc(sem("we"), 16)
            sp.dma_start(GW.rearrange("p (h c) d -> p h c d", h=H1),
                         t_in["gatW"].rearrange("h (c p) k -> p h c k", p=P)).then_inc(sem("we"), 16)

            def load_bias(raw, rawb, ih, hh, name):
                sp.dma_start(raw[0:3, 0:3 * D], t_in[ih].partition_broadcast(3)).then_inc(sem(name), 16)
                sp.dma_start(raw[0:3, 3 * D:4 * D], t_in[hh][2 * D:3 * D].partition_broadcast(3)).then_inc(sem(name), 16)
                sp.dma_start(rawb[0:3, :], t_in[hh][0:2 * D].partition_broadcast(3)).then_inc(sem(name), 16)

            sp.wait_ge(sem("h1"), NT)
            sp.dma_start(H_D, H32).then_inc(sem("h_saved"), 16)
            sp.wait_ge(sem("et"), 1)
            sp.wait_ge(sem("u_mm"), 1)
            sp.dma_start(EP_D.rearrange("t h q -> (t h) q"), ET[0:NT * H1, :]).then_inc(sem("ep"), 16)
            sp.wait_ge(sem("ep"), 16)
            for h in range(H1):
                sp.dma_start(EB[:, h, :].rearrange("p (t q) -> p t q", q=P),
                             EP_D[:, h, :].partition_broadcast(P)).then_inc(sem("eb"), 16)
            load_bias(BR, BRB, "edge_bih", "edge_bhh", "be")
            def save_products(t):
                sp.wait_ge(sem("hw_lo"), H1 * (t + 1))
                sp.dma_start(HW_D[:, :, t, :].rearrange("h p c -> p h c"),
                             HWS.rearrange("p h a c -> p h (a c)")).then_inc(sem("hw_dma"), 16)

            for t in range(NT + 2):
                if 2 <= t < NT:
                    save_products(t - 2)
                if t < NT:
                    for c in range(2):
                        if t >= 1:
                            sp.wait_ge(sem("rmax"), H1 * (2 * t + c - 1))
                        sp.dma_start(AROW[:, c, :], t_in["adj"][t * P:(t + 1) * P, c * QUARTER:(c + 1) * QUARTER]
                                     ).then_inc(sem(f"arow{c}"), 16)
                if t >= NT:
                    save_products(t - 2)
            sp.wait_ge(sem("hw_dma"), 16 * NT)
            sp.wait_ge(sem("gru_x"), NT)
            sp.wait_ge(sem("h_saved"), 16)

            def load_head(h):
                if h >= 2:
                    sp.wait_ge(sem("bank_full1"), (h - 1) * NT)
                sp.dma_start(HW[:, h % 2, :, :], HW_D[h]).then_inc(sem(f"hwb{h % 2}"), 16)
                if h >= 2:
                    sp.wait_ge(sem("t_built"), (h - 1) * len(G0) * NT)
                sp.dma_start(MB[:, h % 2, :].rearrange("p (t q) -> p t q", q=P),
                             MN_D[:, h, :].partition_broadcast(P)).then_inc(sem(f"mb{h % 2}"), 16)

            sp.dma_start(WIH2, t_in["node_WihT"].rearrange("(c p) n -> p c n", p=P)).then_inc(sem("wn"), 16)
            sp.wait_ge(sem("mt"), 1)
            sp.dma_start(MN_D.rearrange("t h q -> (t h) q"), ET[0:NT * H1, :]).then_inc(sem("mn"), 16)
            sp.wait_ge(sem("mn"), 16)
            for h in range(H1):
                load_head(h)
            sp.wait_ge(sem("bank_full1"), 2 * NT)
            sp.dma_start(H32B, H_D).then_inc(sem("h_back"), 16)
            sp.wait_ge(sem("t_built"), 2 * len(G0) * NT)
            sp.dma_start(WHH2, t_in["node_WhhT"].rearrange("(c p) n -> p c n", p=P)).then_inc(sem("wn"), 16)
            sp.wait_ge(sem("es_done"), NT * H1)
            load_bias(BR2, BRB2, "node_bih", "node_bhh", "bn")
            sp.wait_ge(sem("gru_x"), 2 * NT)
            sp.dma_start(W2, t_in["W2T"].rearrange("(c p) n -> p c n", p=P)).then_inc(sem("w2"), 16)
            def write_out(done, before):
                for g, (b0, nb) in enumerate(G0):
                    sp.wait_ge(sem(done), before + b0 + nb)
                    last = b0 + nb == NT
                    full = nb - 1 if last else nb
                    sp.dma_start(out[b0 * P:(b0 + full) * P, :].rearrange("(t p) d -> p t d", p=P),
                                 X[:, b0:b0 + full, :]).then_inc(sem("out"), 16)
                    if last:
                        sp.dma_start(out[(NT - 1) * P:NREAL, :], X[0:NREAL - (NT - 1) * P, NT - 1, :]
                                     ).then_inc(sem("out"), 16)
                sp.wait_ge(sem("out"), 16 * (len(G0) + 1))

            with sp.If(layer3_needed(sp) == 1):
                sp.wait_ge(sem("x_l2"), NT)
                sp.dma_start(W3, t_in["W3"].rearrange("(c p) n -> p c n", p=P)).then_inc(sem("w3"), 16)
                sp.dma_start(B3, t_in["B3"].partition_broadcast(P)).then_inc(sem("w3"), 16)
                for m, (g, j) in enumerate(chunk0):
                    b0, nb = G0[g]
                    if m >= 4:
                        sp.wait_ge(sem("w_built"), m - 3)
                    sp.dma_start(DIST[:, m % 4, 0:nb * P], adjT[j, :, b0 * P:(b0 + nb) * P]
                                 ).then_inc(sem(f"stg{m % 4}"), 16)
                write_out("x_l3", 0)
            with sp.Else():
                write_out("x_l2", 0)

        @block.gpsimd
        def _(pool):
            link = link_on(pool, "pool_chain")
            link(pool.memset(ident[:], 0.0))
            pool.affine_select(out=ident[:], in_=ident[:], compare_op=ALU.not_equal, fill=1.0, base=0,
                               pattern=[[-1, P]], channel_multiplier=1).then_inc(sem("consts"), 1)
            pool.wait_ge(sem("consts"), 1)
            pool.tensor_scalar(NOTI[:], ident[:], -1.0, 1.0, ALU.mult, ALU.add).then_inc(sem("consts"), 1)
            pool.memset(ones3[:], 1.0).then_inc(sem("consts"), 1)
            pool.memset(ALR, 0.0).then_inc(sem("consts"), 1)
            pool.memset(HTF.rearrange("p t (h c) -> p t h c", c=C0)[:, :, :, F0:C0], 1.0).then_inc(sem("consts"), 1)
            pool.wait_ge(sem("er_max"), 1)
            pool.partition_all_reduce(small[:, 4:8], small[:, 0:4], P, RMAX).then_inc(sem("er_gmax"), 1)
            pool.wait_ge(sem("coef"), 1)
            for t in range(NT):
                if t >= 3:
                    pool.wait_ge(sem("mov"), t - 2)
                pool.wait_ge(sem("htf"), t + 1)
                pool.tensor_tensor(TS[:, t % 3, :].rearrange("p (h b c) -> p h b c", h=H0, b=2)[:, :, 1, :],
                                   HTF[:, t, :].rearrange("p (h c) -> p h c", c=C0),
                                   COEF[:, 3, t * H0:(t + 1) * H0].unsqueeze(2).to_broadcast([P, H0, C0]),
                                   ALU.mult).then_inc(sem("t_d"), 1)
            for n, (g, h) in enumerate(units0):
                b0, nb = G0[g]
                if n == H0 + 2:
                    pool.wait_ge(sem("sens_max"), 1)
                    pool.partition_all_reduce(small[:, 21:22], small[:, 20:21], P, RMAX).then_inc(sem("sens_gmax"), 1)
                Ev = E[:, 0:nb, :]
                Dv = DA[:, 0:nb, h * C0:(h + 1) * C0]
                co = [COEF[:, q, :].rearrange("p (t h) -> p t h", h=H0)[:, b0:b0 + nb, h:h + 1].to_broadcast([P, nb, C0])
                      for q in range(2)]
                pool.wait_ge(sem("bank_free"), banks_before[(g, h + 1)] + nb)
                link(pool.tensor_tensor(Ev[:, :, 0:C0], Ev[:, :, 0:C0], Ev[:, :, 2 * C0:3 * C0], ALU.add))
                link(pool.tensor_tensor(Ev[:, :, C0:2 * C0], Ev[:, :, C0:2 * C0], Ev[:, :, 3 * C0:4 * C0], ALU.add))
                link(pool.tensor_tensor(Ev[:, :, C0:2 * C0], Dv, Ev[:, :, C0:2 * C0], ALU.subtract))
                link(pool.tensor_tensor(Ev[:, :, 0:C0], Ev[:, :, 0:C0], co[0], ALU.mult))
                link(pool.tensor_tensor(Ev[:, :, C0:2 * C0], Ev[:, :, C0:2 * C0], co[1], ALU.mult))
                ins = pool.tensor_tensor(Dv, Ev[:, :, 0:C0], Ev[:, :, C0:2 * C0], ALU.add)
                ins.then_inc(sem("e_used"), 1)
                if h == H0 - 1:
                    pool.wait_ge(sem("rden0"), g + 1)
                    for hh in range(H0):
                        Dh = DA[:, 0:nb, hh * C0:hh * C0 + F0]
                        Xh = X[:, b0:b0 + nb, hh * F0:(hh + 1) * F0]
                        link(pool.tensor_tensor(Dh, Dh, RD[:, 0:nb, hh:hh + 1].to_broadcast([P, nb, F0]), ALU.mult))
                        link(pool.tensor_tensor(Xh, Xh, Dh, ALU.add))
                    pool.sem_inc(sem("da_used"), 1)
            pool.sem_inc(sem("x_l0"), 1)
            pool.memset(HHL[:, :, 0, D:D + 2], 1.0).then_inc(sem("hhl_pad"), 1)
            pool.wait_ge(sem("e_min"), 1)
            pool.partition_all_reduce(small[:, 12:15], small[:, 8:11], P, RMAX).then_inc(sem("shift"), 1)

            def gru_tail(count, t, h_blk, trz, n, d):
                pool.wait_ge(sem("n"), count)
                link(pool.tensor_tensor(d, h_blk, n, ALU.subtract))
                link(pool.tensor_scalar(trz[:, D:2 * D], trz[:, D:2 * D], 0.5, 0.5, ALU.mult, ALU.add))
                link(pool.tensor_tensor(d, trz[:, D:2 * D], d, ALU.mult))
                link(pool.tensor_tensor(d, d, n, ALU.add))
                link(pool.tensor_scalar(d, d, DN[:, t:t + 1], 1.0, ALU.mult, ALU.mult))
                pool.tensor_tensor(X[:, t, :], X[:, t, :], d, ALU.add).then_inc(sem("gru_x"), 1)

            pool.wait_ge(sem("dn"), 16)
            for t in range(NT + 2):
                if t < NT:
                    c, b = divmod(t, NT // 2)
                    pool.wait_ge(sem(f"arow{c}"), 16 * (t + 1))
                    blk = AROW[:, c, b * P:(b + 1) * P]
                    pool.tensor_tensor(blk, blk, NOTI[:], ALU.mult).then_inc(sem("row_diag"), 1)
                if t >= 2:
                    gru_tail(t - 1, t - 2, H32[:, t - 2, :], TRZ, GN, GD)
            pool.wait_ge(sem("h_back"), 16)
            for t in range(NT):
                gru_tail(NT + t + 1, t, H32B[:, t, :], TRZ2, GN2, GD2)
            pool.memset(HHL2[:, :, 0, D:D + 2], 1.0).then_inc(sem("hhl_pad"), 1)
            with pool.If(layer3_needed(pool) == 1):
                m = 0
                for g, (b0, nb) in enumerate(G0):
                    for j in range(NT):
                        pool.wait_ge(sem("near0"), m + 1)
                        v = RCP[:, m % 2, 0:nb * P]
                        pool.tensor_tensor(v, v, DIST[:, m % 4, 0:nb * P], ALU.add).then_inc(sem("no_zero"), 1)
                        m += 1
            with pool.Else():
                pool.nop()

        @block.scalar
        def _(act):
            act.dma_start(WM, t_in["Wm"].rearrange("(c p) n -> p c n", p=P)).then_inc(sem("w0"), 16)
            act.dma_start(WMT, t_in["WmT"].rearrange("(c p) n -> p c n", p=P)).then_inc(sem("w0"), 16)
            act.wait_ge(sem("consts"), 5)
            for h in range(H0):
                for q, name in enumerate(("al", "ar")):
                    act.dma_start(ALR[F0 * (h % 2):F0 * (h % 2) + F0, h // 2, q * H0 + h:q * H0 + h + 1],
                                  t_in[name].unsqueeze(1)).then_inc(sem("w0"), 16)

            def norm_sqrt(q):
                act.wait_ge(sem("var"), q + 1)
                act.activation(ln[:, 1, :], ln[:, 0, :], ACT.Sqrt).then_inc(sem("sqrt"), 1)
                act.wait_ge(sem("rstd"), q + 1)

            def norm_all(q, full, high):
                norm_sqrt(q)
                for t in range(NT):
                    act.activation(full[:, t, :], X[:, t, :], ACT.Relu, bias=ln[:, 5, t:t + 1],
                                   scale=ln[:, 2, t:t + 1]).then_inc(sem(f"h{q}"), 1)
                    if high is not None:
                        act.activation(high[:, t, 0, 0:D], X[:, t, :], ACT.Relu, bias=ln[:, 5, t:t + 1],
                                       scale=ln[:, 2, t:t + 1]).then_inc(sem(f"hi{q}"), 1)

            norm_sqrt(0)

            def norm(t):
                if t >= 2:
                    act.wait_ge(sem("h_tr"), t - 1)
                act.activation(HS[:, t % 2, :], X[:, t, :], ACT.Relu, bias=ln[:, 5, t:t + 1],
                               scale=ln[:, 2, t:t + 1]).then_inc(sem("h"), 1)

            def ht_out(t):
                act.wait_ge(sem("ht_mm"), t + 1)
                act.activation(HTF[:, t, :].rearrange("p (h c) -> p h c", c=C0)[:, :, 0:F0],
                               PS[:, 2 + t % 2, 0:D].rearrange("p (h c) -> p h c", c=F0), ACT.Copy
                               ).then_inc(sem("htf"), 1)

            norm(0)
            for t in range(NT):
                if t + 1 < NT:
                    norm(t + 1)
                act.wait_ge(sem("h_tr"), t + 1)
                if t >= 2:
                    act.wait_ge(sem("ht_mm"), t - 1)
                act.activation(HTS[:, t % 2, :], PS[:, t % 2, 0:D], ACT.Copy).then_inc(sem("hT"), 1)
                if t >= 1:
                    ht_out(t - 1)
            ht_out(NT - 1)
            act.wait_ge(sem("arg"), 1)
            act.activation(COEF, COEF, ACT.Exp).then_inc(sem("coef"), 1)
            act.wait_ge(sem("coef"), 1)
            for t in range(NT):
                act.wait_ge(sem("t_b"), t + 1)
                act.wait_ge(sem("t_d"), t + 1)
                act.activation(MOV[:, t, :, 0, :], TS[:, t % 3, :].rearrange("p (h c) -> p h c", h=H0), ACT.Copy
                               ).then_inc(sem("mov_hi"), 1)
            pos = 0
            casts = list(range(NT, 3 * NT))
            for g, (b0, nb) in enumerate(G0):
                for u in range(H0 + 1):
                    if g == 0 and u < 4:
                        for n in casts[11 * u:11 * (u + 1)]:
                            gg, j = chunk0[n]
                            bb, nn = G0[gg]
                            act.wait_ge(sem(f"stg{n % 4}"), 16 * (n // 4 + 1))
                            act.activation(AT[:, j, bb * P:(bb + nn) * P], STG[:, n % 4, 0:nn * P], ACT.Copy, saturate=False
                                           ).then_inc(sem("stg_used"), 1)
                    if u == 0:
                        if g >= 1:
                            act.wait_ge(sem("da_used"), g)
                    elif g * H0 + u - 1 >= 1:
                        act.wait_ge(sem("e_used"), g * H0 + u - 1)
                    if g == 0 and u == 0:
                        act.wait_ge(sem("mov"), NT)
                    for k in range(nb):
                        act.wait_ge(sem("bank_full"), banks_before[(g, u)] + k + 1)
                        act.activation((DA if u == 0 else E)[:, k, :], PS[:, k, 0:4 * C0], ACT.Copy
                                       ).then_inc(sem("bank_free"), 1)
            def turn_mask(g, j):
                blk = AT[:, j, G0[g][0] * P:(G0[g][0] + G0[g][1]) * P]
                act.activation(blk, blk, ACT.Copy, scale=-MASKED, bias=MASKED, saturate=False).then_inc(sem("ab"), 1)

            norm_sqrt(1)
            for t in range(NT + 1):
                if t < NT:
                    act.activation(H32[:, t, :], X[:, t, :], ACT.Relu, bias=ln[:, 5, t:t + 1],
                                   scale=ln[:, 2, t:t + 1]).then_inc(sem("h1"), 1)
                t -= 1
                if t < 0:
                    continue
                act.wait_ge(sem("h1_tr"), t + 1)
                if t >= 2:
                    act.wait_ge(sem("hu_mm"), t - 1)
                act.activation(SH[:, (t % 2) * 2 * P:(t % 2 + 1) * 2 * P], PS[:, t % 2, 0:D], ACT.Copy
                               ).then_inc(sem("h1T"), 1)
            act.wait_ge(sem("hu_mm"), NT)
            act.wait_ge(sem("fr_arg"), 1)
            act.activation(FR, FR, ACT.Exp).then_inc(sem("fr"), 1)
            act.wait_ge(sem("bias_e"), 1)

            for t in range(NT + 2):
                if t == 2:
                    act.wait_ge(sem("fr"), 1)
                if t >= 2:
                    act.wait_ge(sem("rz_mm"), t - 1)
                    if t >= 3:
                        act.wait_ge(sem("gru_x"), t - 2)
                    act.activation(TRZ, PS[:, 1 + t % 2, :], ACT.Tanh, scale=0.5).then_inc(sem("trz"), 1)
                    act.wait_ge(sem("hw_mm"), t - 1)
                    if t >= 3:
                        act.wait_ge(sem("hw_dma"), 16 * (t - 2))
                    for h in range(H1):
                        act.activation(HWS[:, h, 0, 0:D], PS[:, 6 + h // 2, (h % 2) * D:(h % 2 + 1) * D], ACT.Copy,
                                       scale=FR[:, (t - 2) * H1 + h:(t - 2) * H1 + h + 1]).then_inc(sem("hw_hi"), 1)
                if 1 <= t <= NT:
                    act.wait_ge(sem("tb"), t)
                    act.activation(SH, PS[:, 0, :], ACT.Copy).then_inc(sem("sh"), 1)
                if t >= 2:
                    act.wait_ge(sem("u"), t - 1)
                    act.activation(GN, GT, ACT.Tanh).then_inc(sem("n"), 1)
                if t < NT:
                    act.wait_ge(sem("ns"), t + 1)
                    act.activation(NSS, PS[:, 5, 0:D], ACT.Copy).then_inc(sem("ns_sb"), 1)
                for g in range(len(G0) - 1):
                    last = G0[g][0] + G0[g][1]
                    for j in range(4 * (t - last), min(4 * (t - last + 1), NT)):
                        if j >= 0:
                            turn_mask(g, j)
            act.wait_ge(sem("gru_x"), NT)

            m = 0
            for h in range(H1):
                for g, (b0, nb) in enumerate(G0):
                    for j in range(NT):
                        act.wait_ge(sem("t_built"), m + 1)
                        if m >= NRING:
                            act.wait_ge(sem("p_used"), m - NRING + 1)
                        act.activation(PW[:, m % NRING, 0:nb * P], T[:, m % NRING, 0:nb * P], ACT.Exp, scale=LN2
                                       ).then_inc(sem("p_exp"), 1)
                        if h == 0 and g < 2 and j % 2 == 1:
                            turn_mask(2, g * NT // 2 + j // 2)
                        m += 1
            act.wait_ge(sem("bias_n"), 1)
            for t in range(NT + 1):
                if t < NT:
                    act.wait_ge(sem("tb"), NT + t + 1)
                    if t >= 2:
                        act.wait_ge(sem("rz_mm"), NT + t - 1)
                    act.activation(SH2 if t % 2 == 0 else SH2B, PS[:, 0 if t % 2 == 0 else 5, :], ACT.Copy
                                   ).then_inc(sem("sh"), 1)
                if t >= 1:
                    act.wait_ge(sem("rz_mm"), NT + t)
                    if t >= 2:
                        act.wait_ge(sem("gru_x"), NT + t - 1)
                    act.activation(TRZ2, PS[:, 1 + (t - 1) % 2, :], ACT.Tanh, scale=0.5).then_inc(sem("trz"), 1)
                    act.wait_ge(sem("u"), NT + t)
                    act.activation(GN2, GT2, ACT.Tanh).then_inc(sem("n"), 1)
            act.wait_ge(sem("gru_x"), 2 * NT)
            norm_all(2, H2, HHL2)
            for t in range(NT + 1):
                if t >= 1:
                    act.wait_ge(sem("tb2"), t)
                    act.activation(SH3, PS[:, 0, :], ACT.Copy).then_inc(sem("sh3"), 1)
                if t < NT:
                    act.wait_ge(sem("rdeg"), t + 1)
                    act.activation(NEI, PS[:, 1 + t % 2, 0:D], ACT.Copy, scale=ln[:, 3, t:t + 1]).then_inc(sem("nei"), 1)
            with act.If(layer3_needed(act) == 1):
                act.wait_ge(sem("x_l2"), NT)
                norm_all(3, H3, None)
                for t in range(NT):
                    act.wait_ge(sem("h3_tr"), t + 1)
                    if t >= 2:
                        act.wait_ge(sem("msg_mm"), t - 1)
                    act.activation(SH4[:, t % 2, :], PS[:, t % 2, 0:D], ACT.Copy).then_inc(sem("h3T"), 1)
                m = 0
                for g, (b0, nb) in enumerate(G0):
                    for j in range(NT):
                        act.wait_ge(sem("rcp"), m + 1)
                        v = RCP[:, m % 2, 0:nb * P]
                        act.activation(v, v, ACT.Square, bias=small[:, 17:18]).then_inc(sem("sq"), 1)
                        act.wait_ge(sem("sq"), m + 1)
                        act.activation(v, v, ACT.Exp, scale=-2.0).then_inc(sem("sens"), 1)
                        m += 1
            with act.Else():
                act.nop()

        @block.vector
        def _(dve):
            link = link_on(dve, "dve_chain")

            def norm_scales(q, ready, value):
                dve.wait_ge(sem(ready), value)
                for t in range(NT):
                    dve.bn_stats(stats[:, t, :], X[:, t, :]).then_inc(sem("st"), 1)
                dve.wait_ge(sem("st"), (q + 1) * NT)
                for t in range(NT):
                    dve.bn_aggr(mv[:, t, :], stats[:, t, :]).then_inc(sem("ag"), 1)
                dve.wait_ge(sem("ag"), (q + 1) * NT)
                dve.tensor_scalar(ln[:, 0, :], mv[:, :, 1], EPS, None, ALU.add).then_inc(sem("var"), 1)
                dve.wait_ge(sem("sqrt"), q + 1)
                dve.wait_ge(sem("var"), q + 1)
                link(dve.reciprocal(ln[:, 3, :], ln[:, 1, :]))
                link(dve.tensor_tensor(ln[:, 4, :], ln[:, 3, :], ln[:, 3, :], ALU.mult))
                link(dve.tensor_tensor(ln[:, 4, :], ln[:, 4, :], ln[:, 0, :], ALU.mult))
                link(dve.tensor_scalar(ln[:, 4, :], ln[:, 4, :], -0.5, 1.5, ALU.mult, ALU.add))
                link(dve.tensor_tensor(ln[:, 2, :], ln[:, 3, :], ln[:, 4, :], ALU.mult))
                dve.scalar_tensor_tensor(out=ln[:, 5, :], in0=mv[:, :, 0], scalar=-1.0, in1=ln[:, 2, :],
                                         op0=ALU.mult, op1=ALU.mult).then_inc(sem("rstd"), 1)

            norm_scales(0, "x_in", 32)
            def count_sensitive(n):
                nb = G0[chunk0[n][0]][1]
                if n >= 1:
                    dve.wait_ge(sem("checked"), n)
                dve.scalar_tensor_tensor(out=junk[:, 0:nb * P], in0=STG[:, n % 4, 0:nb * P], scalar=1.0,
                                         in1=STG[:, n % 4, 0:nb * P], op0=ALU.is_lt, op1=ALU.logical_and,
                                         accum_out=sens_count[:, n:n + 1]).then_inc(sem("checked"), 1)

            dve.wait_ge(sem("rstd"), 1)
            for t in range(8):
                nb = G0[0][1]
                dve.wait_ge(sem(f"stg{t % 4}"), 16 * (t // 4 + 1))
                dve.tensor_copy(AT[:, t, 0:nb * P], STG[:, t % 4, 0:nb * P], saturate=False).then_inc(sem("stg_used"), 1)
                count_sensitive(t)
            dve.wait_ge(sem("wal_mm"), 1)
            dve.tensor_copy(WAL, PS[:, 4, 0:2 * DC * H0].rearrange("p (c n) -> p c n", c=DC)).then_inc(sem("wal"), 1)
            for t in range(8, NT):
                nb = G0[0][1]
                dve.wait_ge(sem(f"stg{t % 4}"), 16 * (t // 4 + 1))
                dve.tensor_copy(AT[:, t, 0:nb * P], STG[:, t % 4, 0:nb * P], saturate=False).then_inc(sem("stg_used"), 1)
                count_sensitive(t)
            dve.wait_ge(sem("ht_mm"), NT)
            link(dve.tensor_copy(ELR, PS[:, 5, 0:NT * 2 * H0].rearrange("p (t n) -> p t n", n=2 * H0)))
            dve.tensor_copy(ELC.rearrange("p (t h) -> p t h", h=H0), ELR[:, :, 0:H0]).then_inc(sem("elc"), 1)
            dve.tensor_reduce(small[:, 0:4], ELR[:, :, H0:2 * H0].rearrange("p t h -> p h t"), AX.X, ALU.max
                              ).then_inc(sem("er_max"), 1)
            link(dve.tensor_scalar(NER, ELR[:, :, H0:2 * H0], -1.0, None, ALU.mult))
            dve.wait_ge(sem("er_gmax"), 1)
            Gb = small[:, 4:8].unsqueeze(1).to_broadcast([P, NT, H0])
            CO = [COEF[:, q, :].rearrange("p (t h) -> p t h", h=H0) for q in range(4)]
            MXv = MX.rearrange("p (t h) -> p t h", h=H0)
            link(dve.tensor_tensor(CO[0], ELR[:, :, 0:H0], Gb, ALU.add))
            link(dve.scalar_tensor_tensor(out=MXv, in0=CO[0], scalar=SLOPE, in1=CO[0], op0=ALU.mult, op1=ALU.max))
            link(dve.scalar_tensor_tensor(out=CO[1], in0=CO[0], scalar=SLOPE, in1=MXv, op0=ALU.mult, op1=ALU.subtract))
            link(dve.tensor_tensor(CO[0], CO[0], MXv, ALU.subtract))
            link(dve.tensor_tensor(CO[2], ELR[:, :, H0:2 * H0], Gb, ALU.subtract))
            dve.tensor_scalar(CO[3], CO[2], SLOPE, None, ALU.mult).then_inc(sem("arg"), 1)
            dve.wait_ge(sem("elT_mm"), 1)
            dve.tensor_copy(ELT[0:NT * H0, :], PS[0:NT * H0, 6, 0:P]).then_inc(sem("el_t"), 1)
            dve.wait_ge(sem("coef"), 1)

            def low_part(t):
                dve.wait_ge(sem("mov_hi"), t + 1)
                dve.tensor_tensor(MOV[:, t, :, 1, :], TS[:, t % 3, :].rearrange("p (h c) -> p h c", h=H0),
                                  MOV[:, t, :, 0, :], ALU.subtract).then_inc(sem("mov"), 1)

            for t in range(NT):
                if t >= 3:
                    dve.wait_ge(sem("mov"), t - 2)
                dve.wait_ge(sem("htf"), t + 1)
                dve.tensor_tensor(TS[:, t % 3, :].rearrange("p (h b c) -> p h b c", h=H0, b=2)[:, :, 0, :],
                                  HTF[:, t, :].rearrange("p (h c) -> p h c", c=C0),
                                  COEF[:, 2, t * H0:(t + 1) * H0].unsqueeze(2).to_broadcast([P, H0, C0]),
                                  ALU.mult).then_inc(sem("t_b"), 1)
                if t >= 1:
                    low_part(t - 1)
            low_part(NT - 1)
            dve.wait_ge(sem("mov"), NT)
            dve.wait_ge(sem("t_d"), NT)
            for n, (g, h) in enumerate(units0):
                b0, nb = G0[g]
                dve.wait_ge(sem(f"elb{n % 2}"), 16 * (n // 2 + 1))
                for j in range(NT):
                    m = n * NT + j
                    if g >= 1 and h == 0:
                        dve.wait_ge(sem("stg_used"), g * NT + j + 1)
                    if g == 0 and h == 0 and j == 0:
                        dve.wait_ge(sem("stg_used"), NT)
                    if m >= NMASK:
                        n_old, j_old = divmod(m - NMASK, NT)
                        g_old, h_old = units0[n_old]
                        if j_old < NT - 1:
                            dve.wait_ge(sem("mask_used"), n_old * (NT - 1) + j_old + 1)
                        else:
                            dve.wait_ge(sem("bank_full"), banks_before[(g_old, h_old + 1)] + G0[g_old][1])
                    dve.scalar_tensor_tensor(out=MASK[:, m % NMASK, 0:nb * P], in0=ELB[:, n % 2, 0:nb * P],
                                             scalar=NER[:, j, h:h + 1], in1=AT[:, j, b0 * P:(b0 + nb) * P],
                                             op0=ALU.is_gt, op1=ALU.mult, saturate=False).then_inc(sem("masks_built"), 1)
                    if g == 0 and j % 2 == 1:
                        nn = NT + h * NT // 2 + j // 2
                        dve.wait_ge(sem(f"stg{nn % 4}"), 16 * (nn // 4 + 1))
                        count_sensitive(nn)
                if n == H0:
                    dve.wait_ge(sem("checked"), len(chunk0))
                    dve.tensor_reduce(small[:, 20:21], sens_count[:], AX.X, ALU.max).then_inc(sem("sens_max"), 1)
                if n == H0 + 3:
                    dve.wait_ge(sem("sens_gmax"), 1)
                    dve.tensor_scalar(sens_any[:], small[:, 21:22], 0.0, None, ALU.is_gt).then_inc(sem("flag"), 1)
                if h == 0 and g >= 1 or n == len(units0) - 1:
                    gs = [g - 1] if n < len(units0) - 1 else [g]
                    for gg in gs:
                        dve.wait_ge(sem("e_used"), (gg + 1) * H0)
                        RDg = RD[:, 0:G0[gg][1], :]
                        link(dve.tensor_scalar(RDg, DA[:, 0:G0[gg][1], :].rearrange("p k (h c) -> p k h c", c=C0)
                                               [:, :, :, F0], TINY, None, ALU.max))
                        dve.reciprocal(RDg, RDg).then_inc(sem("rden0"), 1)
            norm_scales(1, "x_l0", 1)
            dve.memset(small[:, 17:18], -1.0).then_inc(sem("minus1"), 1)
            dve.wait_ge(sem("consts"), 5)
            for t in range(NT):
                blk = AT[:, t, t * P:(t + 1) * P]
                dve.tensor_tensor(blk, blk, NOTI[:], ALU.mult, saturate=False).then_inc(sem("diag0"), 1)
            dve.wait_ge(sem("hhl_pad"), 1)
            for t in range(NT):
                dve.wait_ge(sem("h1"), t + 1)
                dve.tensor_copy(HHL[:, t, 0, 0:D], H32[:, t, :]).then_inc(sem("hi1"), 1)
                dve.wait_ge(sem("hi1"), t + 1)
                dve.tensor_tensor(HHL[:, t, 1, 0:D], H32[:, t, :], HHL[:, t, 0, 0:D], ALU.subtract
                                  ).then_inc(sem("lo1"), 1)
                if t == 0:
                    dve.wait_ge(sem("u_mm"), 1)
                    dve.tensor_copy(U1[:], PS[:, 3, 0:DC * H1].rearrange("p (c h) -> p c h", c=DC)).then_inc(sem("u1"), 1)

            def bias_parts(br, brb, bp, bias, loaded, done):
                dve.wait_ge(sem(loaded), 48)
                link(dve.tensor_tensor(br[0:3, 0:2 * D], br[0:3, 0:2 * D], brb[0:3, :], ALU.add))
                for k in range(3):
                    link(dve.tensor_copy(bp[0:3, :], br[0:3, :]))
                    link(dve.tensor_tensor(br[0:3, :], br[0:3, :], bp[0:3, :], ALU.subtract))
                    if k == 0:
                        ins = dve.tensor_scalar(bias[0:3, :], bp[0:3, :], ident[0:3, 0:1], None, ALU.mult)
                    else:
                        ins = dve.scalar_tensor_tensor(out=bias[0:3, :], in0=bp[0:3, :], scalar=ident[0:3, k:k + 1],
                                                       in1=bias[0:3, :], op0=ALU.mult, op1=ALU.add)
                    link(ins)
                dve.sem_inc(sem(done), 1)

            dve.wait_ge(sem("hu_mm"), NT)
            link(dve.tensor_copy(E1[:], PS[:, 2, 0:NT * H1].rearrange("p (t h) -> p t h", h=H1)))
            for k in range(3):
                part = UP[:, :, k * H1:(k + 1) * H1]
                link(dve.tensor_copy(part, E1[:]))
                if k < 2:
                    link(dve.tensor_tensor(E1[:], E1[:], part, ALU.subtract))
            dve.sem_inc(sem("up"), 1)
            dve.wait_ge(sem("e_mm"), 1)
            link(dve.tensor_copy(E3, PS[:, 4, 0:NT * 3 * H1].rearrange("p (t c) -> p t c", t=NT)))
            link(dve.tensor_tensor(E1[:], E3[:, :, H1:2 * H1], E3[:, :, 2 * H1:3 * H1], ALU.add))
            link(dve.tensor_tensor(E1[:], E3[:, :, 0:H1], E1[:], ALU.add))
            link(dve.scalar_tensor_tensor(out=E1[:], in0=E1[:], scalar=SLOPE, in1=E1[:], op0=ALU.mult, op1=ALU.max))
            E2v = E2[:].rearrange("p (t h) -> p t h", h=H1)
            FRv = FR.rearrange("p (t h) -> p t h", h=H1)
            link(dve.tensor_scalar(E2v, E1[:], LOG2E, ROUND, ALU.mult, ALU.add))
            link(dve.tensor_scalar(E2v, E2v, -ROUND, None, ALU.add))
            link(dve.tensor_reduce(small[:, 8:11], E2v.rearrange("p t h -> p h t"), AX.X, ALU.min))
            dve.tensor_scalar(small[:, 8:11], small[:, 8:11], -1.0, None, ALU.mult).then_inc(sem("e_min"), 1)
            link(dve.scalar_tensor_tensor(out=FRv, in0=E2v, scalar=-LN2_HIGH, in1=E1[:], op0=ALU.mult, op1=ALU.add))
            dve.scalar_tensor_tensor(out=FRv, in0=E2v, scalar=-LN2_LOW, in1=FRv, op0=ALU.mult, op1=ALU.add
                                     ).then_inc(sem("fr_arg"), 1)
            dve.wait_ge(sem("shift"), 1)
            shift = small[:, 12:15].unsqueeze(1).to_broadcast([P, NT, H1])
            dve.tensor_tensor(E1[:], E2v, shift, ALU.add).then_inc(sem("e2"), 1)
            dve.wait_ge(sem("eT_mm"), 1)
            dve.tensor_copy(ET[0:NT * H1, :], PS[0:NT * H1, 5, 0:P]).then_inc(sem("et"), 1)
            bias_parts(BR, BRB, BP, BIAS, "be", "bias_e")
            for h in range(H1):
                dve.memset(HWS[:, h, :, D:D + 2], 1.0).then_inc(sem("hws_pad"), 1)
            dve.wait_ge(sem("eb"), 16 * H1)

            def row_max(t, c):
                dve.wait_ge(sem(f"arow{c}"), 16 * (t + 1))
                if t // (NT // 2) == c:
                    dve.wait_ge(sem("row_diag"), t + 1)
                for h in range(H1):
                    if t + c + h > 0:
                        dve.wait_ge(sem("rmax"), H1 * (2 * t + c) + h)
                    dve.tensor_tensor_reduce(junk, AROW[:, c, :],
                                             EB[:, h, c * QUARTER:(c + 1) * QUARTER], 1.0, 0.0, ALU.mult, ALU.max,
                                             M2[:, t, c, h:h + 1]).then_inc(sem("rmax"), 1)

            def gru_new(count, t, trz, gt):
                dve.wait_ge(sem("trz"), count)
                dve.wait_ge(sem("nb_mm"), count)
                if count >= 2:
                    dve.wait_ge(sem("n"), count - 1)
                nb_bank = PS[:, 3 + t % 2, :]
                link(dve.scalar_tensor_tensor(out=gt, in0=trz[:, 0:D], scalar=1.0, in1=nb_bank[:, D:2 * D],
                                              op0=ALU.add, op1=ALU.mult))
                dve.scalar_tensor_tensor(out=gt, in0=gt, scalar=0.5, in1=nb_bank[:, 0:D],
                                         op0=ALU.mult, op1=ALU.add).then_inc(sem("u"), 1)

            for t in range(NT + 2):
                if t >= 2:
                    gru_new(t - 1, t - 2, TRZ, GT)
                if t >= 2:
                    for h in range(H1):
                        dve.wait_ge(sem("hw_hi"), H1 * (t - 1))
                        dve.scalar_tensor_tensor(out=HWS[:, h, 1, 0:D], in0=PS[:, 6 + h // 2, (h % 2) * D:(h % 2 + 1) * D],
                                                 scalar=FR[:, (t - 2) * H1 + h:(t - 2) * H1 + h + 1],
                                                 in1=HWS[:, h, 0, 0:D], op0=ALU.mult, op1=ALU.subtract).then_inc(sem("hw_lo"), 1)
                if t < NT:
                    row_max(t, 0)
                    row_max(t, 1)
            dve.wait_ge(sem("rmax"), 2 * NT * H1)
            link(dve.tensor_tensor(E2v, M2[:, :, 0, :], M2[:, :, 1, :], ALU.max))
            dve.tensor_scalar(E2v, E2v, -1.0, None, ALU.mult).then_inc(sem("e2"), 1)
            dve.wait_ge(sem("eT_mm"), 2)
            dve.wait_ge(sem("ep"), 16)
            dve.tensor_copy(ET[0:NT * H1, :], PS[0:NT * H1, 0, 0:P]).then_inc(sem("mt"), 1)
            dve.wait_ge(sem("gru_x"), NT)
            dve.wait_ge(sem("ns"), NT)

            def denominators(h):
                dve.wait_ge(sem(f"hwb{h % 2}"), 16 * (h // 2 + 1))
                w = HW[:, h % 2, :, :]
                f = FRv[:, :, h:h + 1]
                link(dve.tensor_copy(w[:, :, D:D + 1], f))
                dve.tensor_tensor(w[:, :, 2 * D + 2:2 * D + 3], f, w[:, :, D:D + 1], ALU.subtract
                                  ).then_inc(sem("hw_f"), 1)

            def attention_out(n):
                h, g = units1[n]
                b0, nb = G0[g]
                for k0 in range(0, nb, 4):
                    k1 = min(k0 + 4, nb)
                    dve.wait_ge(sem("bank_full1"), h * NT + b0 + k1)
                    link(dve.tensor_scalar(ln[:, 3, k0:k1], PS[:, k0:k1, D], TINY, float(H1), ALU.max, ALU.mult))
                    link(dve.reciprocal(ln[:, 4, k0:k1], ln[:, 3, k0:k1]))
                    for k in range(k0, k1):
                        if h == 0:
                            ins = dve.tensor_scalar(ES[:, b0 + k, :], PS[:, k, 0:D], ln[:, 4, k:k + 1], None, ALU.mult)
                        else:
                            ins = dve.scalar_tensor_tensor(out=ES[:, b0 + k, :], in0=PS[:, k, 0:D],
                                                           scalar=ln[:, 4, k:k + 1], in1=ES[:, b0 + k, :],
                                                           op0=ALU.mult, op1=ALU.add)
                        ins.then_inc(sem("es_done"), 1)

            m = 0
            for n, (h, g) in enumerate(units1):
                b0, nb = G0[g]
                if g == 0:
                    dve.wait_ge(sem(f"mb{h % 2}"), 16 * (h // 2 + 1))
                    denominators(h)
                if h == 0:
                    dve.wait_ge(sem("ab"), (g + 1) * NT)
                for j in range(NT):
                    if m >= NRING:
                        dve.wait_ge(sem("p_exp"), m - NRING + 1)
                    dve.scalar_tensor_tensor(out=T[:, m % NRING, 0:nb * P], in0=MB[:, h % 2, b0 * P:(b0 + nb) * P],
                                             scalar=E1[:, j, h:h + 1], in1=AT[:, j, b0 * P:(b0 + nb) * P],
                                             op0=ALU.add, op1=ALU.min).then_inc(sem("t_built"), 1)
                    if j == 2 and n >= 1:
                        attention_out(n - 1)
                    m += 1
            attention_out(len(units1) - 1)
            dve.wait_ge(sem("p_used"), H1 * len(G0) * NT)
            bias_parts(BR2, BRB2, BP2, BIAS2, "bn", "bias_n")
            for t in range(NT + 1):
                if t < NT:
                    link(dve.tensor_scalar(AT[:, t, :], AT[:, t, :], 0.0, None, ALU.is_equal, saturate=False))
                    blk = AT[:, t, t * P:(t + 1) * P]
                    dve.scalar_tensor_tensor(out=blk, in0=ident[:], scalar=DN[:, t:t + 1], in1=blk, op0=ALU.mult,
                                             op1=ALU.add, saturate=False).then_inc(sem("at_back"), 1)
                if t >= 1:
                    gru_new(NT + t, t - 1, TRZ2, GT2)
            norm_scales(2, "gru_x", 2 * NT)
            for t in range(NT):
                dve.wait_ge(sem("h2"), t + 1)
                dve.wait_ge(sem("hi2"), t + 1)
                dve.tensor_tensor(HHL2[:, t, 1, 0:D], H2[:, t, :], HHL2[:, t, 0, 0:D], ALU.subtract
                                  ).then_inc(sem("lo2"), 1)
            for t in range(NT + 1):
                if t < NT:
                    dve.wait_ge(sem("agg"), t + 1)
                    link(dve.tensor_scalar(ln[:, 4, t:t + 1], PS[:, 1 + t % 2, D:D + 1], 1.0, None, ALU.add))
                    dve.reciprocal(ln[:, 3, t:t + 1], ln[:, 4, t:t + 1]).then_inc(sem("rdeg"), 1)
                if t >= 1:
                    dve.wait_ge(sem("lin"), t)
                    dve.tensor_tensor(X[:, t - 1, :], X[:, t - 1, :], PS[:, 3 + (t - 1) % 2, 0:D], ALU.add
                                      ).then_inc(sem("x_l2"), 1)
            with dve.If(layer3_needed(dve) == 1):
                norm_scales(3, "x_l2", NT)
                dve.wait_ge(sem("w3"), 32)
                for t in range(NT):
                    dve.wait_ge(sem("msg_mm"), t + 1)
                    dve.tensor_tensor(MSG[:, t, :], PS[:, 2 + t % 2, 0:D], B3, ALU.add).then_inc(sem("msg"), 1)

                def weights(m, nb):
                    dve.wait_ge(sem("sens"), m + 1)
                    if m >= 3:
                        dve.wait_ge(sem("w_used"), m - 2)
                    dve.scalar_tensor_tensor(out=WT[:, m % 3, 0:nb * P], in0=DIST[:, m % 4, 0:nb * P], scalar=1.0,
                                             in1=RCP[:, m % 2, 0:nb * P], op0=ALU.is_lt, op1=ALU.mult
                                             ).then_inc(sem("w_built"), 1)

                m = 0
                for g, (b0, nb) in enumerate(G0):
                    for j in range(NT):
                        dve.wait_ge(sem(f"stg{m % 4}"), stg_before[m % 4] + 16 * (m // 4 + 1))
                        if m >= 2:
                            dve.wait_ge(sem("w_built"), m - 1)
                        dve.tensor_scalar(RCP[:, m % 2, 0:nb * P], DIST[:, m % 4, 0:nb * P], 0.0, NEAR_ZERO,
                                          ALU.is_equal, ALU.mult).then_inc(sem("near0"), 1)
                        dve.wait_ge(sem("no_zero"), m + 1)
                        dve.reciprocal(RCP[:, m % 2, 0:nb * P], RCP[:, m % 2, 0:nb * P]).then_inc(sem("rcp"), 1)
                        if j >= 1:
                            weights(m - 1, nb)
                        m += 1
                    weights(m - 1, nb)
                    for k in range(nb):
                        dve.wait_ge(sem("bank_full3"), b0 + k + 1)
                        dve.tensor_tensor(X[:, b0 + k, :], X[:, b0 + k, :], PS[:, k, 0:D], ALU.add).then_inc(sem("x_l3"), 1)
            with dve.Else():
                dve.nop()

        @block.tensor
        def _(pe):
            pe.wait_ge(sem("w0"), 160)
            for kc in range(DC):
                for c in range(DC):
                    ins = pe.matmul(PS[:, 4, kc * 8:kc * 8 + 8], WMT[:, c, kc * P:(kc + 1) * P], ALR[:, c, :],
                                    start=(c == 0), stop=(c == DC - 1))
            ins.then_inc(sem("wal_mm"), 1)
            pe.wait_ge(sem("consts"), 1)

            def transposes(t):
                pe.wait_ge(sem("h"), t + 1)
                if t >= 2:
                    pe.wait_ge(sem("hT"), t - 1)
                for c in range(DC):
                    ins = pe.transpose(PS[:, t % 2, c * P:(c + 1) * P], HS[:, t % 2, c * P:(c + 1) * P], ident[:])
                ins.then_inc(sem("h_tr"), 1)

            transposes(0)
            for t in range(NT):
                if t + 1 < NT:
                    transposes(t + 1)
                pe.wait_ge(sem("hT"), t + 1)
                if t == 0:
                    pe.wait_ge(sem("wal"), 1)
                if t >= 2:
                    pe.wait_ge(sem("htf"), t - 1)
                for c in range(DC):
                    pe.matmul(PS[:, 5, t * 8:t * 8 + 8], HTS[:, t % 2, c * P:(c + 1) * P], WAL[:, c, :],
                              start=(c == 0), stop=(c == DC - 1))
                for c in range(DC):
                    ins = pe.matmul(PS[:, 2 + t % 2, 0:D], HTS[:, t % 2, c * P:(c + 1) * P], WM[:, c, :],
                                    start=(c == 0), stop=(c == DC - 1))
                ins.then_inc(sem("ht_mm"), 1)
            pe.wait_ge(sem("elc"), 1)
            pe.transpose(PS[0:NT * H0, 6, 0:P], ELC, ident[:]).then_inc(sem("elT_mm"), 1)
            pe.wait_ge(sem("el_t"), 1)
            pe.wait_ge(sem("mov"), NT)
            for g, (b0, nb) in enumerate(G0):
                for j in range(NT):
                    pe.wait_ge(sem("stg_used"), g * NT + j + 1)
                    for k in range(nb):
                        if j == 0 and g >= 1:
                            pe.wait_ge(sem("bank_free"), min(banks_before[(g, 0)], banks_before[(g, 0)] - G0[g - 1][1] + k + 1))
                        for q in range(2):
                            ins = pe.matmul(PS[:, k, 0:4 * C0], AT[:, j, (b0 + k) * P:(b0 + k + 1) * P],
                                            MOV[:, j, :, q, C0:2 * C0], start=(j == 0 and q == 0),
                                            stop=(j == NT - 1 and q == 1))
                        if j == NT - 1:
                            ins.then_inc(sem("bank_full"), 1)
                for h in range(H0):
                    n = g * H0 + h
                    for j in range(NT):
                        m = n * NT + j
                        pe.wait_ge(sem("masks_built"), m + 1)
                        for k in range(nb):
                            if j == 0:
                                pe.wait_ge(sem("bank_free"), banks_before[(g, h)] + k + 1)
                            ins = pe.matmul(PS[:, k, 0:4 * C0], MASK[:, m % NMASK, k * P:(k + 1) * P],
                                            MOV[:, j, h, :, :].rearrange("p q c -> p (q c)"), start=(j == 0), stop=(j == NT - 1))
                            if j == NT - 1:
                                ins.then_inc(sem("bank_full"), 1)
                        if j < NT - 1:
                            ins.then_inc(sem("mask_used"), 1)
            pe.wait_ge(sem("w1"), 32)
            for kc in range(DC):
                for h in range(H1):
                    for c in range(DC):
                        ins = pe.matmul(PS[:, 3, kc * H1 + h:kc * H1 + h + 1], GWT[:, h * DC + c, kc * P:(kc + 1) * P],
                                        A1[:, c, h:h + 1], start=(c == 0), stop=(c == DC - 1))
            ins.then_inc(sem("u_mm"), 1)

            def h1_transposes(t):
                pe.wait_ge(sem("h1"), t + 1)
                if t >= 2:
                    pe.wait_ge(sem("h1T"), t - 1)
                for c in range(DC):
                    ins = pe.transpose(PS[:, t % 2, c * P:(c + 1) * P], H32[:, t, c * P:(c + 1) * P], ident[:])
                ins.then_inc(sem("h1_tr"), 1)

            h1_transposes(0)
            pe.wait_ge(sem("u1"), 1)
            for t in range(NT):
                if t + 1 < NT:
                    h1_transposes(t + 1)
                pe.wait_ge(sem("h1T"), t + 1)
                for c in range(DC):
                    ins = pe.matmul(PS[:, 2, t * H1:(t + 1) * H1], SH[:, (t % 2) * 2 * P + c * P:(t % 2) * 2 * P + (c + 1) * P],
                                    U1[:, c, :], start=(c == 0), stop=(c == DC - 1))
                ins.then_inc(sem("hu_mm"), 1)
            pe.wait_ge(sem("diag0"), NT)
            pe.wait_ge(sem("up"), 1)
            for t in range(NT):
                for j in range(NT):
                    ins = pe.matmul(PS[:, 4, t * 3 * H1:(t + 1) * 3 * H1], AT[:, j, t * P:(t + 1) * P], UP[:, j, 0:3 * H1],
                                    start=(j == 0), stop=(j == NT - 1))
            ins.then_inc(sem("e_mm"), 1)
            pe.wait_ge(sem("e2"), 1)
            pe.transpose(PS[0:NT * H1, 5, 0:P], E1[:].rearrange("p t h -> p (t h)"), ident[:]).then_inc(sem("eT_mm"), 1)
            pe.wait_ge(sem("et"), 1)
            pe.wait_ge(sem("lo1"), NT)
            pe.wait_ge(sem("we"), 48)
            pe.wait_ge(sem("bias_e"), 1)
            pe.wait_ge(sem("consts"), 5)

            def gru_mm(count, t, sh, wih, whh, bias):
                pe.wait_ge(sem("sh"), count)
                if count >= 3:
                    pe.wait_ge(sem("trz"), count - 2)
                    pe.wait_ge(sem("u"), count - 2)
                rz = PS[:, 1 + t % 2, :]
                for c in range(DC):
                    pe.matmul(rz, sh[:, c * P:(c + 1) * P], wih[:, c, 0:2 * D], start=(c == 0), stop=False)
                    pe.matmul(rz, sh[:, (DC + c) * P:(DC + c + 1) * P], whh[:, c, 0:2 * D], start=False, stop=False)
                pe.matmul(rz, ones3[0:3, :], bias[0:3, 0:2 * D], start=False, stop=True).then_inc(sem("rz_mm"), 1)
                for q, w in ((0, wih), (1, whh)):
                    o = PS[:, 3 + t % 2, q * D:(q + 1) * D]
                    for c in range(DC):
                        pe.matmul(o, sh[:, (DC * q + c) * P:(DC * q + c + 1) * P], w[:, c, 2 * D:3 * D],
                                  start=(c == 0), stop=False)
                    ins = pe.matmul(o, ones3[0:3, :], bias[0:3, (2 + q) * D:(3 + q) * D], start=False, stop=True)
                ins.then_inc(sem("nb_mm"), 1)

            for t in range(NT + 1):
                if t >= 1:
                    pe.wait_ge(sem("ns_sb"), t)
                    if t >= 2:
                        pe.wait_ge(sem("sh"), t - 1)
                    for c in range(DC):
                        pe.transpose(PS[:, 0, c * P:(c + 1) * P], NSS[:, c * P:(c + 1) * P], ident[:])
                    for c in range(DC):
                        ins = pe.transpose(PS[:, 0, (DC + c) * P:(DC + c + 1) * P], H32[:, t - 1, c * P:(c + 1) * P], ident[:])
                    ins.then_inc(sem("tb"), 1)
                if t < NT:
                    for j in range(NT):
                        for q in range(2):
                            ins = pe.matmul(PS[:, 5, 0:D], AT[:, j, t * P:(t + 1) * P], HHL[:, j, q, 0:D],
                                            start=(j == 0 and q == 0), stop=(j == NT - 1 and q == 1))
                    ins.then_inc(sem("ns"), 1)
                if t >= 1:
                    gru_mm(t, t - 1, SH, WIH, WHH, BIAS)
                    if t >= 2:
                        pe.wait_ge(sem("hw_lo"), H1 * (t - 1))
                    for h in range(H1):
                        for c in range(DC):
                            ins = pe.matmul(PS[:, 6 + h // 2, (h % 2) * D:(h % 2 + 1) * D],
                                            SH[:, (DC + c) * P:(DC + c + 1) * P], GW[:, h * DC + c, :],
                                            start=(c == 0), stop=(c == DC - 1))
                    ins.then_inc(sem("hw_mm"), 1)
            pe.wait_ge(sem("e2"), 2)
            pe.transpose(PS[0:NT * H1, 0, 0:P], E2[:], ident[:]).then_inc(sem("eT_mm"), 1)
            pe.wait_ge(sem("mt"), 1)
            pe.wait_ge(sem("hw_lo"), H1 * NT)
            pe.wait_ge(sem("u"), NT)
            m = 0
            for h in range(H1):
                pe.wait_ge(sem("hw_f"), h + 1)
                for g, (b0, nb) in enumerate(G0):
                    for j in range(NT):
                        pe.wait_ge(sem("p_exp"), m + 1)
                        for k in range(nb):
                            if j == 0 and (h, g) != (0, 0):
                                nb_old = G0[g - 1][1]
                                pe.wait_ge(sem("es_done"), h * NT + b0 - nb_old + min(k + 1, nb_old))
                            weights, w = PW[:, m % NRING, k * P:(k + 1) * P], HW[:, h % 2, j, :]
                            pe.matmul(PS[:, k, 0:D + 1], weights, w[:, 0:D + 1], start=(j == 0), stop=False)
                            ins = pe.matmul(PS[:, k, 0:D + 1], weights, w[:, D + 2:2 * D + 3], start=False,
                                            stop=(j == NT - 1))
                            if j == NT - 1:
                                ins.then_inc(sem("bank_full1"), 1)
                            elif k == nb - 1:
                                ins.then_inc(sem("p_used"), 1)
                        if j == NT - 1:
                            pe.wait_ge(sem("bank_full1"), h * NT + b0 + nb)
                            pe.sem_inc(sem("p_used"), 1)
                        m += 1
            pe.wait_ge(sem("wn"), 32)
            pe.wait_ge(sem("h_back"), 16)
            pe.wait_ge(sem("es_done"), NT * H1)
            pe.wait_ge(sem("bias_n"), 1)

            def node_transposes(t):
                if t >= 2:
                    pe.wait_ge(sem("sh"), NT + t - 1)
                bank = 0 if t % 2 == 0 else 5
                for c in range(DC):
                    pe.transpose(PS[:, bank, c * P:(c + 1) * P], ES[:, t, c * P:(c + 1) * P], ident[:])
                for c in range(DC):
                    ins = pe.transpose(PS[:, bank, (DC + c) * P:(DC + c + 1) * P], H32B[:, t, c * P:(c + 1) * P], ident[:])
                ins.then_inc(sem("tb"), 1)

            node_transposes(0)
            for t in range(NT):
                if t + 1 < NT:
                    node_transposes(t + 1)
                gru_mm(NT + t + 1, t, SH2 if t % 2 == 0 else SH2B, WIH2, WHH2, BIAS2)
            pe.wait_ge(sem("at_back"), NT)
            pe.wait_ge(sem("hhl_pad"), 2)
            pe.wait_ge(sem("lo2"), NT)
            pe.wait_ge(sem("w2"), 16)
            for t in range(NT + 1):
                if t >= 1:
                    pe.wait_ge(sem("nei"), t)
                    if t >= 2:
                        pe.wait_ge(sem("sh3"), t - 1)
                    for c in range(DC):
                        pe.transpose(PS[:, 0, c * P:(c + 1) * P], H2[:, t - 1, c * P:(c + 1) * P], ident[:])
                    for c in range(DC):
                        ins = pe.transpose(PS[:, 0, (DC + c) * P:(DC + c + 1) * P], NEI[:, c * P:(c + 1) * P], ident[:])
                    ins.then_inc(sem("tb2"), 1)
                if t < NT:
                    if t >= 2:
                        pe.wait_ge(sem("nei"), t - 1)
                    o = PS[:, 1 + t % 2, :]
                    for j in range(NT):
                        pe.matmul(o[:, 0:D + 1], AT[:, j, t * P:(t + 1) * P], HHL2[:, j, 0, 0:D + 1], start=(j == 0), stop=False)
                        ins = pe.matmul(o[:, 0:D], AT[:, j, t * P:(t + 1) * P], HHL2[:, j, 1, 0:D], start=False,
                                        stop=(j == NT - 1))
                    ins.then_inc(sem("agg"), 1)
                if t >= 1:
                    pe.wait_ge(sem("sh3"), t)
                    if t >= 3:
                        pe.wait_ge(sem("x_l2"), t - 2)
                    for c in range(2 * DC):
                        ins = pe.matmul(PS[:, 3 + (t - 1) % 2, 0:D], SH3[:, c * P:(c + 1) * P], W2[:, c, :],
                                        start=(c == 0), stop=(c == 2 * DC - 1))
                    ins.then_inc(sem("lin"), 1)
            with pe.If(layer3_needed(pe) == 1):
                pe.wait_ge(sem("w3"), 32)

                def h3_transposes(t):
                    pe.wait_ge(sem("h3"), t + 1)
                    if t >= 2:
                        pe.wait_ge(sem("h3T"), t - 1)
                    for c in range(DC):
                        ins = pe.transpose(PS[:, t % 2, c * P:(c + 1) * P], H3[:, t, c * P:(c + 1) * P], ident[:])
                    ins.then_inc(sem("h3_tr"), 1)

                h3_transposes(0)
                for t in range(NT):
                    if t + 1 < NT:
                        h3_transposes(t + 1)
                    pe.wait_ge(sem("h3T"), t + 1)
                    if t >= 2:
                        pe.wait_ge(sem("msg"), t - 1)
                    for c in range(DC):
                        ins = pe.matmul(PS[:, 2 + t % 2, 0:D], SH4[:, t % 2, c * P:(c + 1) * P], W3[:, c, :],
                                        start=(c == 0), stop=(c == DC - 1))
                    ins.then_inc(sem("msg_mm"), 1)
                pe.wait_ge(sem("msg"), NT)
                m = 0
                for g, (b0, nb) in enumerate(G0):
                    for j in range(NT):
                        pe.wait_ge(sem("w_built"), m + 1)
                        for k in range(nb):
                            if j == 0 and g >= 1:
                                nb_old = G0[g - 1][1]
                                pe.wait_ge(sem("x_l3"), b0 - nb_old + min(k + 1, nb_old))
                            ins = pe.matmul(PS[:, k, 0:D], WT[:, m % 3, k * P:(k + 1) * P], MSG[:, j, :],
                                            start=(j == 0), stop=(j == NT - 1))
                            if j == NT - 1:
                                ins.then_inc(sem("bank_full3"), 1)
                            elif k == nb - 1:
                                ins.then_inc(sem("w_used"), 1)
                        if j == NT - 1:
                            pe.wait_ge(sem("bank_full3"), b0 + nb)
                            pe.sem_inc(sem("w_used"), 1)
                        m += 1
            with pe.Else():
                pe.nop()


def kernel(**inputs):
    import numpy as _np
    import concourse.bacc as _bacc
    from concourse import mybir as _mybir
    from concourse.bass_utils import run_bass_kernel_spmd as _run

    n = inputs["x"].shape[0]
    padded = -(-n // 128) * 128

    def padded_to(a, rows, cols):
        out = _np.zeros((rows, cols), a.dtype)
        out[:a.shape[0], :a.shape[1]] = a
        return out

    a = {k: _np.asarray(v) for k, v in inputs.items()}
    arrays = {
        "x": padded_to(a["x"], padded, a["x"].shape[1]),
        "adjT": padded_to(a["adj"].T, padded, padded),
        "Wm": a["L0_gnn_Wm"],
        "WmT": a["L0_gnn_Wm"].T,
        "al": a["L0_gnn_al"],
        "ar": a["L0_gnn_ar"],
        "adj": padded_to(a["adj"], padded, padded),
        "diag": padded_to(_np.diagonal(a["adj"])[None], 1, padded).reshape(padded // 128, 128).T,
        "gatW": a["L1_gnn_gat_W"],
        "gatWT": a["L1_gnn_gat_W"].transpose(0, 2, 1),
        "gat_a": a["L1_gnn_gat_a"][:, :256, 0].reshape(3, 2, 128).transpose(2, 1, 0),
        "edge_WihT": a["L1_gnn_edge_Wih"].T,
        "edge_WhhT": a["L1_gnn_edge_Whh"].T,
        "edge_bih": a["L1_gnn_edge_bih"],
        "edge_bhh": a["L1_gnn_edge_bhh"],
        "node_WihT": a["L1_gnn_node_Wih"].T,
        "node_WhhT": a["L1_gnn_node_Whh"].T,
        "node_bih": a["L1_gnn_node_bih"],
        "node_bhh": a["L1_gnn_node_bhh"],
        "W2T": a["L2_gnn_W"].T,
        "W3": a["L3_gnn_W"],
        "B3": a["L3_gnn_B"],
    }
    arrays = {k: _np.ascontiguousarray(v) for k, v in arrays.items()}
    nc = _bacc.Bacc("TRN2", target_bir_lowering=False, num_devices=1)
    t_in = {k: nc.dram_tensor(f"in_{k}", v.shape, _mybir.dt.from_np(v.dtype), kind="ExternalInput").ap()
            for k, v in arrays.items()}
    out = nc.dram_tensor("out", (n, a["x"].shape[1]), _mybir.dt.float32, kind="ExternalOutput").ap()
    gnn_stack_kernel(nc, t_in, out)
    r = _run(nc, [{f"in_{k}": v for k, v in arrays.items()}], core_ids=[0])
    return r.results[0]["out"]
```

```python
from contextlib import ExitStack

import numpy as np
import concourse.bass as bass
from concourse import mybir

F32 = mybir.dt.float32
F16 = mybir.dt.float16
BF16 = mybir.dt.bfloat16
FP8 = mybir.dt.float8e4
ALU = mybir.AluOpType
ACT = mybir.ActivationFunctionType
AX = mybir.AxisListType
RMAX = bass.bass_isa.ReduceOp.max

P = 128


def gnn_stack_kernel(nc, t_in, out):
    N, D = t_in["x"].shape[0], 256
    NREAL = out.shape[0]
    NT = N // P
    DC = D // P
    H0, F0 = 4, 64
    C0 = F0 + 1
    H1 = 3
    EPS = 1e-5
    TINY = 1e-30
    NEAR_ZERO = 1e-12
    SLOPE = 0.2
    G0 = [(0, 8), (8, 7), (15, 7)]
    G1 = [(0, 6), (6, 6), (12, 5), (17, 5)]
    LOG2E = 1.0 / float(np.log(2.0))
    LN2 = float(np.log(2.0))
    LN2_HIGH = 0.693359375
    LN2_LOW = LN2 - LN2_HIGH
    ROUND = 1.5 * 2.0 ** 23
    NORM1 = [(0, 15), (15, NT)]
    NORM2 = [(0, 11), (11, 18), (18, NT)]
    NORM_LAG = 3
    HW_EARLY = 17
    NRING = 5
    NMASK = 29
    MASKED = -240.0
    QUARTER = NT * P // 2
    assert N == NT * P and DC == 2

    with ExitStack() as ctx:
        def sb(name, shape, dt=F32):
            return ctx.enter_context(nc.sbuf_tensor(name, shape, dt))

        sems = {}

        def sem(name):
            if name not in sems:
                sems[name] = ctx.enter_context(nc.semaphore(name))
            return sems[name]

        AT = sb("AT", [P, NT, N], FP8)
        X = sb("X", [P, NT, D])
        ident = sb("ident", [P, P])
        scratch = sb("scratch", [P, QUARTER // 2])
        stats = scratch[:, 0:NT * 6].rearrange("p (t c) -> p t c", c=6)
        E3 = scratch[:, NT * 6:NT * 15].rearrange("p (t c) -> p t c", c=9)
        junk = scratch[:].bitcast(BF16)
        mv = sb("mv", [P, NT, 2])
        ln = sb("ln", [P, 6, NT])
        small = sb("small", [P, 32])
        sens_count = sb("sens_count", [P, len(G0) * NT])
        sens_any = sb("sens_any", [P, 1], mybir.dt.int32)
        AR = 30298
        arena = sb("arena", [P, AR])
        PS = ctx.enter_context(nc.psum_tensor("PS", [P, 8, 512], F32))

        class Arena:
            def __init__(self):
                self.at = 0

            def take(self, *dims, dt=F32, size=4):
                n = int(np.prod(dims))
                words = -(-n * size // 4)
                words += words % 2
                v = arena[:, self.at:self.at + words]
                self.at += words
                assert self.at <= AR, (self.at, AR)
                if dt != F32:
                    v = v.bitcast(dt)
                v = v[:, 0:n]
                if len(dims) == 2:
                    v = v.rearrange("p (a b) -> p a b", a=dims[0])
                if len(dims) == 3:
                    v = v.rearrange("p (a b c) -> p a b c", a=dims[0], b=dims[1])
                if len(dims) == 4:
                    v = v.rearrange("p (a b c d) -> p a b c d", a=dims[0], b=dims[1], c=dims[2])
                return v

        a0 = Arena()
        MOV = a0.take(NT, H0, 2, 2 * C0, dt=F16, size=2)
        mask_at = a0.at
        MASK = a0.take(NMASK, 1024, dt=FP8, size=1)
        a0m = Arena()
        a0m.at = mask_at
        HTF = a0m.take(NT, H0 * C0)
        assert a0m.at <= a0.at
        ELB = a0.take(2, 1024)
        STG = a0.take(4, 1024)
        e_at = a0.at
        E = a0.take(8, 4 * C0)
        DA = a0.take(8, 4 * C0)
        a0w = Arena()
        a0w.at = e_at
        WM = a0w.take(DC, D)
        WMT = a0w.take(DC, D)
        TS = a0w.take(3, 4 * 2 * C0)
        HS = a0w.take(2, D)
        HTS = a0w.take(2, D)
        assert a0w.at <= a0.at
        ALR = a0.take(DC, 2 * H0)
        WAL = a0.take(DC, 2 * H0)
        ELR = a0.take(NT, 2 * H0)
        ELC = a0.take(NT * H0)
        NER = a0.take(NT, H0)
        COEF = a0.take(4, NT * H0)
        MX = a0.take(NT * H0)
        ELT = a0.take(P)
        RD = a0.take(8, H0)

        a1 = Arena()
        H32 = a1.take(NT, D)
        HHL = a1.take(NT, 2, D + 2, dt=F16, size=2)
        EB = a1.take(H1, N)
        ab = Arena()
        ab.at = a1.at - H1 * N
        GWT = ab.take(H1 * DC, D)
        AROW = a1.take(2, QUARTER)
        HT1 = AROW[:, 0, 0:4 * P].rearrange("p (s c) -> p s c", s=2)
        WIH = a1.take(DC, 3 * D)
        WHH = a1.take(DC, 3 * D)
        GW = a1.take(H1 * DC, D)
        gru_at = a1.at
        SH = a1.take(4 * P)
        NSS = a1.take(D)
        au = Arena()
        au.at = a1.at - D
        UP = au.take(NT, 3 * H1 + 1, dt=F16, size=2)
        HWS = a1.take(H1, 2, D + 2, dt=F16, size=2)
        TRZ = a1.take(2 * D)
        GT = a1.take(D)
        GN = a1.take(D)
        GD = TRZ[:, 0:D]
        BIAS = a1.take(4 * D, dt=BF16, size=2)
        tmp = Arena()
        tmp.at = gru_at + 4 * P + D
        BR = tmp.take(4 * D)
        BRB = tmp.take(2 * D)
        assert tmp.at <= a1.at - 2 * D
        BP = scratch[:, 0:2 * D].bitcast(BF16)
        a2 = Arena()
        HW = a2.take(2, NT, 2 * (D + 2), dt=F16, size=2)
        MB = a2.take(2, N)
        a2t_at = a2.at
        T = a2.take(NRING, 1024, dt=BF16, size=2)
        PW = a2.take(NRING, 1024, dt=BF16, size=2)
        a2t = Arena()
        a2t.at = a2t_at
        SH2 = a2t.take(4 * P)
        TRZ2 = a2t.take(2 * D)
        GT2 = a2t.take(D)
        GN2 = a2t.take(D)
        GD2 = TRZ2[:, 0:D]
        SH2B = a2t.take(4 * P)
        assert a2t.at <= a2.at
        ES = a2.take(NT, D)
        WIH2 = a2.take(DC, 3 * D)
        last_at = a2.at
        BIAS2 = a2.take(4 * D, dt=BF16, size=2)
        BRB2 = a2.take(2 * D)
        BP2 = BP
        a2h = Arena()
        a2h.at = NT * (D + 2)
        H32B = a2h.take(NT, D)
        a2m = Arena()
        a2m.at = 2 * NT * (D + 2) + N
        WHH2 = a2m.take(DC, 3 * D)
        BR2 = a2m.take(4 * D)
        assert a2m.at <= a2t_at
        a3 = Arena()
        HHL2 = a3.take(NT, 2, D + 2, dt=F16, size=2)
        H2 = a3.take(NT, D)
        NEI = a3.take(D)
        SH3 = a3.take(4 * P)
        a3.at = last_at
        W2 = a3.take(2 * DC, D)
        a4 = Arena()
        MSG = a4.take(NT, D)
        H3 = a4.take(NT, D)
        W3 = a4.take(DC, D)
        B3 = a4.take(D)
        SH4 = a4.take(2, DC * P)
        DIST = a4.take(4, 1024)
        RCP = a4.take(2, 1024)
        WT = a4.take(3, 1024)
        DN = sb("DN", [P, NT])
        NOTI = sb("NOTI", [P, P])
        E1 = sb("E1", [P, NT, H1])
        E2 = sb("E2", [P, NT * H1])
        FR = ln[:, 0:H1, :].rearrange("p a b -> p (a b)")
        M2 = sb("M2", [P, NT, 2, H1])
        A1 = sb("A1", [P, DC, H1])
        U1 = sb("U1", [P, DC, H1])
        ET = sb("ET", [P, P])
        ones3 = sb("ones3", [4, P], BF16)
        EP_D = nc.dram_tensor("e_rows", [NT, H1, P], F32, kind="Internal").ap()
        MN_D = nc.dram_tensor("m_rows", [NT, H1, P], F32, kind="Internal").ap()
        H_D = nc.dram_tensor("h_saved", [P, NT, D], F32, kind="Internal").ap()
        HW_D = nc.dram_tensor("hw_saved", [H1, P, NT, 2 * (D + 2)], F16, kind="Internal").ap()

        EL_D = nc.dram_tensor("el_rows", [NT, H0, P], F32, kind="Internal").ap()

        block = ctx.enter_context(nc.Block())
        adjT = t_in["adjT"].rearrange("(j p) i -> j p i", p=P)
        units0 = [(g, h) for g in range(len(G0)) for h in range(H0)]
        chunk0 = [(g, j) for g in range(len(G0)) for j in range(NT)]
        banks_before = {}
        cnt = 0
        for g, (b0, nb) in enumerate(G0):
            for u in range(H0 + 1):
                banks_before[(g, u)] = cnt
                cnt += nb
        stg_before = [16 * len(range(q, len(chunk0), 4)) for q in range(4)]

        norm_parts = {0: [(0, NT)], 1: NORM1, 2: NORM2, 3: [(0, NT)]}

        def parts_before(q):
            return sum(len(norm_parts[i]) for i in range(q))

        def norm2_blocks(t):
            blocks = []
            for t0, t1 in NORM2[:-1]:
                per_step = 3 if t1 < NT - 6 else 4
                first = t0 + per_step * (t - t1 - NORM_LAG)
                blocks += list(range(max(first, t0), min(first + per_step, t1))) if t >= t1 + NORM_LAG else []
            return blocks

        def row_items(t):
            done = [min(2 * NT, max(0, 2 * NT * s // (NT - 1))) for s in (t - 1, t)]
            return [divmod(i, 2) for i in range(*done)]

        units1 = [(h, g) for h in range(H1) for g in range(len(G0))]

        def layer3_needed(eng):
            eng.wait_ge(sem("flag"), 1)
            return eng.value_load(sens_any[0:1, 0:1], min_val=0, max_val=1)

        def link_on(eng, name):
            s = sem(name)
            state = [0]

            def link(ins):
                state[0] += 1
                ins.then_inc(s, 1)
                eng.wait_ge(s, state[0])
            return link

        @block.sync
        def _(sp):
            for c in range(2):
                sp.dma_start(X[:, c * 11:(c + 1) * 11, :],
                             t_in["x"][c * 11 * P:(c + 1) * 11 * P, :].rearrange("(t p) d -> p t d", p=P)
                             ).then_inc(sem("x_in"), 16)

            def load_chunk(n):
                g, j = chunk0[n]
                b0, nb = G0[g]
                if n >= 4:
                    sp.wait_ge(sem("stg_used"), n - 3)
                    sp.wait_ge(sem("checked"), n - 3)
                sp.dma_start(STG[:, n % 4, 0:nb * P], adjT[j, :, b0 * P:(b0 + nb) * P]
                             ).then_inc(sem(f"stg{n % 4}"), 16)

            def load_el(n):
                g, h = units0[n]
                b0, nb = G0[g]
                if n >= 2:
                    sp.wait_ge(sem("masks_built"), (n - 1) * NT)
                sp.dma_start(ELB[:, n % 2, 0:nb * P].rearrange("p (k q) -> p k q", q=P),
                             EL_D[b0:b0 + nb, h, :].partition_broadcast(P)).then_inc(sem(f"elb{n % 2}"), 16)

            for n in range(NT):
                load_chunk(n)
            sp.wait_ge(sem("el_t"), 1)
            sp.dma_start(EL_D.rearrange("t h q -> (t h) q"), ELT[0:NT * H0, :]).then_inc(sem("el_rows"), 16)
            sp.wait_ge(sem("el_rows"), 16)
            load_el(0)
            load_el(1)
            for q in range(4):
                for n in range(NT + 11 * q, NT + 11 * (q + 1)):
                    load_chunk(n)
                load_el(2 + q)
            for n in range(6, len(units0)):
                load_el(n)
            sp.dma_start(A1[:], t_in["gat_a"]).then_inc(sem("w1"), 16)
            sp.dma_start(DN[:], t_in["diag"]).then_inc(sem("dn"), 16)
            sp.wait_ge(sem("bank_full"), banks_before[(len(G0) - 1, H0)] + G0[-1][1])
            sp.dma_start(GWT.rearrange("p (h c) d -> p h c d", h=H1),
                         t_in["gatWT"].rearrange("h (c p) k -> p h c k", p=P)).then_inc(sem("w1"), 16)

            def load_bias(raw, rawb, ih, hh, name):
                sp.dma_start(raw[0:3, 0:3 * D], t_in[ih].partition_broadcast(3)).then_inc(sem(name), 16)
                sp.dma_start(raw[0:3, 3 * D:4 * D], t_in[hh][2 * D:3 * D].partition_broadcast(3)).then_inc(sem(name), 16)
                sp.dma_start(rawb[0:3, :], t_in[hh][0:2 * D].partition_broadcast(3)).then_inc(sem(name), 16)

            sp.wait_ge(sem("x_l0"), 1)
            load_bias(BR, BRB, "edge_bih", "edge_bhh", "be")
            sp.dma_start(WIH, t_in["edge_WihT"].rearrange("(c p) n -> p c n", p=P)).then_inc(sem("we"), 16)
            sp.dma_start(WHH, t_in["edge_WhhT"].rearrange("(c p) n -> p c n", p=P)).then_inc(sem("we"), 16)
            sp.dma_start(GW.rearrange("p (h c) d -> p h c d", h=H1),
                         t_in["gatW"].rearrange("h (c p) k -> p h c k", p=P)).then_inc(sem("we"), 16)
            sp.wait_ge(sem("h1"), NT)
            sp.dma_start(H_D, H32).then_inc(sem("h_saved"), 16)
            sp.wait_ge(sem("et"), 1)
            sp.wait_ge(sem("u_mm"), 1)
            sp.dma_start(EP_D.rearrange("t h q -> (t h) q"), ET[0:NT * H1, :]).then_inc(sem("ep"), 16)
            sp.wait_ge(sem("ep"), 16)
            for h in range(H1):
                sp.dma_start(EB[:, h, :].rearrange("p (t q) -> p t q", q=P),
                             EP_D[:, h, :].partition_broadcast(P)).then_inc(sem("eb"), 16)

            def save_products(t):
                sp.wait_ge(sem("hw_lo"), H1 * (t + 1))
                sp.dma_start(HW_D[:, :, t, :].rearrange("h p c -> p h c"),
                             HWS.rearrange("p h a c -> p h (a c)")).then_inc(sem("hw_dma"), 16)

            def load_rows(t, c):
                if t >= 1:
                    sp.wait_ge(sem("rmax"), H1 * (2 * t + c - 1))
                sp.dma_start(AROW[:, c, :], t_in["adj"][t * P:(t + 1) * P, c * QUARTER:(c + 1) * QUARTER]
                             ).then_inc(sem(f"arow{c}"), 16)

            def load_products(h, t0, t1):
                sp.dma_start(HW[:, h % 2, t0:t1, :], HW_D[h, :, t0:t1, :]).then_inc(sem(f"hwb{h % 2}"), 16)

            def load_maxima(h):
                sp.dma_start(MB[:, h % 2, :].rearrange("p (t q) -> p t q", q=P),
                             MN_D[:, h, :].partition_broadcast(P)).then_inc(sem(f"mb{h % 2}"), 16)

            for t in range(NT + 1):
                if t >= 2:
                    save_products(t - 2)
                for r, c in row_items(t + 1):
                    load_rows(r, c)
            sp.wait_ge(sem("mt"), 1)
            sp.dma_start(MN_D.rearrange("t h q -> (t h) q"), ET[0:NT * H1, :]).then_inc(sem("mn"), 16)
            sp.wait_ge(sem("mn"), 16)
            load_maxima(0)
            sp.wait_ge(sem("hw_dma"), 16 * (NT - 1))
            sp.wait_ge(sem("gru_x"), HW_EARLY + 2)
            sp.wait_ge(sem("h_saved"), 16)
            load_products(0, 0, HW_EARLY)
            save_products(NT - 1)
            sp.wait_ge(sem("hw_dma"), 16 * NT)
            sp.wait_ge(sem("gru_x"), NT)
            load_products(0, HW_EARLY, NT)
            load_products(1, 0, NT)
            load_maxima(1)
            sp.dma_start(WIH2, t_in["node_WihT"].rearrange("(c p) n -> p c n", p=P)).then_inc(sem("wn"), 16)
            sp.wait_ge(sem("bank_full1"), NT)
            load_products(2, 0, NT)
            load_maxima(2)
            sp.wait_ge(sem("bank_full1"), 2 * NT)
            sp.dma_start(H32B, H_D).then_inc(sem("h_back"), 16)
            sp.dma_start(WHH2, t_in["node_WhhT"].rearrange("(c p) n -> p c n", p=P)).then_inc(sem("wn"), 16)
            load_bias(BR2, BRB2, "node_bih", "node_bhh", "bn")
            sp.wait_ge(sem("nb_mm"), 2 * NT)
            sp.dma_start(W2, t_in["W2T"].rearrange("(c p) n -> p c n", p=P)).then_inc(sem("w2"), 16)
            def write_out(done, before):
                for g, (b0, nb) in enumerate(G0):
                    sp.wait_ge(sem(done), before + b0 + nb)
                    last = b0 + nb == NT
                    full = nb - 1 if last else nb
                    sp.dma_start(out[b0 * P:(b0 + full) * P, :].rearrange("(t p) d -> p t d", p=P),
                                 X[:, b0:b0 + full, :]).then_inc(sem("out"), 16)
                    if last:
                        sp.dma_start(out[(NT - 1) * P:NREAL, :], X[0:NREAL - (NT - 1) * P, NT - 1, :]
                                     ).then_inc(sem("out"), 16)
                sp.wait_ge(sem("out"), 16 * (len(G0) + 1))

            with sp.If(layer3_needed(sp) == 1):
                sp.wait_ge(sem("x_l2"), NT)
                sp.dma_start(W3, t_in["W3"].rearrange("(c p) n -> p c n", p=P)).then_inc(sem("w3"), 16)
                sp.dma_start(B3, t_in["B3"].partition_broadcast(P)).then_inc(sem("w3"), 16)
                for m, (g, j) in enumerate(chunk0):
                    b0, nb = G0[g]
                    if m >= 4:
                        sp.wait_ge(sem("w_built"), m - 3)
                    sp.dma_start(DIST[:, m % 4, 0:nb * P], adjT[j, :, b0 * P:(b0 + nb) * P]
                                 ).then_inc(sem(f"stg{m % 4}"), 16)
                write_out("x_l3", 0)
            with sp.Else():
                write_out("x_l2", 0)

        @block.gpsimd
        def _(pool):
            link = link_on(pool, "pool_chain")
            link(pool.memset(ident[:], 0.0))
            pool.affine_select(out=ident[:], in_=ident[:], compare_op=ALU.not_equal, fill=1.0, base=0,
                               pattern=[[-1, P]], channel_multiplier=1).then_inc(sem("consts"), 1)
            pool.wait_ge(sem("consts"), 1)
            pool.tensor_scalar(NOTI[:], ident[:], -1.0, 1.0, ALU.mult, ALU.add).then_inc(sem("consts"), 1)
            pool.memset(ones3[:], 1.0).then_inc(sem("consts"), 1)
            pool.memset(ALR, 0.0).then_inc(sem("consts"), 1)
            pool.memset(HTF.rearrange("p t (h c) -> p t h c", c=C0)[:, :, :, F0:C0], 1.0).then_inc(sem("consts"), 1)
            pool.wait_ge(sem("er_max"), 1)
            pool.partition_all_reduce(small[:, 4:8], small[:, 0:4], P, RMAX).then_inc(sem("er_gmax"), 1)
            pool.wait_ge(sem("coef"), 1)
            for t in range(NT):
                if t >= 3:
                    pool.wait_ge(sem("mov"), t - 2)
                pool.wait_ge(sem("htf"), t + 1)
                pool.tensor_tensor(TS[:, t % 3, :].rearrange("p (h b c) -> p h b c", h=H0, b=2)[:, :, 1, :],
                                   HTF[:, t, :].rearrange("p (h c) -> p h c", c=C0),
                                   COEF[:, 3, t * H0:(t + 1) * H0].unsqueeze(2).to_broadcast([P, H0, C0]),
                                   ALU.mult).then_inc(sem("t_d"), 1)
            for n, (g, h) in enumerate(units0):
                b0, nb = G0[g]
                if n == H0 + 2:
                    pool.wait_ge(sem("sens_max"), 1)
                    pool.partition_all_reduce(small[:, 21:22], small[:, 20:21], P, RMAX).then_inc(sem("sens_gmax"), 1)
                Ev = E[:, 0:nb, :]
                Dv = DA[:, 0:nb, h * C0:(h + 1) * C0]
                co = [COEF[:, q, :].rearrange("p (t h) -> p t h", h=H0)[:, b0:b0 + nb, h:h + 1].to_broadcast([P, nb, C0])
                      for q in range(2)]
                if n < len(units0) - 1:
                    pool.wait_ge(sem("bank_free"), banks_before[(g, h + 1)] + nb)
                    link(pool.tensor_tensor(Ev[:, :, 0:C0], Ev[:, :, 0:C0], Ev[:, :, 2 * C0:3 * C0], ALU.add))
                    link(pool.tensor_tensor(Ev[:, :, C0:2 * C0], Ev[:, :, C0:2 * C0], Ev[:, :, 3 * C0:4 * C0], ALU.add))
                    link(pool.tensor_tensor(Ev[:, :, C0:2 * C0], Dv, Ev[:, :, C0:2 * C0], ALU.subtract))
                    link(pool.tensor_tensor(Ev[:, :, 0:C0], Ev[:, :, 0:C0], co[0], ALU.mult))
                    link(pool.tensor_tensor(Ev[:, :, C0:2 * C0], Ev[:, :, C0:2 * C0], co[1], ALU.mult))
                    ins = pool.tensor_tensor(Dv, Ev[:, :, 0:C0], Ev[:, :, C0:2 * C0], ALU.add)
                    ins.then_inc(sem("e_used"), 1)
                heads = H0 if g < len(G0) - 1 else H0 - 1
                if h == heads - 1:
                    pool.wait_ge(sem("rden0"), g + 1)
                    for hh in range(heads):
                        Dh = DA[:, 0:nb, hh * C0:hh * C0 + F0]
                        Xh = X[:, b0:b0 + nb, hh * F0:(hh + 1) * F0]
                        link(pool.tensor_tensor(Dh, Dh, RD[:, 0:nb, hh:hh + 1].to_broadcast([P, nb, F0]), ALU.mult))
                        link(pool.tensor_tensor(Xh, Xh, Dh, ALU.add))
                    pool.sem_inc(sem("da_used"), 1)
            pool.wait_ge(sem("bank_full"), banks_before[(len(G0) - 1, H0)] + G0[-1][1])
            pool.memset(HHL[:, :, 0, D:D + 2], 1.0).then_inc(sem("hhl_pad"), 1)
            for t in range(NT):
                pool.wait_ge(sem("h1"), t + 1)
                pool.tensor_copy(HHL[:, t, 0, 0:D], H32[:, t, :]).then_inc(sem("hi1"), 1)
            pool.wait_ge(sem("e_min"), 1)
            pool.partition_all_reduce(small[:, 12:15], small[:, 8:11], P, RMAX).then_inc(sem("shift"), 1)

            def gru_tail(count, t, h_blk, trz, n, d):
                pool.wait_ge(sem("n"), count)
                link(pool.tensor_tensor(d, h_blk, n, ALU.subtract))
                link(pool.tensor_scalar(trz[:, D:2 * D], trz[:, D:2 * D], 0.5, 0.5, ALU.mult, ALU.add))
                link(pool.tensor_tensor(d, trz[:, D:2 * D], d, ALU.mult))
                link(pool.tensor_tensor(d, d, n, ALU.add))
                link(pool.tensor_scalar(d, d, DN[:, t:t + 1], 1.0, ALU.mult, ALU.mult))
                pool.tensor_tensor(X[:, t, :], X[:, t, :], d, ALU.add).then_inc(sem("gru_x"), 1)

            pool.wait_ge(sem("dn"), 16)
            for t in range(NT + 2):
                for r, half in row_items(t):
                    c, b = divmod(r, NT // 2)
                    if half == c:
                        pool.wait_ge(sem(f"arow{c}"), 16 * (r + 1))
                        blk = AROW[:, c, b * P:(b + 1) * P]
                        pool.tensor_tensor(blk, blk, NOTI[:], ALU.mult).then_inc(sem("row_diag"), 1)
                if t >= 2:
                    gru_tail(t - 1, t - 2, H32[:, t - 2, :], TRZ, GN, GD)
            pool.wait_ge(sem("bank_full1"), H1 * NT)
            pool.memset(HHL2[:, :, 0, D:D + 2], 1.0).then_inc(sem("hhl_pad"), 1)
            pool.wait_ge(sem("h_back"), 16)
            for t in range(NT):
                gru_tail(NT + t + 1, t, H32B[:, t, :], TRZ2, GN2, GD2)
            with pool.If(layer3_needed(pool) == 1):
                m = 0
                for g, (b0, nb) in enumerate(G0):
                    for j in range(NT):
                        pool.wait_ge(sem("near0"), m + 1)
                        v = RCP[:, m % 2, 0:nb * P]
                        pool.tensor_tensor(v, v, DIST[:, m % 4, 0:nb * P], ALU.add).then_inc(sem("no_zero"), 1)
                        m += 1
            with pool.Else():
                pool.nop()

        @block.scalar
        def _(act):
            act.dma_start(WM, t_in["Wm"].rearrange("(c p) n -> p c n", p=P)).then_inc(sem("w0"), 16)
            act.dma_start(WMT, t_in["WmT"].rearrange("(c p) n -> p c n", p=P)).then_inc(sem("w0"), 16)
            act.wait_ge(sem("consts"), 5)
            for h in range(H0):
                for q, name in enumerate(("al", "ar")):
                    act.dma_start(ALR[F0 * (h % 2):F0 * (h % 2) + F0, h // 2, q * H0 + h:q * H0 + h + 1],
                                  t_in[name].unsqueeze(1)).then_inc(sem("w0"), 16)

            def norm_sqrt(q, part=0):
                t0, t1 = norm_parts[q][part]
                count = parts_before(q) + part + 1
                act.wait_ge(sem("var"), count)
                act.activation(ln[:, 1, t0:t1], ln[:, 0, t0:t1], ACT.Sqrt).then_inc(sem("sqrt"), 1)

            def norm_ready(q, part=0):
                act.wait_ge(sem("rstd"), parts_before(q) + part + 1)

            def norm_block(q, t, full, high=None):
                act.activation(full[:, t, :], X[:, t, :], ACT.Relu, bias=ln[:, 5, t:t + 1],
                               scale=ln[:, 2, t:t + 1]).then_inc(sem(f"h{q}"), 1)
                if high is not None:
                    act.activation(high[:, t, 0, 0:D], X[:, t, :], ACT.Relu, bias=ln[:, 5, t:t + 1],
                                   scale=ln[:, 2, t:t + 1]).then_inc(sem(f"hi{q}"), 1)

            norm_sqrt(0)
            norm_ready(0)

            def norm(t):
                if t >= 2:
                    act.wait_ge(sem("h_tr"), t - 1)
                act.activation(HS[:, t % 2, :], X[:, t, :], ACT.Relu, bias=ln[:, 5, t:t + 1],
                               scale=ln[:, 2, t:t + 1]).then_inc(sem("h"), 1)

            def ht_out(t):
                act.wait_ge(sem("ht_mm"), t + 1)
                act.activation(HTF[:, t, :].rearrange("p (h c) -> p h c", c=C0)[:, :, 0:F0],
                               PS[:, 2 + t % 2, 0:D].rearrange("p (h c) -> p h c", c=F0), ACT.Copy
                               ).then_inc(sem("htf"), 1)

            norm(0)
            for t in range(NT):
                if t + 1 < NT:
                    norm(t + 1)
                act.wait_ge(sem("h_tr"), t + 1)
                if t >= 2:
                    act.wait_ge(sem("ht_mm"), t - 1)
                act.activation(HTS[:, t % 2, :], PS[:, t % 2, 0:D], ACT.Copy).then_inc(sem("hT"), 1)
                if t >= 1:
                    ht_out(t - 1)
            ht_out(NT - 1)
            act.wait_ge(sem("arg"), 1)
            act.activation(COEF, COEF, ACT.Exp).then_inc(sem("coef"), 1)
            act.wait_ge(sem("coef"), 1)
            for t in range(NT):
                act.wait_ge(sem("t_b"), t + 1)
                act.wait_ge(sem("t_d"), t + 1)
                act.activation(MOV[:, t, :, 0, :], TS[:, t % 3, :].rearrange("p (h c) -> p h c", h=H0), ACT.Copy
                               ).then_inc(sem("mov_hi"), 1)
            pos = 0
            casts = list(range(NT, 3 * NT))
            for g, (b0, nb) in enumerate(G0):
                for u in range(H0 + 1):
                    if g == 0 and u < 4:
                        for n in casts[11 * u:11 * (u + 1)]:
                            gg, j = chunk0[n]
                            bb, nn = G0[gg]
                            act.wait_ge(sem(f"stg{n % 4}"), 16 * (n // 4 + 1))
                            act.activation(AT[:, j, bb * P:(bb + nn) * P], STG[:, n % 4, 0:nn * P], ACT.Copy, saturate=False
                                           ).then_inc(sem("stg_used"), 1)
                    if u == 0:
                        if g >= 1:
                            act.wait_ge(sem("da_used"), g)
                    elif g * H0 + u - 1 >= 1:
                        act.wait_ge(sem("e_used"), g * H0 + u - 1)
                    if g == len(G0) - 1 and u == H0:
                        norm_sqrt(1, 0)
                    if g == 0 and u == 0:
                        act.wait_ge(sem("mov"), NT)
                    for k in range(nb):
                        act.wait_ge(sem("bank_full"), banks_before[(g, u)] + k + 1)
                        act.activation((DA if u == 0 else E)[:, k, :], PS[:, k, 0:4 * C0], ACT.Copy
                                       ).then_inc(sem("bank_free"), 1)
            def turn_mask(g, j):
                blk = AT[:, j, G0[g][0] * P:(G0[g][0] + G0[g][1]) * P]
                act.activation(blk, blk, ACT.Copy, scale=-MASKED, bias=MASKED, saturate=False).then_inc(sem("ab"), 1)

            norm_ready(1, 0)
            for t in range(NT + 1):
                if t == NORM1[1][0] // 2:
                    norm_sqrt(1, 1)
                if t == NORM1[1][0]:
                    norm_ready(1, 1)
                if t < NT:
                    norm_block(1, t, H32)
                t -= 1
                if t < 0:
                    continue
                act.wait_ge(sem("h1_tr"), t + 1)
                if t >= 2:
                    act.wait_ge(sem("hu_mm"), t - 1)
                act.activation(HT1[:, t % 2, :], PS[:, t % 2, 0:D], ACT.Copy
                               ).then_inc(sem("h1T"), 1)
            act.wait_ge(sem("hu_mm"), NT)
            act.wait_ge(sem("fr_arg"), 1)
            act.activation(FR, FR, ACT.Exp).then_inc(sem("fr"), 1)
            act.wait_ge(sem("bias_e"), 1)

            for t in range(NT + 2):
                if t == 2:
                    act.wait_ge(sem("fr"), 1)
                if t >= 2:
                    act.wait_ge(sem("rz_mm"), t - 1)
                    if t >= 3:
                        act.wait_ge(sem("gru_x"), t - 2)
                    act.activation(TRZ, PS[:, 1 + t % 2, :], ACT.Tanh, scale=0.5).then_inc(sem("trz"), 1)
                    act.wait_ge(sem("hw_mm"), t - 1)
                    if t >= 3:
                        act.wait_ge(sem("hw_dma"), 16 * (t - 2))
                    for h in range(H1):
                        act.activation(HWS[:, h, 0, 0:D], PS[:, 6 + h // 2, (h % 2) * D:(h % 2 + 1) * D], ACT.Copy,
                                       scale=FR[:, (t - 2) * H1 + h:(t - 2) * H1 + h + 1]).then_inc(sem("hw_hi"), 1)
                if 1 <= t <= NT:
                    act.wait_ge(sem("tb"), t)
                    act.activation(SH, PS[:, 0, :], ACT.Copy).then_inc(sem("sh"), 1)
                if t >= 2:
                    act.wait_ge(sem("u"), t - 1)
                    act.activation(GN, GT, ACT.Tanh).then_inc(sem("n"), 1)
                if t < NT:
                    act.wait_ge(sem("ns"), t + 1)
                    act.activation(NSS, PS[:, 5, 0:D], ACT.Copy).then_inc(sem("ns_sb"), 1)
                for g in range(len(G0) - 1):
                    last = G0[g][0] + G0[g][1]
                    for j in range(4 * (t - last), min(4 * (t - last + 1), NT)):
                        if j >= 0:
                            turn_mask(g, j)
            act.wait_ge(sem("gru_x"), NT)

            m = 0
            for h in range(H1):
                for g, (b0, nb) in enumerate(G0):
                    for j in range(NT):
                        act.wait_ge(sem("t_built"), m + 1)
                        if m >= NRING:
                            act.wait_ge(sem("p_used"), m - NRING + 1)
                        act.activation(PW[:, m % NRING, 0:nb * P], T[:, m % NRING, 0:nb * P], ACT.Exp, scale=LN2
                                       ).then_inc(sem("p_exp"), 1)
                        if h == 0 and g < 2 and j % 2 == 1:
                            turn_mask(2, g * NT // 2 + j // 2)
                        m += 1
            for t in range(NT + 1):
                if t < NT:
                    act.wait_ge(sem("tb"), NT + t + 1)
                    if t >= 2:
                        act.wait_ge(sem("rz_mm"), NT + t - 1)
                    act.activation(SH2 if t % 2 == 0 else SH2B, PS[:, 0 if t % 2 == 0 else 5, :], ACT.Copy
                                   ).then_inc(sem("sh"), 1)
                if t >= 1:
                    act.wait_ge(sem("rz_mm"), NT + t)
                    if t >= 2:
                        act.wait_ge(sem("gru_x"), NT + t - 1)
                    act.activation(TRZ2, PS[:, 1 + (t - 1) % 2, :], ACT.Tanh, scale=0.5).then_inc(sem("trz"), 1)
                    act.wait_ge(sem("u"), NT + t)
                    act.activation(GN2, GT2, ACT.Tanh).then_inc(sem("n"), 1)
                for part, (t0, t1) in enumerate(NORM2[:-1]):
                    if t == t1 + NORM_LAG:
                        norm_sqrt(2, part)
                        norm_ready(2, part)
                for b in norm2_blocks(t):
                    norm_block(2, b, H2, HHL2)
            norm_sqrt(2, len(NORM2) - 1)
            norm_ready(2, len(NORM2) - 1)
            for b in range(NORM2[-1][0], NT):
                norm_block(2, b, H2, HHL2)
            for t in range(NT + 1):
                if t >= 1:
                    act.wait_ge(sem("tb2"), t)
                    act.activation(SH3, PS[:, 0, :], ACT.Copy).then_inc(sem("sh3"), 1)
                if t < NT:
                    act.wait_ge(sem("rdeg"), t + 1)
                    act.activation(NEI, PS[:, 1 + t % 2, 0:D], ACT.Copy, scale=ln[:, 3, t:t + 1]).then_inc(sem("nei"), 1)
            with act.If(layer3_needed(act) == 1):
                act.wait_ge(sem("x_l2"), NT)
                norm_sqrt(3)
                norm_ready(3)
                for t in range(NT):
                    norm_block(3, t, H3)
                for t in range(NT):
                    act.wait_ge(sem("h3_tr"), t + 1)
                    if t >= 2:
                        act.wait_ge(sem("msg_mm"), t - 1)
                    act.activation(SH4[:, t % 2, :], PS[:, t % 2, 0:D], ACT.Copy).then_inc(sem("h3T"), 1)
                m = 0
                for g, (b0, nb) in enumerate(G0):
                    for j in range(NT):
                        act.wait_ge(sem("rcp"), m + 1)
                        v = RCP[:, m % 2, 0:nb * P]
                        act.activation(v, v, ACT.Square, bias=small[:, 17:18]).then_inc(sem("sq"), 1)
                        act.wait_ge(sem("sq"), m + 1)
                        act.activation(v, v, ACT.Exp, scale=-2.0).then_inc(sem("sens"), 1)
                        m += 1
            with act.Else():
                act.nop()

        @block.vector
        def _(dve):
            link = link_on(dve, "dve_chain")

            def norm_stats(q, t):
                dve.bn_stats(stats[:, t, :], X[:, t, :]).then_inc(sem("st"), 1)
                dve.wait_ge(sem("st"), q * NT + t + 1)
                dve.bn_aggr(mv[:, t, :], stats[:, t, :]).then_inc(sem("ag"), 1)

            def norm_scales(q, part=0):
                t0, t1 = norm_parts[q][part]
                count = parts_before(q) + part + 1
                row = [ln[:, i, t0:t1] for i in range(6)]
                dve.wait_ge(sem("ag"), q * NT + t1)
                dve.tensor_scalar(row[0], mv[:, t0:t1, 1], EPS, None, ALU.add).then_inc(sem("var"), 1)
                dve.wait_ge(sem("sqrt"), count)
                dve.wait_ge(sem("var"), count)
                link(dve.reciprocal(row[3], row[1]))
                link(dve.tensor_tensor(row[4], row[3], row[3], ALU.mult))
                link(dve.tensor_tensor(row[4], row[4], row[0], ALU.mult))
                link(dve.tensor_scalar(row[4], row[4], -0.5, 1.5, ALU.mult, ALU.add))
                link(dve.tensor_tensor(row[2], row[3], row[4], ALU.mult))
                dve.scalar_tensor_tensor(out=row[5], in0=mv[:, t0:t1, 0], scalar=-1.0, in1=row[2],
                                         op0=ALU.mult, op1=ALU.mult).then_inc(sem("rstd"), 1)

            for t in range(NT):
                if t == 0:
                    dve.wait_ge(sem("x_in"), 32)
                norm_stats(0, t)
            norm_scales(0)

            def count_sensitive(n):
                nb = G0[chunk0[n][0]][1]
                if n >= 1:
                    dve.wait_ge(sem("checked"), n)
                dve.scalar_tensor_tensor(out=junk[:, 0:nb * P], in0=STG[:, n % 4, 0:nb * P], scalar=1.0,
                                         in1=STG[:, n % 4, 0:nb * P], op0=ALU.is_lt, op1=ALU.logical_and,
                                         accum_out=sens_count[:, n:n + 1]).then_inc(sem("checked"), 1)

            dve.wait_ge(sem("rstd"), 1)
            for t in range(8):
                nb = G0[0][1]
                dve.wait_ge(sem(f"stg{t % 4}"), 16 * (t // 4 + 1))
                dve.tensor_copy(AT[:, t, 0:nb * P], STG[:, t % 4, 0:nb * P], saturate=False).then_inc(sem("stg_used"), 1)
                count_sensitive(t)
            dve.wait_ge(sem("wal_mm"), 1)
            dve.tensor_copy(WAL, PS[:, 4, 0:2 * DC * H0].rearrange("p (c n) -> p c n", c=DC)).then_inc(sem("wal"), 1)
            for t in range(8, NT):
                nb = G0[0][1]
                dve.wait_ge(sem(f"stg{t % 4}"), 16 * (t // 4 + 1))
                dve.tensor_copy(AT[:, t, 0:nb * P], STG[:, t % 4, 0:nb * P], saturate=False).then_inc(sem("stg_used"), 1)
                count_sensitive(t)
            dve.wait_ge(sem("ht_mm"), NT)
            link(dve.tensor_copy(ELR, PS[:, 5, 0:NT * 2 * H0].rearrange("p (t n) -> p t n", n=2 * H0)))
            dve.tensor_copy(ELC.rearrange("p (t h) -> p t h", h=H0), ELR[:, :, 0:H0]).then_inc(sem("elc"), 1)
            dve.tensor_reduce(small[:, 0:4], ELR[:, :, H0:2 * H0].rearrange("p t h -> p h t"), AX.X, ALU.max
                              ).then_inc(sem("er_max"), 1)
            link(dve.tensor_scalar(NER, ELR[:, :, H0:2 * H0], -1.0, None, ALU.mult))
            dve.wait_ge(sem("er_gmax"), 1)
            Gb = small[:, 4:8].unsqueeze(1).to_broadcast([P, NT, H0])
            CO = [COEF[:, q, :].rearrange("p (t h) -> p t h", h=H0) for q in range(4)]
            MXv = MX.rearrange("p (t h) -> p t h", h=H0)
            link(dve.tensor_tensor(CO[0], ELR[:, :, 0:H0], Gb, ALU.add))
            link(dve.scalar_tensor_tensor(out=MXv, in0=CO[0], scalar=SLOPE, in1=CO[0], op0=ALU.mult, op1=ALU.max))
            link(dve.scalar_tensor_tensor(out=CO[1], in0=CO[0], scalar=SLOPE, in1=MXv, op0=ALU.mult, op1=ALU.subtract))
            link(dve.tensor_tensor(CO[0], CO[0], MXv, ALU.subtract))
            link(dve.tensor_tensor(CO[2], ELR[:, :, H0:2 * H0], Gb, ALU.subtract))
            dve.tensor_scalar(CO[3], CO[2], SLOPE, None, ALU.mult).then_inc(sem("arg"), 1)
            dve.wait_ge(sem("elT_mm"), 1)
            dve.tensor_copy(ELT[0:NT * H0, :], PS[0:NT * H0, 6, 0:P]).then_inc(sem("el_t"), 1)
            dve.wait_ge(sem("coef"), 1)

            def low_part(t):
                dve.wait_ge(sem("mov_hi"), t + 1)
                dve.tensor_tensor(MOV[:, t, :, 1, :], TS[:, t % 3, :].rearrange("p (h c) -> p h c", h=H0),
                                  MOV[:, t, :, 0, :], ALU.subtract).then_inc(sem("mov"), 1)

            for t in range(NT):
                if t >= 3:
                    dve.wait_ge(sem("mov"), t - 2)
                dve.wait_ge(sem("htf"), t + 1)
                dve.tensor_tensor(TS[:, t % 3, :].rearrange("p (h b c) -> p h b c", h=H0, b=2)[:, :, 0, :],
                                  HTF[:, t, :].rearrange("p (h c) -> p h c", c=C0),
                                  COEF[:, 2, t * H0:(t + 1) * H0].unsqueeze(2).to_broadcast([P, H0, C0]),
                                  ALU.mult).then_inc(sem("t_b"), 1)
                if t >= 1:
                    low_part(t - 1)
            low_part(NT - 1)
            dve.wait_ge(sem("mov"), NT)
            dve.wait_ge(sem("t_d"), NT)

            def reciprocals(g, heads):
                dve.wait_ge(sem("e_used"), g * H0 + heads)
                RDg = RD[:, 0:G0[g][1], 0:heads]
                link(dve.tensor_scalar(RDg, DA[:, 0:G0[g][1], :].rearrange("p k (h c) -> p k h c", c=C0)
                                       [:, :, 0:heads, F0], TINY, None, ALU.max))
                dve.reciprocal(RDg, RDg).then_inc(sem("rden0"), 1)

            for n, (g, h) in enumerate(units0):
                b0, nb = G0[g]
                dve.wait_ge(sem(f"elb{n % 2}"), 16 * (n // 2 + 1))
                for j in range(NT):
                    m = n * NT + j
                    if g >= 1 and h == 0:
                        dve.wait_ge(sem("stg_used"), g * NT + j + 1)
                    if g == 0 and h == 0 and j == 0:
                        dve.wait_ge(sem("stg_used"), NT)
                    if m >= NMASK:
                        n_old, j_old = divmod(m - NMASK, NT)
                        g_old, h_old = units0[n_old]
                        if j_old < NT - 1:
                            dve.wait_ge(sem("mask_used"), n_old * (NT - 1) + j_old + 1)
                        else:
                            dve.wait_ge(sem("bank_full"), banks_before[(g_old, h_old + 1)] + G0[g_old][1])
                    dve.scalar_tensor_tensor(out=MASK[:, m % NMASK, 0:nb * P], in0=ELB[:, n % 2, 0:nb * P],
                                             scalar=NER[:, j, h:h + 1], in1=AT[:, j, b0 * P:(b0 + nb) * P],
                                             op0=ALU.is_gt, op1=ALU.mult, saturate=False).then_inc(sem("masks_built"), 1)
                    if n == len(units0) - 1 and 3 <= j < 3 + NORM1[0][1]:
                        if j == 3:
                            dve.wait_ge(sem("da_used"), len(G0) - 1)
                        norm_stats(1, j - 3)
                    if g == 0 and j % 2 == 1:
                        nn = NT + h * NT // 2 + j // 2
                        dve.wait_ge(sem(f"stg{nn % 4}"), 16 * (nn // 4 + 1))
                        count_sensitive(nn)
                if n == H0:
                    dve.wait_ge(sem("checked"), len(chunk0))
                    dve.tensor_reduce(small[:, 20:21], sens_count[:], AX.X, ALU.max).then_inc(sem("sens_max"), 1)
                if n == H0 + 3:
                    dve.wait_ge(sem("sens_gmax"), 1)
                    dve.tensor_scalar(sens_any[:], small[:, 21:22], 0.0, None, ALU.is_gt).then_inc(sem("flag"), 1)
                if h == 0 and g >= 1:
                    reciprocals(g - 1, H0)
            norm_scales(1, 0)
            reciprocals(len(G0) - 1, H0 - 1)
            dve.wait_ge(sem("bank_full"), banks_before[(len(G0) - 1, 1)])
            for t in range(NT):
                blk = AT[:, t, t * P:(t + 1) * P]
                dve.tensor_tensor(blk, blk, NOTI[:], ALU.mult, saturate=False).then_inc(sem("diag0"), 1)
            g, h = units0[-1]
            b0, nb = G0[g]
            Ev, Dv = E[:, 0:nb, :], DA[:, 0:nb, h * C0:(h + 1) * C0]
            co = [COEF[:, q, :].rearrange("p (t h) -> p t h", h=H0)[:, b0:b0 + nb, h:h + 1].to_broadcast([P, nb, C0])
                  for q in range(2)]
            dve.wait_ge(sem("bank_free"), banks_before[(g, h + 1)] + nb)
            link(dve.tensor_tensor(Ev[:, :, 0:2 * C0], Ev[:, :, 0:2 * C0], Ev[:, :, 2 * C0:4 * C0], ALU.add))
            link(dve.tensor_tensor(Ev[:, :, C0:2 * C0], Dv, Ev[:, :, C0:2 * C0], ALU.subtract))
            link(dve.tensor_tensor(Ev[:, :, 0:C0], Ev[:, :, 0:C0], co[0], ALU.mult))
            link(dve.tensor_tensor(Ev[:, :, C0:2 * C0], Ev[:, :, C0:2 * C0], co[1], ALU.mult))
            link(dve.tensor_tensor(Dv, Ev[:, :, 0:C0], Ev[:, :, C0:2 * C0], ALU.add))
            link(dve.tensor_scalar(RD[:, 0:nb, h:h + 1], Dv[:, :, F0:C0], TINY, None, ALU.max))
            link(dve.reciprocal(RD[:, 0:nb, h:h + 1], RD[:, 0:nb, h:h + 1]))
            link(dve.tensor_tensor(Dv[:, :, 0:F0], Dv[:, :, 0:F0], RD[:, 0:nb, h:h + 1].to_broadcast([P, nb, F0]), ALU.mult))
            Xh = X[:, b0:b0 + nb, h * F0:(h + 1) * F0]
            link(dve.tensor_tensor(Xh, Xh, Dv[:, :, 0:F0], ALU.add))
            dve.wait_ge(sem("da_used"), len(G0))
            dve.sem_inc(sem("x_l0"), 1)
            dve.wait_ge(sem("u_mm"), 1)
            dve.tensor_copy(U1[:], PS[:, 3, 0:DC * H1].rearrange("p (c h) -> p c h", c=DC)).then_inc(sem("u1"), 1)
            for t in range(*NORM1[1]):
                norm_stats(1, t)
            norm_scales(1, 1)
            dve.memset(small[:, 17:18], -1.0).then_inc(sem("minus1"), 1)
            for t in range(NT):
                dve.wait_ge(sem("hi1"), t + 1)
                dve.tensor_tensor(HHL[:, t, 1, 0:D], H32[:, t, :], HHL[:, t, 0, 0:D], ALU.subtract
                                  ).then_inc(sem("lo1"), 1)

            def bias_sum(br, brb, loaded, count):
                dve.wait_ge(sem(loaded), count)
                link(dve.tensor_tensor(br[0:3, 0:2 * D], br[0:3, 0:2 * D], brb[0:3, :], ALU.add))

            def bias_part(k, br, bp, bias):
                link(dve.tensor_copy(bp[0:3, :], br[0:3, :]))
                if k < 2:
                    link(dve.tensor_tensor(br[0:3, :], br[0:3, :], bp[0:3, :], ALU.subtract))
                if k == 0:
                    ins = dve.tensor_scalar(bias[0:3, :], bp[0:3, :], ident[0:3, 0:1], None, ALU.mult)
                else:
                    ins = dve.scalar_tensor_tensor(out=bias[0:3, :], in0=bp[0:3, :], scalar=ident[0:3, k:k + 1],
                                                   in1=bias[0:3, :], op0=ALU.mult, op1=ALU.add)
                link(ins)

            dve.wait_ge(sem("hu_mm"), NT)
            link(dve.tensor_copy(E1[:], PS[:, 2, 0:NT * H1].rearrange("p (t h) -> p t h", h=H1)))
            for k in range(3):
                part = UP[:, :, k * H1:(k + 1) * H1]
                link(dve.tensor_copy(part, E1[:]))
                if k < 2:
                    link(dve.tensor_tensor(E1[:], E1[:], part, ALU.subtract))
            dve.sem_inc(sem("up"), 1)
            bias_sum(BR, BRB, "be", 48)
            for k in range(3):
                bias_part(k, BR, BP, BIAS)
            dve.sem_inc(sem("bias_e"), 1)
            for h in range(H1):
                dve.memset(HWS[:, h, :, D:D + 2], 1.0).then_inc(sem("hws_pad"), 1)
            dve.wait_ge(sem("e_mm"), 1)
            link(dve.tensor_copy(E3, PS[:, 4, 0:NT * 3 * H1].rearrange("p (t c) -> p t c", t=NT)))
            link(dve.tensor_tensor(E1[:], E3[:, :, H1:2 * H1], E3[:, :, 2 * H1:3 * H1], ALU.add))
            link(dve.tensor_tensor(E1[:], E3[:, :, 0:H1], E1[:], ALU.add))
            link(dve.scalar_tensor_tensor(out=E1[:], in0=E1[:], scalar=SLOPE, in1=E1[:], op0=ALU.mult, op1=ALU.max))
            E2v = E2[:].rearrange("p (t h) -> p t h", h=H1)
            FRv = FR.rearrange("p (t h) -> p t h", h=H1)
            link(dve.tensor_scalar(E2v, E1[:], LOG2E, ROUND, ALU.mult, ALU.add))
            link(dve.tensor_scalar(E2v, E2v, -ROUND, None, ALU.add))
            link(dve.tensor_reduce(small[:, 8:11], E2v.rearrange("p t h -> p h t"), AX.X, ALU.min))
            dve.tensor_scalar(small[:, 8:11], small[:, 8:11], -1.0, None, ALU.mult).then_inc(sem("e_min"), 1)
            link(dve.scalar_tensor_tensor(out=FRv, in0=E2v, scalar=-LN2_HIGH, in1=E1[:], op0=ALU.mult, op1=ALU.add))
            dve.scalar_tensor_tensor(out=FRv, in0=E2v, scalar=-LN2_LOW, in1=FRv, op0=ALU.mult, op1=ALU.add
                                     ).then_inc(sem("fr_arg"), 1)
            dve.wait_ge(sem("shift"), 1)
            shift = small[:, 12:15].unsqueeze(1).to_broadcast([P, NT, H1])
            dve.tensor_tensor(E1[:], E2v, shift, ALU.add).then_inc(sem("e2"), 1)
            dve.wait_ge(sem("eT_mm"), 1)
            dve.tensor_copy(ET[0:NT * H1, :], PS[0:NT * H1, 5, 0:P]).then_inc(sem("et"), 1)
            dve.wait_ge(sem("eb"), 16 * H1)

            def row_max(t, c):
                dve.wait_ge(sem(f"arow{c}"), 16 * (t + 1))
                if t // (NT // 2) == c:
                    dve.wait_ge(sem("row_diag"), t + 1)
                for h in range(H1):
                    if t + c + h > 0:
                        dve.wait_ge(sem("rmax"), H1 * (2 * t + c) + h)
                    dve.tensor_tensor_reduce(junk, AROW[:, c, :],
                                             EB[:, h, c * QUARTER:(c + 1) * QUARTER], 1.0, 0.0, ALU.mult, ALU.max,
                                             M2[:, t, c, h:h + 1]).then_inc(sem("rmax"), 1)

            def gru_new(count, t, trz, gt):
                dve.wait_ge(sem("trz"), count)
                dve.wait_ge(sem("nb_mm"), count)
                if count >= 2:
                    dve.wait_ge(sem("n"), count - 1)
                nb_bank = PS[:, 3 + t % 2, :]
                link(dve.scalar_tensor_tensor(out=gt, in0=trz[:, 0:D], scalar=1.0, in1=nb_bank[:, D:2 * D],
                                              op0=ALU.add, op1=ALU.mult))
                dve.scalar_tensor_tensor(out=gt, in0=gt, scalar=0.5, in1=nb_bank[:, 0:D],
                                         op0=ALU.mult, op1=ALU.add).then_inc(sem("u"), 1)

            for t in range(NT + 2):
                if t >= 2:
                    gru_new(t - 1, t - 2, TRZ, GT)
                if t >= 2:
                    for h in range(H1):
                        dve.wait_ge(sem("hw_hi"), H1 * (t - 1))
                        dve.scalar_tensor_tensor(out=HWS[:, h, 1, 0:D], in0=PS[:, 6 + h // 2, (h % 2) * D:(h % 2 + 1) * D],
                                                 scalar=FR[:, (t - 2) * H1 + h:(t - 2) * H1 + h + 1],
                                                 in1=HWS[:, h, 0, 0:D], op0=ALU.mult, op1=ALU.subtract).then_inc(sem("hw_lo"), 1)
                for r, c in row_items(t):
                    row_max(r, c)
                if t == NT - 1:
                    dve.wait_ge(sem("rmax"), 2 * NT * H1)
                    link(dve.tensor_tensor(E2v, M2[:, :, 0, :], M2[:, :, 1, :], ALU.max))
                    dve.tensor_scalar(E2v, E2v, -1.0, None, ALU.mult).then_inc(sem("e2"), 1)
                if t == NT:
                    dve.wait_ge(sem("eT_mm"), 2)
                    dve.wait_ge(sem("ep"), 16)
                    dve.tensor_copy(ET[0:NT * H1, :], PS[0:NT * H1, 0, 0:P]).then_inc(sem("mt"), 1)

            def denominators(h, t0, t1, loads):
                dve.wait_ge(sem(f"hwb{h % 2}"), 16 * loads)
                w = HW[:, h % 2, t0:t1, :]
                f = FRv[:, t0:t1, h:h + 1]
                link(dve.tensor_copy(w[:, :, D:D + 1], f))
                dve.tensor_tensor(w[:, :, 2 * D + 2:2 * D + 3], f, w[:, :, D:D + 1], ALU.subtract
                                  ).then_inc(sem("hw_f"), 1)

            def attention_out(n):
                h, g = units1[n]
                b0, nb = G0[g]
                for k0 in range(0, nb, 4):
                    k1 = min(k0 + 4, nb)
                    dve.wait_ge(sem("bank_full1"), h * NT + b0 + k1)
                    link(dve.tensor_scalar(ln[:, 3, k0:k1], PS[:, k0:k1, D], TINY, float(H1), ALU.max, ALU.mult))
                    link(dve.reciprocal(ln[:, 4, k0:k1], ln[:, 3, k0:k1]))
                    for k in range(k0, k1):
                        if h == 0:
                            ins = dve.tensor_scalar(ES[:, b0 + k, :], PS[:, k, 0:D], ln[:, 4, k:k + 1], None, ALU.mult)
                        else:
                            ins = dve.scalar_tensor_tensor(out=ES[:, b0 + k, :], in0=PS[:, k, 0:D],
                                                           scalar=ln[:, 4, k:k + 1], in1=ES[:, b0 + k, :],
                                                           op0=ALU.mult, op1=ALU.add)
                        ins.then_inc(sem("es_done"), 1)

            m = 0
            for n, (h, g) in enumerate(units1):
                b0, nb = G0[g]
                if g == 0:
                    dve.wait_ge(sem(f"mb{h % 2}"), 16 * (h // 2 + 1))
                    denominators(h, 0, HW_EARLY if h == 0 else NT, [1, 1, 3][h])
                if h == 0:
                    dve.wait_ge(sem("ab"), (g + 1) * NT)
                for j in range(NT):
                    if m >= NRING:
                        dve.wait_ge(sem("p_exp"), m - NRING + 1)
                    dve.scalar_tensor_tensor(out=T[:, m % NRING, 0:nb * P], in0=MB[:, h % 2, b0 * P:(b0 + nb) * P],
                                             scalar=E1[:, j, h:h + 1], in1=AT[:, j, b0 * P:(b0 + nb) * P],
                                             op0=ALU.add, op1=ALU.min).then_inc(sem("t_built"), 1)
                    if n == 0 and j == 3:
                        denominators(0, HW_EARLY, NT, 2)
                    if n == 1 and j == 2:
                        dve.wait_ge(sem("gru_x"), NT)
                    if n == 7 and j == 5:
                        bias_sum(BR2, BRB2, "bn", 48)
                    if n == 7 and j in (7, 11, 15):
                        bias_part((j - 7) // 4, BR2, BP2, BIAS2)
                    if j == 2 and n >= 1:
                        attention_out(n - 1)
                    m += 1
            attention_out(len(units1) - 1)
            dve.sem_inc(sem("bias_n"), 1)
            dve.wait_ge(sem("p_used"), H1 * len(G0) * NT)

            def low_half(t):
                dve.wait_ge(sem("h2"), t + 1)
                dve.wait_ge(sem("hi2"), t + 1)
                dve.tensor_tensor(HHL2[:, t, 1, 0:D], H2[:, t, :], HHL2[:, t, 0, 0:D], ALU.subtract
                                  ).then_inc(sem("lo2"), 1)

            for t in range(NT + 1):
                if t < NT:
                    link(dve.tensor_scalar(AT[:, t, :], AT[:, t, :], 0.0, None, ALU.is_equal, saturate=False))
                    blk = AT[:, t, t * P:(t + 1) * P]
                    dve.scalar_tensor_tensor(out=blk, in0=ident[:], scalar=DN[:, t:t + 1], in1=blk, op0=ALU.mult,
                                             op1=ALU.add, saturate=False).then_inc(sem("at_back"), 1)
                if t >= 1:
                    gru_new(NT + t, t - 1, TRZ2, GT2)
                if t >= NORM_LAG:
                    dve.wait_ge(sem("gru_x"), NT + t - NORM_LAG + 1)
                    norm_stats(2, t - NORM_LAG)
                for part, (t0, t1) in enumerate(NORM2[:-1]):
                    if t == t1 + NORM_LAG:
                        norm_scales(2, part)
                for b in norm2_blocks(t - 1):
                    low_half(b)
            for b in norm2_blocks(NT):
                low_half(b)
            for t in range(NT - NORM_LAG + 1, NT):
                dve.wait_ge(sem("gru_x"), NT + t + 1)
                norm_stats(2, t)
            norm_scales(2, len(NORM2) - 1)
            for b in range(NORM2[-1][0], NT):
                low_half(b)
            for t in range(NT + 1):
                if t < NT:
                    dve.wait_ge(sem("agg"), t + 1)
                    link(dve.tensor_scalar(ln[:, 4, t:t + 1], PS[:, 1 + t % 2, D:D + 1], 1.0, None, ALU.add))
                    dve.reciprocal(ln[:, 3, t:t + 1], ln[:, 4, t:t + 1]).then_inc(sem("rdeg"), 1)
                if t >= 1:
                    dve.wait_ge(sem("lin"), t)
                    dve.tensor_tensor(X[:, t - 1, :], X[:, t - 1, :], PS[:, 3 + (t - 1) % 2, 0:D], ALU.add
                                      ).then_inc(sem("x_l2"), 1)
            with dve.If(layer3_needed(dve) == 1):
                dve.wait_ge(sem("x_l2"), NT)
                for t in range(NT):
                    norm_stats(3, t)
                norm_scales(3)
                dve.wait_ge(sem("w3"), 32)
                for t in range(NT):
                    dve.wait_ge(sem("msg_mm"), t + 1)
                    dve.tensor_tensor(MSG[:, t, :], PS[:, 2 + t % 2, 0:D], B3, ALU.add).then_inc(sem("msg"), 1)

                def weights(m, nb):
                    dve.wait_ge(sem("sens"), m + 1)
                    if m >= 3:
                        dve.wait_ge(sem("w_used"), m - 2)
                    dve.scalar_tensor_tensor(out=WT[:, m % 3, 0:nb * P], in0=DIST[:, m % 4, 0:nb * P], scalar=1.0,
                                             in1=RCP[:, m % 2, 0:nb * P], op0=ALU.is_lt, op1=ALU.mult
                                             ).then_inc(sem("w_built"), 1)

                m = 0
                for g, (b0, nb) in enumerate(G0):
                    for j in range(NT):
                        dve.wait_ge(sem(f"stg{m % 4}"), stg_before[m % 4] + 16 * (m // 4 + 1))
                        if m >= 2:
                            dve.wait_ge(sem("w_built"), m - 1)
                        dve.tensor_scalar(RCP[:, m % 2, 0:nb * P], DIST[:, m % 4, 0:nb * P], 0.0, NEAR_ZERO,
                                          ALU.is_equal, ALU.mult).then_inc(sem("near0"), 1)
                        dve.wait_ge(sem("no_zero"), m + 1)
                        dve.reciprocal(RCP[:, m % 2, 0:nb * P], RCP[:, m % 2, 0:nb * P]).then_inc(sem("rcp"), 1)
                        if j >= 1:
                            weights(m - 1, nb)
                        m += 1
                    weights(m - 1, nb)
                    for k in range(nb):
                        dve.wait_ge(sem("bank_full3"), b0 + k + 1)
                        dve.tensor_tensor(X[:, b0 + k, :], X[:, b0 + k, :], PS[:, k, 0:D], ALU.add).then_inc(sem("x_l3"), 1)
            with dve.Else():
                dve.nop()

        @block.tensor
        def _(pe):
            pe.wait_ge(sem("w0"), 160)
            for kc in range(DC):
                for c in range(DC):
                    ins = pe.matmul(PS[:, 4, kc * 8:kc * 8 + 8], WMT[:, c, kc * P:(kc + 1) * P], ALR[:, c, :],
                                    start=(c == 0), stop=(c == DC - 1))
            ins.then_inc(sem("wal_mm"), 1)
            pe.wait_ge(sem("consts"), 1)

            def transposes(t):
                pe.wait_ge(sem("h"), t + 1)
                if t >= 2:
                    pe.wait_ge(sem("hT"), t - 1)
                for c in range(DC):
                    ins = pe.transpose(PS[:, t % 2, c * P:(c + 1) * P], HS[:, t % 2, c * P:(c + 1) * P], ident[:])
                ins.then_inc(sem("h_tr"), 1)

            transposes(0)
            for t in range(NT):
                if t + 1 < NT:
                    transposes(t + 1)
                pe.wait_ge(sem("hT"), t + 1)
                if t == 0:
                    pe.wait_ge(sem("wal"), 1)
                if t >= 2:
                    pe.wait_ge(sem("htf"), t - 1)
                for c in range(DC):
                    pe.matmul(PS[:, 5, t * 8:t * 8 + 8], HTS[:, t % 2, c * P:(c + 1) * P], WAL[:, c, :],
                              start=(c == 0), stop=(c == DC - 1))
                for c in range(DC):
                    ins = pe.matmul(PS[:, 2 + t % 2, 0:D], HTS[:, t % 2, c * P:(c + 1) * P], WM[:, c, :],
                                    start=(c == 0), stop=(c == DC - 1))
                ins.then_inc(sem("ht_mm"), 1)
            pe.wait_ge(sem("elc"), 1)
            pe.transpose(PS[0:NT * H0, 6, 0:P], ELC, ident[:]).then_inc(sem("elT_mm"), 1)
            pe.wait_ge(sem("el_t"), 1)
            pe.wait_ge(sem("mov"), NT)
            for g, (b0, nb) in enumerate(G0):
                for j in range(NT):
                    pe.wait_ge(sem("stg_used"), g * NT + j + 1)
                    for k in range(nb):
                        if j == 0 and g >= 1:
                            pe.wait_ge(sem("bank_free"), min(banks_before[(g, 0)], banks_before[(g, 0)] - G0[g - 1][1] + k + 1))
                        for q in range(2):
                            ins = pe.matmul(PS[:, k, 0:4 * C0], AT[:, j, (b0 + k) * P:(b0 + k + 1) * P],
                                            MOV[:, j, :, q, C0:2 * C0], start=(j == 0 and q == 0),
                                            stop=(j == NT - 1 and q == 1))
                        if j == NT - 1:
                            ins.then_inc(sem("bank_full"), 1)
                for h in range(H0):
                    n = g * H0 + h
                    for j in range(NT):
                        m = n * NT + j
                        pe.wait_ge(sem("masks_built"), m + 1)
                        for k in range(nb):
                            if j == 0:
                                pe.wait_ge(sem("bank_free"), banks_before[(g, h)] + k + 1)
                            ins = pe.matmul(PS[:, k, 0:4 * C0], MASK[:, m % NMASK, k * P:(k + 1) * P],
                                            MOV[:, j, h, :, :].rearrange("p q c -> p (q c)"), start=(j == 0), stop=(j == NT - 1))
                            if j == NT - 1:
                                ins.then_inc(sem("bank_full"), 1)
                        if j < NT - 1:
                            ins.then_inc(sem("mask_used"), 1)
            pe.wait_ge(sem("w1"), 32)
            pe.wait_ge(sem("bank_free"), banks_before[(len(G0) - 1, H0)] + G0[-1][1])
            for kc in range(DC):
                for h in range(H1):
                    for c in range(DC):
                        ins = pe.matmul(PS[:, 3, kc * H1 + h:kc * H1 + h + 1], GWT[:, h * DC + c, kc * P:(kc + 1) * P],
                                        A1[:, c, h:h + 1], start=(c == 0), stop=(c == DC - 1))
            ins.then_inc(sem("u_mm"), 1)

            def h1_transposes(t):
                pe.wait_ge(sem("h1"), t + 1)
                if t >= 2:
                    pe.wait_ge(sem("h1T"), t - 1)
                for c in range(DC):
                    ins = pe.transpose(PS[:, t % 2, c * P:(c + 1) * P], H32[:, t, c * P:(c + 1) * P], ident[:])
                ins.then_inc(sem("h1_tr"), 1)

            h1_transposes(0)
            pe.wait_ge(sem("u1"), 1)
            for t in range(NT):
                if t + 1 < NT:
                    h1_transposes(t + 1)
                pe.wait_ge(sem("h1T"), t + 1)
                for c in range(DC):
                    ins = pe.matmul(PS[:, 2, t * H1:(t + 1) * H1], HT1[:, t % 2, c * P:(c + 1) * P],
                                    U1[:, c, :], start=(c == 0), stop=(c == DC - 1))
                ins.then_inc(sem("hu_mm"), 1)
            pe.wait_ge(sem("diag0"), NT)
            pe.wait_ge(sem("up"), 1)
            for t in range(NT):
                for j in range(NT):
                    ins = pe.matmul(PS[:, 4, t * 3 * H1:(t + 1) * 3 * H1], AT[:, j, t * P:(t + 1) * P], UP[:, j, 0:3 * H1],
                                    start=(j == 0), stop=(j == NT - 1))
            ins.then_inc(sem("e_mm"), 1)
            pe.wait_ge(sem("e2"), 1)
            pe.transpose(PS[0:NT * H1, 5, 0:P], E1[:].rearrange("p t h -> p (t h)"), ident[:]).then_inc(sem("eT_mm"), 1)
            pe.wait_ge(sem("et"), 1)
            pe.wait_ge(sem("lo1"), NT)
            pe.wait_ge(sem("we"), 48)
            pe.wait_ge(sem("bias_e"), 1)
            pe.wait_ge(sem("consts"), 5)

            def gru_mm(count, t, sh, wih, whh, bias):
                pe.wait_ge(sem("sh"), count)
                if count >= 3:
                    pe.wait_ge(sem("trz"), count - 2)
                    pe.wait_ge(sem("u"), count - 2)
                rz = PS[:, 1 + t % 2, :]
                for c in range(DC):
                    pe.matmul(rz, sh[:, c * P:(c + 1) * P], wih[:, c, 0:2 * D], start=(c == 0), stop=False)
                    pe.matmul(rz, sh[:, (DC + c) * P:(DC + c + 1) * P], whh[:, c, 0:2 * D], start=False, stop=False)
                pe.matmul(rz, ones3[0:3, :], bias[0:3, 0:2 * D], start=False, stop=True).then_inc(sem("rz_mm"), 1)
                for q, w in ((0, wih), (1, whh)):
                    o = PS[:, 3 + t % 2, q * D:(q + 1) * D]
                    for c in range(DC):
                        pe.matmul(o, sh[:, (DC * q + c) * P:(DC * q + c + 1) * P], w[:, c, 2 * D:3 * D],
                                  start=(c == 0), stop=False)
                    ins = pe.matmul(o, ones3[0:3, :], bias[0:3, (2 + q) * D:(3 + q) * D], start=False, stop=True)
                ins.then_inc(sem("nb_mm"), 1)

            for t in range(NT + 1):
                if t >= 1:
                    pe.wait_ge(sem("ns_sb"), t)
                    if t >= 2:
                        pe.wait_ge(sem("sh"), t - 1)
                    for c in range(DC):
                        pe.transpose(PS[:, 0, c * P:(c + 1) * P], NSS[:, c * P:(c + 1) * P], ident[:])
                    for c in range(DC):
                        ins = pe.transpose(PS[:, 0, (DC + c) * P:(DC + c + 1) * P], H32[:, t - 1, c * P:(c + 1) * P], ident[:])
                    ins.then_inc(sem("tb"), 1)
                if t < NT:
                    for j in range(NT):
                        for q in range(2):
                            ins = pe.matmul(PS[:, 5, 0:D], AT[:, j, t * P:(t + 1) * P], HHL[:, j, q, 0:D],
                                            start=(j == 0 and q == 0), stop=(j == NT - 1 and q == 1))
                    ins.then_inc(sem("ns"), 1)
                if t >= 1:
                    gru_mm(t, t - 1, SH, WIH, WHH, BIAS)
                    if t == NT:
                        pe.wait_ge(sem("e2"), 2)
                        pe.transpose(PS[0:NT * H1, 0, 0:P], E2[:], ident[:]).then_inc(sem("eT_mm"), 1)
                    if t >= 2:
                        pe.wait_ge(sem("hw_lo"), H1 * (t - 1))
                    for h in range(H1):
                        for c in range(DC):
                            ins = pe.matmul(PS[:, 6 + h // 2, (h % 2) * D:(h % 2 + 1) * D],
                                            SH[:, (DC + c) * P:(DC + c + 1) * P], GW[:, h * DC + c, :],
                                            start=(c == 0), stop=(c == DC - 1))
                    ins.then_inc(sem("hw_mm"), 1)
            pe.wait_ge(sem("mt"), 1)
            pe.wait_ge(sem("hw_lo"), H1 * NT)
            pe.wait_ge(sem("u"), NT)
            m = 0
            for h in range(H1):
                pe.wait_ge(sem("hw_f"), [1, 3, 4][h])
                for g, (b0, nb) in enumerate(G0):
                    for j in range(NT):
                        pe.wait_ge(sem("p_exp"), m + 1)
                        if m == HW_EARLY:
                            pe.wait_ge(sem("hw_f"), 2)
                        for k in range(nb):
                            if j == 0 and (h, g) != (0, 0):
                                nb_old = G0[g - 1][1]
                                pe.wait_ge(sem("es_done"), h * NT + b0 - nb_old + min(k + 1, nb_old))
                            weights, w = PW[:, m % NRING, k * P:(k + 1) * P], HW[:, h % 2, j, :]
                            pe.matmul(PS[:, k, 0:D + 1], weights, w[:, 0:D + 1], start=(j == 0), stop=False)
                            ins = pe.matmul(PS[:, k, 0:D + 1], weights, w[:, D + 2:2 * D + 3], start=False,
                                            stop=(j == NT - 1))
                            if j == NT - 1:
                                ins.then_inc(sem("bank_full1"), 1)
                            elif k == nb - 1:
                                ins.then_inc(sem("p_used"), 1)
                        if j == NT - 1:
                            pe.wait_ge(sem("bank_full1"), h * NT + b0 + nb)
                            pe.sem_inc(sem("p_used"), 1)
                        m += 1
            pe.wait_ge(sem("wn"), 32)
            pe.wait_ge(sem("h_back"), 16)

            def node_transposes(t):
                if t >= 2:
                    pe.wait_ge(sem("sh"), NT + t - 1)
                bank = 0 if t % 2 == 0 else 5
                for c in range(DC):
                    pe.transpose(PS[:, bank, c * P:(c + 1) * P], ES[:, t, c * P:(c + 1) * P], ident[:])
                for c in range(DC):
                    ins = pe.transpose(PS[:, bank, (DC + c) * P:(DC + c + 1) * P], H32B[:, t, c * P:(c + 1) * P], ident[:])
                ins.then_inc(sem("tb"), 1)

            pe.wait_ge(sem("es_done"), NT * (H1 - 1) + G0[-1][0] + 1)
            node_transposes(0)
            pe.wait_ge(sem("es_done"), NT * H1)
            pe.wait_ge(sem("bias_n"), 1)
            for t in range(NT):
                if t + 1 < NT:
                    node_transposes(t + 1)
                gru_mm(NT + t + 1, t, SH2 if t % 2 == 0 else SH2B, WIH2, WHH2, BIAS2)
            pe.wait_ge(sem("at_back"), NT)
            pe.wait_ge(sem("hhl_pad"), 2)
            pe.wait_ge(sem("lo2"), NT)
            pe.wait_ge(sem("w2"), 16)
            for t in range(NT + 1):
                if t >= 1:
                    pe.wait_ge(sem("nei"), t)
                    if t >= 2:
                        pe.wait_ge(sem("sh3"), t - 1)
                    for c in range(DC):
                        pe.transpose(PS[:, 0, c * P:(c + 1) * P], H2[:, t - 1, c * P:(c + 1) * P], ident[:])
                    for c in range(DC):
                        ins = pe.transpose(PS[:, 0, (DC + c) * P:(DC + c + 1) * P], NEI[:, c * P:(c + 1) * P], ident[:])
                    ins.then_inc(sem("tb2"), 1)
                if t < NT:
                    if t >= 2:
                        pe.wait_ge(sem("nei"), t - 1)
                    o = PS[:, 1 + t % 2, :]
                    for j in range(NT):
                        pe.matmul(o[:, 0:D + 1], AT[:, j, t * P:(t + 1) * P], HHL2[:, j, 0, 0:D + 1], start=(j == 0), stop=False)
                        ins = pe.matmul(o[:, 0:D], AT[:, j, t * P:(t + 1) * P], HHL2[:, j, 1, 0:D], start=False,
                                        stop=(j == NT - 1))
                    ins.then_inc(sem("agg"), 1)
                if t >= 1:
                    pe.wait_ge(sem("sh3"), t)
                    if t >= 3:
                        pe.wait_ge(sem("x_l2"), t - 2)
                    for c in range(2 * DC):
                        ins = pe.matmul(PS[:, 3 + (t - 1) % 2, 0:D], SH3[:, c * P:(c + 1) * P], W2[:, c, :],
                                        start=(c == 0), stop=(c == 2 * DC - 1))
                    ins.then_inc(sem("lin"), 1)
            with pe.If(layer3_needed(pe) == 1):
                pe.wait_ge(sem("w3"), 32)

                def h3_transposes(t):
                    pe.wait_ge(sem("h3"), t + 1)
                    if t >= 2:
                        pe.wait_ge(sem("h3T"), t - 1)
                    for c in range(DC):
                        ins = pe.transpose(PS[:, t % 2, c * P:(c + 1) * P], H3[:, t, c * P:(c + 1) * P], ident[:])
                    ins.then_inc(sem("h3_tr"), 1)

                h3_transposes(0)
                for t in range(NT):
                    if t + 1 < NT:
                        h3_transposes(t + 1)
                    pe.wait_ge(sem("h3T"), t + 1)
                    if t >= 2:
                        pe.wait_ge(sem("msg"), t - 1)
                    for c in range(DC):
                        ins = pe.matmul(PS[:, 2 + t % 2, 0:D], SH4[:, t % 2, c * P:(c + 1) * P], W3[:, c, :],
                                        start=(c == 0), stop=(c == DC - 1))
                    ins.then_inc(sem("msg_mm"), 1)
                pe.wait_ge(sem("msg"), NT)
                m = 0
                for g, (b0, nb) in enumerate(G0):
                    for j in range(NT):
                        pe.wait_ge(sem("w_built"), m + 1)
                        for k in range(nb):
                            if j == 0 and g >= 1:
                                nb_old = G0[g - 1][1]
                                pe.wait_ge(sem("x_l3"), b0 - nb_old + min(k + 1, nb_old))
                            ins = pe.matmul(PS[:, k, 0:D], WT[:, m % 3, k * P:(k + 1) * P], MSG[:, j, :],
                                            start=(j == 0), stop=(j == NT - 1))
                            if j == NT - 1:
                                ins.then_inc(sem("bank_full3"), 1)
                            elif k == nb - 1:
                                ins.then_inc(sem("w_used"), 1)
                        if j == NT - 1:
                            pe.wait_ge(sem("bank_full3"), b0 + nb)
                            pe.sem_inc(sem("w_used"), 1)
                        m += 1
            with pe.Else():
                pe.nop()


def kernel(**inputs):
    import numpy as _np
    import concourse.bacc as _bacc
    from concourse import mybir as _mybir
    from concourse.bass_utils import run_bass_kernel_spmd as _run

    n = inputs["x"].shape[0]
    padded = -(-n // 128) * 128

    def padded_to(a, rows, cols):
        out = _np.zeros((rows, cols), a.dtype)
        out[:a.shape[0], :a.shape[1]] = a
        return out

    a = {k: _np.asarray(v) for k, v in inputs.items()}
    arrays = {
        "x": padded_to(a["x"], padded, a["x"].shape[1]),
        "adjT": padded_to(a["adj"].T, padded, padded),
        "Wm": a["L0_gnn_Wm"],
        "WmT": a["L0_gnn_Wm"].T,
        "al": a["L0_gnn_al"],
        "ar": a["L0_gnn_ar"],
        "adj": padded_to(a["adj"], padded, padded),
        "diag": padded_to(_np.diagonal(a["adj"])[None], 1, padded).reshape(padded // 128, 128).T,
        "gatW": a["L1_gnn_gat_W"],
        "gatWT": a["L1_gnn_gat_W"].transpose(0, 2, 1),
        "gat_a": a["L1_gnn_gat_a"][:, :256, 0].reshape(3, 2, 128).transpose(2, 1, 0),
        "edge_WihT": a["L1_gnn_edge_Wih"].T,
        "edge_WhhT": a["L1_gnn_edge_Whh"].T,
        "edge_bih": a["L1_gnn_edge_bih"],
        "edge_bhh": a["L1_gnn_edge_bhh"],
        "node_WihT": a["L1_gnn_node_Wih"].T,
        "node_WhhT": a["L1_gnn_node_Whh"].T,
        "node_bih": a["L1_gnn_node_bih"],
        "node_bhh": a["L1_gnn_node_bhh"],
        "W2T": a["L2_gnn_W"].T,
        "W3": a["L3_gnn_W"],
        "B3": a["L3_gnn_B"],
    }
    arrays = {k: _np.ascontiguousarray(v) for k, v in arrays.items()}
    nc = _bacc.Bacc("TRN2", target_bir_lowering=False, num_devices=1)
    t_in = {k: nc.dram_tensor(f"in_{k}", v.shape, _mybir.dt.from_np(v.dtype), kind="ExternalInput").ap()
            for k, v in arrays.items()}
    out = nc.dram_tensor("out", (n, a["x"].shape[1]), _mybir.dt.float32, kind="ExternalOutput").ap()
    gnn_stack_kernel(nc, t_in, out)
    r = _run(nc, [{f"in_{k}": v for k, v in arrays.items()}], core_ids=[0])
    return r.results[0]["out"]
```

```python
from contextlib import ExitStack

import numpy as np
import concourse.bass as bass
from concourse import mybir

F32 = mybir.dt.float32
F16 = mybir.dt.float16
BF16 = mybir.dt.bfloat16
FP8 = mybir.dt.float8e4
ALU = mybir.AluOpType
ACT = mybir.ActivationFunctionType
AX = mybir.AxisListType
RMAX = bass.bass_isa.ReduceOp.max

P = 128


def gnn_stack_kernel(nc, t_in, out):
    N, D = t_in["x"].shape[0], 256
    NREAL = out.shape[0]
    NT = N // P
    DC = D // P
    H0, F0 = 4, 64
    C0 = F0 + 1
    H1 = 3
    EPS = 1e-5
    TINY = 1e-30
    NEAR_ZERO = 1e-12
    SLOPE = 0.2
    G0 = [(0, 8), (8, 7), (15, 7)]
    LOG2E = 1.0 / float(np.log(2.0))
    LN2 = float(np.log(2.0))
    LN2_HIGH = 0.693359375
    LN2_LOW = LN2 - LN2_HIGH
    ROUND = 1.5 * 2.0 ** 23
    NORM1 = [(0, 15), (15, NT)]
    NORM2 = [(0, 11), (11, 17), (17, NT)]
    WSCALE = 1024.0
    AGG_BANK = [6, 7, 5, 1]
    NORM_LAG = 3
    HW_EARLY = 14
    NRING = 5
    NMASK = 29
    MASKED = -240.0
    QUARTER = NT * P // 2
    assert N == NT * P and DC == 2

    with ExitStack() as ctx:
        def sb(name, shape, dt=F32):
            return ctx.enter_context(nc.sbuf_tensor(name, shape, dt))

        sems = {}

        def sem(name):
            if name not in sems:
                sems[name] = ctx.enter_context(nc.semaphore(name))
            return sems[name]

        AT = sb("AT", [P, NT, N], FP8)
        X = sb("X", [P, NT, D])
        ident = sb("ident", [P, P])
        scratch = sb("scratch", [P, QUARTER // 2])
        stats = scratch[:, 0:NT * 6].rearrange("p (t c) -> p t c", c=6)
        E3 = scratch[:, NT * 6:NT * 15].rearrange("p (t c) -> p t c", c=9)
        junk = scratch[:].bitcast(BF16)
        mv = sb("mv", [P, NT, 2])
        ln = sb("ln", [P, 6, NT])
        small = sb("small", [P, 32])
        sens_count = sb("sens_count", [P, len(G0) * NT])
        sens_any = sb("sens_any", [P, 1], mybir.dt.int32)
        AR = 30298
        arena = sb("arena", [P, AR])
        PS = ctx.enter_context(nc.psum_tensor("PS", [P, 8, 512], F32))

        class Arena:
            def __init__(self):
                self.at = 0

            def take(self, *dims, dt=F32, size=4):
                n = int(np.prod(dims))
                words = -(-n * size // 4)
                words += words % 2
                v = arena[:, self.at:self.at + words]
                self.at += words
                assert self.at <= AR, (self.at, AR)
                if dt != F32:
                    v = v.bitcast(dt)
                v = v[:, 0:n]
                if len(dims) == 2:
                    v = v.rearrange("p (a b) -> p a b", a=dims[0])
                if len(dims) == 3:
                    v = v.rearrange("p (a b c) -> p a b c", a=dims[0], b=dims[1])
                if len(dims) == 4:
                    v = v.rearrange("p (a b c d) -> p a b c d", a=dims[0], b=dims[1], c=dims[2])
                return v

        a0 = Arena()
        MOV = a0.take(NT, H0, 2, 2 * C0, dt=F16, size=2)
        mask_at = a0.at
        MASK = a0.take(NMASK, 1024, dt=FP8, size=1)
        a0m = Arena()
        a0m.at = mask_at
        HTF = a0m.take(NT, H0 * C0)
        assert a0m.at <= a0.at
        ELB = a0.take(2, 1024)
        stg_at = a0.at
        STG = a0.take(4, 1024)
        e_at = a0.at
        E = a0.take(8, 4 * C0)
        DA = a0.take(8, 4 * C0)
        a0w = Arena()
        a0w.at = e_at
        WM = a0w.take(DC, D)
        WMT = a0w.take(DC, D)
        TS = a0w.take(3, 4 * 2 * C0)
        HS = a0w.take(2, D)
        HTS = a0w.take(2, D)
        assert a0w.at <= a0.at
        ALR = a0.take(DC, 2 * H0)
        WAL = a0.take(DC, 2 * H0)
        ELR = a0.take(NT, 2 * H0)
        ELC = a0.take(NT * H0)
        NER = a0.take(NT, H0)
        COEF = a0.take(4, NT * H0)
        MX = a0.take(NT * H0)
        ELT = a0.take(P)
        RD = a0.take(8, H0)

        a1 = Arena()
        H32 = a1.take(NT, D)
        HHL = a1.take(NT, 2, D + 2, dt=F16, size=2)
        EB = a1.take(H1, N)
        AROW = a1.take(2, QUARTER)
        ab = Arena()
        ab.at = a1.at - 2 * QUARTER + 1156
        GWT = ab.take(H1 * DC, D)
        assert ab.at <= a1.at and ab.at - H1 * DC * D >= stg_at
        HT1 = AROW[:, 0, 0:4 * P].rearrange("p (s c) -> p s c", s=2)
        WIH = a1.take(DC, 3 * D)
        WHH = a1.take(DC, 3 * D)
        GW = a1.take(H1 * DC, D)
        gru_at = a1.at
        SH = a1.take(4 * P)
        NSS = a1.take(D)
        au = Arena()
        au.at = a1.at - D
        UP = au.take(NT, 3 * H1 + 1, dt=F16, size=2)
        HWS = a1.take(H1, 2, D + 2, dt=F16, size=2)
        TRZ = a1.take(2 * D)
        GT = a1.take(D)
        GN = a1.take(D)
        GD = TRZ[:, 0:D]
        BIAS = a1.take(4 * D, dt=BF16, size=2)
        tmp = Arena()
        tmp.at = gru_at + 4 * P + D
        BR = tmp.take(4 * D)
        BRB = tmp.take(2 * D)
        assert tmp.at <= a1.at - 2 * D
        BP = scratch[:, 0:2 * D].bitcast(BF16)
        a2 = Arena()
        HW = a2.take(2, NT, 2 * (D + 2), dt=F16, size=2)
        MB = a2.take(2, N)
        a2t_at = a2.at
        T = a2.take(NRING, 1024, dt=BF16, size=2)
        PW = a2.take(NRING, 1024, dt=BF16, size=2)
        a2t = Arena()
        a2t.at = a2t_at
        SH2 = a2t.take(2, 4 * P, dt=F16, size=2)
        TRZ2 = a2t.take(2, 2 * D)
        GT2 = a2t.take(2, D)
        GN2 = a2t.take(2, D)
        GD2 = TRZ2[:, :, 0:D]
        SH2B = a2t.take(2, 4 * P, dt=F16, size=2)
        assert a2t.at <= a2.at
        ES = a2.take(NT, D)
        a2w = Arena()
        a2w.at = a2.at
        WIH2 = a2.take(DC, 3 * D)
        WIH2S = a2w.take(DC, 3, 2, D, dt=F16, size=2)
        last_at = a2.at
        BIAS2 = a2.take(4 * D, dt=BF16, size=2)
        BRB2 = a2.take(2 * D)
        BP2 = BP
        a2h = Arena()
        a2h.at = NT * (D + 2)
        H32B = a2h.take(NT, D)
        a2m = Arena()
        a2m.at = 2 * NT * (D + 2) + N
        a2w = Arena()
        a2w.at = a2m.at
        WHH2 = a2m.take(DC, 3 * D)
        WHH2S = a2w.take(DC, 3, 2, D, dt=F16, size=2)
        BR2 = a2m.take(4 * D)
        assert a2m.at <= a2t_at
        a3 = Arena()
        HHL2 = a3.take(NT, 2, D + 2, dt=F16, size=2)
        H2 = a3.take(NT, D)
        NEI = a3.take(D)
        SH3 = a3.take(4 * P)
        a3.at = last_at
        W2 = a3.take(2 * DC, D)
        a4 = Arena()
        MSG = a4.take(NT, D)
        H3 = a4.take(NT, D)
        W3 = a4.take(DC, D)
        B3 = a4.take(D)
        SH4 = a4.take(2, DC * P)
        DIST = a4.take(4, 1024)
        RCP = a4.take(2, 1024)
        WT = a4.take(3, 1024)
        DN = sb("DN", [P, NT])
        NOTI = sb("NOTI", [P, P])
        WT_HI = NOTI[:].bitcast(F16)
        WT_LO = scratch[:, 2 * D:2 * D + P].bitcast(F16)
        E1 = sb("E1", [P, NT, H1])
        E2 = sb("E2", [P, NT * H1])
        FR = ln[:, 0:H1, :].rearrange("p a b -> p (a b)")
        M2 = sb("M2", [P, NT, 2, H1])
        A1 = sb("A1", [P, DC, H1])
        U1 = sb("U1", [P, DC, H1])
        ET = sb("ET", [P, P])
        ones3 = sb("ones3", [4, P], BF16)
        EP_D = nc.dram_tensor("e_rows", [NT, H1, P], F32, kind="Internal").ap()
        MN_D = nc.dram_tensor("m_rows", [NT, H1, P], F32, kind="Internal").ap()
        H_D = nc.dram_tensor("h_saved", [P, NT, D], F32, kind="Internal").ap()
        HW_D = nc.dram_tensor("hw_saved", [H1, P, NT, 2 * (D + 2)], F16, kind="Internal").ap()

        EL_D = nc.dram_tensor("el_rows", [NT, H0, P], F32, kind="Internal").ap()

        block = ctx.enter_context(nc.Block())
        adjT = t_in["adjT"].rearrange("(j p) i -> j p i", p=P)
        units0 = [(g, h) for g in range(len(G0)) for h in range(H0)]
        chunk0 = [(g, j) for g in range(len(G0)) for j in range(NT)]
        banks_before = {}
        cnt = 0
        for g, (b0, nb) in enumerate(G0):
            for u in range(H0 + 1):
                banks_before[(g, u)] = cnt
                cnt += nb
        stg_before = [16 * len(range(q, len(chunk0), 4)) for q in range(4)]

        norm_parts = {0: [(0, NT)], 1: NORM1, 2: NORM2, 3: [(0, NT)]}

        def parts_before(q):
            return sum(len(norm_parts[i]) for i in range(q))

        def norm2_blocks(t):
            blocks = []
            for t0, t1 in NORM2[:-1]:
                first = t0 + 3 * (t - t1 - NORM_LAG - 1)
                blocks += list(range(first, min(first + 3, t1))) if first >= t0 else []
            return blocks

        casts_before = {}
        n = NT
        for g, counts in enumerate([(8, 5, 5, 4, 0), (10, 4, 4, 4, 0)]):
            for u, c in enumerate(counts):
                casts_before[(g, u)] = list(range(n, n + c))
                n += c
        assert n == len(chunk0)

        def rounds(size):
            return ([list(range(size))] + [[j] for j in range(size, NT - size)] + [list(range(NT - size, NT))])

        def row_items(t):
            done = [min(2 * NT, max(0, 2 * NT * s // (NT - 1))) for s in (t - 1, t)]
            return [divmod(i, 2) for i in range(*done)]

        units1 = [(h, g) for h in range(H1) for g in range(len(G0))]

        def layer3_needed(eng):
            eng.wait_ge(sem("flag"), 1)
            return eng.value_load(sens_any[0:1, 0:1], min_val=0, max_val=1)

        def link_on(eng, name):
            s = sem(name)
            state = [0]

            def link(ins):
                state[0] += 1
                ins.then_inc(s, 1)
                eng.wait_ge(s, state[0])
            return link

        @block.sync
        def _(sp):
            for c in range(2):
                sp.dma_start(X[:, c * 11:(c + 1) * 11, :],
                             t_in["x"][c * 11 * P:(c + 1) * 11 * P, :].rearrange("(t p) d -> p t d", p=P)
                             ).then_inc(sem("x_in"), 16)

            def load_chunk(n):
                g, j = chunk0[n]
                b0, nb = G0[g]
                if 4 <= n < NT + 4:
                    sp.wait_ge(sem("stg_cast" if n % 2 == 0 else "stg_cast_pool"), (n - 4) // 2 + 1)
                    sp.wait_ge(sem("checked"), n - 3)
                if n >= NT + 4:
                    sp.wait_ge(sem("summed"), n - 3 - NT)
                sp.dma_start(STG[:, n % 4, 0:nb * P], adjT[j, :, b0 * P:(b0 + nb) * P]
                             ).then_inc(sem(f"stg{n % 4}"), 16)

            def load_el(n):
                g, h = units0[n]
                b0, nb = G0[g]
                if n >= 2:
                    sp.wait_ge(sem("masks_built"), (n - 1) * NT)
                sp.dma_start(ELB[:, n % 2, 0:nb * P].rearrange("p (k q) -> p k q", q=P),
                             EL_D[b0:b0 + nb, h, :].partition_broadcast(P)).then_inc(sem(f"elb{n % 2}"), 16)

            for n in range(NT):
                load_chunk(n)
            sp.wait_ge(sem("el_t"), 1)
            sp.dma_start(EL_D.rearrange("t h q -> (t h) q"), ELT[0:NT * H0, :]).then_inc(sem("el_rows"), 16)
            sp.wait_ge(sem("el_rows"), 16)
            load_el(0)
            load_el(1)
            for g in range(len(G0) - 1):
                for u in range(H0 + 1):
                    for n in casts_before[(g, u)]:
                        load_chunk(n)
                    for n in [[(2,), (3,), (4,), (5,), ()], [(6,), (), (7,), (8,), ()]][g][u]:
                        load_el(n)
            load_el(len(units0) - 3)
            load_el(len(units0) - 2)
            load_el(len(units0) - 1)
            sp.dma_start(A1[:], t_in["gat_a"]).then_inc(sem("w1"), 16)
            sp.dma_start(DN[:], t_in["diag"]).then_inc(sem("dn"), 16)
            sp.wait_ge(sem("summed"), len(chunk0) - NT)
            sp.dma_start(GWT.rearrange("p (h c) d -> p h c d", h=H1),
                         t_in["gatWT"].rearrange("h (c p) k -> p h c k", p=P)).then_inc(sem("w1"), 16)

            def load_bias(raw, rawb, ih, hh, name):
                sp.dma_start(raw[0:3, 0:3 * D], t_in[ih].partition_broadcast(3)).then_inc(sem(name), 16)
                sp.dma_start(raw[0:3, 3 * D:4 * D], t_in[hh][2 * D:3 * D].partition_broadcast(3)).then_inc(sem(name), 16)
                sp.dma_start(rawb[0:3, :], t_in[hh][0:2 * D].partition_broadcast(3)).then_inc(sem(name), 16)

            sp.wait_ge(sem("x_l0"), 1)
            load_bias(BR, BRB, "edge_bih", "edge_bhh", "be")
            sp.dma_start(WIH, t_in["edge_WihT"].rearrange("(c p) n -> p c n", p=P)).then_inc(sem("we"), 16)
            sp.dma_start(WHH, t_in["edge_WhhT"].rearrange("(c p) n -> p c n", p=P)).then_inc(sem("we"), 16)
            sp.dma_start(GW.rearrange("p (h c) d -> p h c d", h=H1),
                         t_in["gatW"].rearrange("h (c p) k -> p h c k", p=P)).then_inc(sem("we"), 16)
            sp.wait_ge(sem("h1"), NT)
            sp.dma_start(H_D, H32).then_inc(sem("h_saved"), 16)
            sp.wait_ge(sem("et"), 1)
            sp.wait_ge(sem("u_mm"), 1)
            sp.dma_start(EP_D.rearrange("t h q -> (t h) q"), ET[0:NT * H1, :]).then_inc(sem("ep"), 16)
            sp.wait_ge(sem("ep"), 16)
            for h in range(H1):
                sp.dma_start(EB[:, h, :].rearrange("p (t q) -> p t q", q=P),
                             EP_D[:, h, :].partition_broadcast(P)).then_inc(sem(f"eb{h}"), 16)

            def save_products(t):
                sp.wait_ge(sem("hw_lo"), H1 * (t + 1))
                sp.dma_start(HW_D[:, :, t, :].rearrange("h p c -> p h c"),
                             HWS.rearrange("p h a c -> p h (a c)")).then_inc(sem("hw_dma"), 16)

            def load_rows(t, c):
                if t >= 1:
                    sp.wait_ge(sem("rmax"), H1 * (2 * t + c - 1))
                sp.dma_start(AROW[:, c, :], t_in["adj"][t * P:(t + 1) * P, c * QUARTER:(c + 1) * QUARTER]
                             ).then_inc(sem(f"arow{c}"), 16)

            def load_products(h, t0, t1):
                sp.dma_start(HW[:, h % 2, t0:t1, :], HW_D[h, :, t0:t1, :]).then_inc(sem(f"hwb{h % 2}"), 16)

            def load_maxima(h, t0=0, t1=NT):
                sp.dma_start(MB[:, h % 2, t0 * P:t1 * P].rearrange("p (t q) -> p t q", q=P),
                             MN_D[t0:t1, h, :].partition_broadcast(P)).then_inc(sem(f"mb{h % 2}"), 16)

            for t in range(NT + 1):
                if t >= 2:
                    save_products(t - 2)
                for r, c in row_items(t + 1):
                    load_rows(r, c)
                if t == NT - 2:
                    sp.wait_ge(sem("hw_dma"), 16 * (t - 1))
                    sp.wait_ge(sem("gru_x"), HW_EARLY + 2)
                    sp.wait_ge(sem("h_saved"), 16)
                    load_products(0, 0, HW_EARLY)
            sp.wait_ge(sem("mt"), 1)
            sp.dma_start(MN_D.rearrange("t h q -> (t h) q"), ET[0:NT * H1, :]).then_inc(sem("mn"), 16)
            sp.wait_ge(sem("mn"), 16)
            load_maxima(0, 0, G0[0][1])
            sp.wait_ge(sem("mb0"), 16)
            load_maxima(0, G0[0][1], NT)
            save_products(NT - 1)
            sp.wait_ge(sem("hw_dma"), 16 * NT)
            sp.wait_ge(sem("gru_x"), NT)
            load_products(0, HW_EARLY, NT)
            load_products(1, 0, NT)
            load_maxima(1)
            sp.dma_start(WIH2, t_in["node_WihT"].rearrange("(c p) n -> p c n", p=P)).then_inc(sem("wn_ih"), 16)
            sp.wait_ge(sem("bank_full1"), NT)
            load_products(2, 0, NT)
            load_maxima(2)
            sp.wait_ge(sem("bank_full1"), 2 * NT)
            sp.dma_start(H32B, H_D).then_inc(sem("h_back"), 16)
            sp.dma_start(WHH2, t_in["node_WhhT"].rearrange("(c p) n -> p c n", p=P)).then_inc(sem("wn_hh"), 16)
            load_bias(BR2, BRB2, "node_bih", "node_bhh", "bn")
            sp.wait_ge(sem("nb_mm"), 2 * NT)
            sp.dma_start(W2, t_in["W2T"].rearrange("(c p) n -> p c n", p=P)).then_inc(sem("w2"), 16)
            def write_out(done, before):
                for g, (b0, nb) in enumerate(G0):
                    sp.wait_ge(sem(done), before + b0 + nb)
                    last = b0 + nb == NT
                    full = nb - 1 if last else nb
                    sp.dma_start(out[b0 * P:(b0 + full) * P, :].rearrange("(t p) d -> p t d", p=P),
                                 X[:, b0:b0 + full, :]).then_inc(sem("out"), 16)
                    if last:
                        sp.dma_start(out[(NT - 1) * P:NREAL, :], X[0:NREAL - (NT - 1) * P, NT - 1, :]
                                     ).then_inc(sem("out"), 16)
                sp.wait_ge(sem("out"), 16 * (len(G0) + 1))

            with sp.If(layer3_needed(sp) == 1):
                sp.wait_ge(sem("x_l2"), NT)
                sp.dma_start(W3, t_in["W3"].rearrange("(c p) n -> p c n", p=P)).then_inc(sem("w3"), 16)
                sp.dma_start(B3, t_in["B3"].partition_broadcast(P)).then_inc(sem("w3"), 16)
                for m, (g, j) in enumerate(chunk0):
                    b0, nb = G0[g]
                    if m >= 4:
                        sp.wait_ge(sem("w_built"), m - 3)
                    sp.dma_start(DIST[:, m % 4, 0:nb * P], adjT[j, :, b0 * P:(b0 + nb) * P]
                                 ).then_inc(sem(f"stg{m % 4}"), 16)
                write_out("x_l3", 0)
            with sp.Else():
                write_out("x_l2", 0)

        @block.gpsimd
        def _(pool):
            link = link_on(pool, "pool_chain")
            link(pool.memset(ident[:], 0.0))
            pool.affine_select(out=ident[:], in_=ident[:], compare_op=ALU.not_equal, fill=1.0, base=0,
                               pattern=[[-1, P]], channel_multiplier=1).then_inc(sem("consts"), 1)
            pool.wait_ge(sem("consts"), 1)
            pool.tensor_scalar(NOTI[:], ident[:], -1.0, 1.0, ALU.mult, ALU.add).then_inc(sem("consts"), 1)
            pool.memset(ones3[:], 1.0).then_inc(sem("consts"), 1)
            pool.memset(ALR, 0.0).then_inc(sem("consts"), 1)
            pool.memset(HTF.rearrange("p t (h c) -> p t h c", c=C0)[:, :, :, F0:C0], 1.0).then_inc(sem("consts"), 1)
            for t in range(1, NT, 2):
                pool.wait_ge(sem(f"stg{t % 4}"), 16 * (t // 4 + 1))
                pool.tensor_copy(AT[:, t, 0:G0[0][1] * P], STG[:, t % 4, 0:G0[0][1] * P], saturate=False
                                 ).then_inc(sem("stg_cast_pool"), 1)
            pool.wait_ge(sem("er_max"), 1)
            pool.partition_all_reduce(small[:, 4:8], small[:, 0:4], P, RMAX).then_inc(sem("er_gmax"), 1)
            pool.wait_ge(sem("coef"), 1)
            for t in range(NT):
                if t >= 3:
                    pool.wait_ge(sem("mov"), t - 2)
                pool.wait_ge(sem("htf"), t + 1)
                pool.tensor_tensor(TS[:, t % 3, :].rearrange("p (h b c) -> p h b c", h=H0, b=2)[:, :, 1, :],
                                   HTF[:, t, :].rearrange("p (h c) -> p h c", c=C0),
                                   COEF[:, 3, t * H0:(t + 1) * H0].unsqueeze(2).to_broadcast([P, H0, C0]),
                                   ALU.mult).then_inc(sem("t_d"), 1)
            for n, (g, h) in enumerate(units0):
                b0, nb = G0[g]
                if n == 2 * H0 + 2:
                    pool.wait_ge(sem("sens_max"), 1)
                    pool.partition_all_reduce(small[:, 21:22], small[:, 20:21], P, RMAX).then_inc(sem("sens_gmax"), 1)
                Ev = E[:, 0:nb, :]
                Dv = DA[:, 0:nb, h * C0:(h + 1) * C0]
                co = [COEF[:, q, :].rearrange("p (t h) -> p t h", h=H0)[:, b0:b0 + nb, h:h + 1].to_broadcast([P, nb, C0])
                      for q in range(2)]
                if n < len(units0) - 1:
                    pool.wait_ge(sem("bank_free"), banks_before[(g, h + 1)] + nb)
                    link(pool.tensor_tensor(Ev[:, :, 0:C0], Ev[:, :, 0:C0], Ev[:, :, 2 * C0:3 * C0], ALU.add))
                    link(pool.tensor_tensor(Ev[:, :, C0:2 * C0], Ev[:, :, C0:2 * C0], Ev[:, :, 3 * C0:4 * C0], ALU.add))
                    link(pool.tensor_tensor(Ev[:, :, C0:2 * C0], Dv, Ev[:, :, C0:2 * C0], ALU.subtract))
                    link(pool.tensor_tensor(Ev[:, :, 0:C0], Ev[:, :, 0:C0], co[0], ALU.mult))
                    link(pool.tensor_tensor(Ev[:, :, C0:2 * C0], Ev[:, :, C0:2 * C0], co[1], ALU.mult))
                    ins = pool.tensor_tensor(Dv, Ev[:, :, 0:C0], Ev[:, :, C0:2 * C0], ALU.add)
                    ins.then_inc(sem("e_used"), 1)
                heads = H0 if g < len(G0) - 1 else H0 - 1
                if h == heads - 1:
                    pool.wait_ge(sem("rden0"), g + 1)
                    for hh in range(heads):
                        Dh = DA[:, 0:nb, hh * C0:hh * C0 + F0]
                        Xh = X[:, b0:b0 + nb, hh * F0:(hh + 1) * F0]
                        link(pool.tensor_tensor(Dh, Dh, RD[:, 0:nb, hh:hh + 1].to_broadcast([P, nb, F0]), ALU.mult))
                        link(pool.tensor_tensor(Xh, Xh, Dh, ALU.add))
                    pool.sem_inc(sem("da_used"), 1)
            pool.wait_ge(sem("bank_full"), banks_before[(len(G0) - 1, H0)] + G0[-1][1])
            pool.memset(HHL[:, :, 0, D:D + 2], 1.0).then_inc(sem("hhl_pad"), 1)
            for t in range(NT):
                pool.wait_ge(sem("h1"), t + 1)
                pool.tensor_copy(HHL[:, t, 0, 0:D], H32[:, t, :]).then_inc(sem("hi1"), 1)
            pool.wait_ge(sem("e_min"), 1)
            pool.partition_all_reduce(small[:, 12:15], small[:, 8:11], P, RMAX).then_inc(sem("shift"), 1)

            def gru_tail(count, t, h_blk, trz, n, d):
                pool.wait_ge(sem("n"), count)
                link(pool.tensor_tensor(d, h_blk, n, ALU.subtract))
                link(pool.tensor_scalar(trz[:, D:2 * D], trz[:, D:2 * D], 0.5, 0.5, ALU.mult, ALU.add))
                link(pool.tensor_tensor(d, trz[:, D:2 * D], d, ALU.mult))
                link(pool.tensor_tensor(d, d, n, ALU.add))
                link(pool.tensor_scalar(d, d, DN[:, t:t + 1], 1.0, ALU.mult, ALU.mult))
                pool.tensor_tensor(X[:, t, :], X[:, t, :], d, ALU.add).then_inc(sem("gru_x"), 1)

            pool.wait_ge(sem("dn"), 16)
            for t in range(NT + 2):
                for r, half in row_items(t):
                    c, b = divmod(r, NT // 2)
                    if half == c:
                        pool.wait_ge(sem(f"arow{c}"), 16 * (r + 1))
                        blk = AROW[:, c, b * P:(b + 1) * P]
                        pool.tensor_tensor(blk, blk, NOTI[:], ALU.mult).then_inc(sem("row_diag"), 1)
                if t >= 2:
                    gru_tail(t - 1, t - 2, H32[:, t - 2, :], TRZ, GN, GD)

            def split_weights(w, halves, loaded):
                pool.wait_ge(sem(loaded), 16)
                for c in range(DC):
                    for k in range(3):
                        v = w[:, c, k * D:(k + 1) * D]
                        link(pool.tensor_scalar(v, v, WSCALE, 1.0, ALU.mult, ALU.mult))
                        link(pool.tensor_copy(WT_HI, v))
                        link(pool.tensor_tensor(WT_LO, v, WT_HI, ALU.subtract))
                        link(pool.tensor_copy(halves[:, c, k, 0, :], WT_HI))
                        link(pool.tensor_copy(halves[:, c, k, 1, :], WT_LO))
                pool.sem_inc(sem("wn_split"), 1)

            split_weights(WIH2, WIH2S, "wn_ih")
            split_weights(WHH2, WHH2S, "wn_hh")
            pool.wait_ge(sem("bank_full1"), H1 * NT)
            pool.memset(HHL2[:, :, 0, D:D + 2], 1.0).then_inc(sem("hhl_pad"), 1)
            pool.wait_ge(sem("h_back"), 16)
            for t in range(NT):
                gru_tail(NT + t + 1, t, H32B[:, t, :], TRZ2[:, t % 2, :], GN2[:, t % 2, :], GD2[:, t % 2, :])
            with pool.If(layer3_needed(pool) == 1):
                m = 0
                for g, (b0, nb) in enumerate(G0):
                    for j in range(NT):
                        pool.wait_ge(sem("near0"), m + 1)
                        v = RCP[:, m % 2, 0:nb * P]
                        pool.tensor_tensor(v, v, DIST[:, m % 4, 0:nb * P], ALU.add).then_inc(sem("no_zero"), 1)
                        m += 1
            with pool.Else():
                pool.nop()

        @block.scalar
        def _(act):
            act.dma_start(WM, t_in["Wm"].rearrange("(c p) n -> p c n", p=P)).then_inc(sem("w0"), 16)
            act.dma_start(WMT, t_in["WmT"].rearrange("(c p) n -> p c n", p=P)).then_inc(sem("w0"), 16)
            act.wait_ge(sem("consts"), 5)
            for h in range(H0):
                for q, name in enumerate(("al", "ar")):
                    act.dma_start(ALR[F0 * (h % 2):F0 * (h % 2) + F0, h // 2, q * H0 + h:q * H0 + h + 1],
                                  t_in[name].unsqueeze(1)).then_inc(sem("w0"), 16)

            def norm_sqrt(q, part=0):
                t0, t1 = norm_parts[q][part]
                count = parts_before(q) + part + 1
                act.wait_ge(sem("var"), count)
                act.activation(ln[:, 1, t0:t1], ln[:, 0, t0:t1], ACT.Sqrt).then_inc(sem("sqrt"), 1)

            def norm_ready(q, part=0):
                act.wait_ge(sem("rstd"), parts_before(q) + part + 1)

            def norm_block(q, t, full, high=None):
                act.activation(full[:, t, :], X[:, t, :], ACT.Relu, bias=ln[:, 5, t:t + 1],
                               scale=ln[:, 2, t:t + 1]).then_inc(sem(f"h{q}"), 1)
                if high is not None:
                    act.activation(high[:, t, 0, 0:D], X[:, t, :], ACT.Relu, bias=ln[:, 5, t:t + 1],
                                   scale=ln[:, 2, t:t + 1]).then_inc(sem(f"hi{q}"), 1)

            norm_sqrt(0)
            norm_ready(0)

            def norm(t):
                if t >= 2:
                    act.wait_ge(sem("h_tr"), t - 1)
                act.activation(HS[:, t % 2, :], X[:, t, :], ACT.Relu, bias=ln[:, 5, t:t + 1],
                               scale=ln[:, 2, t:t + 1]).then_inc(sem("h"), 1)

            def ht_out(t):
                act.wait_ge(sem("ht_mm"), t + 1)
                act.activation(HTF[:, t, :].rearrange("p (h c) -> p h c", c=C0)[:, :, 0:F0],
                               PS[:, 2 + t % 2, 0:D].rearrange("p (h c) -> p h c", c=F0), ACT.Copy
                               ).then_inc(sem("htf"), 1)

            norm(0)
            for t in range(NT):
                if t + 1 < NT:
                    norm(t + 1)
                act.wait_ge(sem("h_tr"), t + 1)
                if t >= 2:
                    act.wait_ge(sem("ht_mm"), t - 1)
                act.activation(HTS[:, t % 2, :], PS[:, t % 2, 0:D], ACT.Copy).then_inc(sem("hT"), 1)
                if t >= 1:
                    ht_out(t - 1)
            ht_out(NT - 1)
            act.wait_ge(sem("arg"), 1)
            act.activation(COEF, COEF, ACT.Exp).then_inc(sem("coef"), 1)
            act.wait_ge(sem("coef"), 1)
            for t in range(NT):
                act.wait_ge(sem("t_b"), t + 1)
                act.wait_ge(sem("t_d"), t + 1)
                act.activation(MOV[:, t, :, 0, :], TS[:, t % 3, :].rearrange("p (h c) -> p h c", h=H0), ACT.Copy
                               ).then_inc(sem("mov_hi"), 1)
            pos = 0

            def deviations(n):
                v = STG[:, n % 4, 0:G0[chunk0[n][0]][1] * P]
                act.wait_ge(sem("squared"), n - NT + 1)
                act.activation(v, v, ACT.Abs, bias=small[:, 19:20], accum_out=sens_count[:, n:n + 1]
                               ).then_inc(sem("summed"), 1)

            act.wait_ge(sem("halves"), 2)
            for g, (b0, nb) in enumerate(G0):
                for u in range(H0 + 1):
                    for n in casts_before.get((g, u), []):
                        gg, j = chunk0[n]
                        bb, nn = G0[gg]
                        act.wait_ge(sem(f"stg{n % 4}"), 16 * (n // 4 + 1))
                        act.activation(AT[:, j, bb * P:(bb + nn) * P], STG[:, n % 4, 0:nn * P], ACT.Copy, saturate=False
                                       ).then_inc(sem("stg_used"), 1)
                        v = STG[:, n % 4, 0:nn * P]
                        act.wait_ge(sem("stg_used"), n - NT + 1)
                        act.activation(v, v, ACT.Square, bias=small[:, 18:19]).then_inc(sem("squared"), 1)
                        if n > NT:
                            deviations(n - 1)
                        if n == len(chunk0) - 1:
                            deviations(n)
                    if u == 0:
                        if g >= 1:
                            act.wait_ge(sem("da_used"), g)
                    elif g * H0 + u - 1 >= 1:
                        act.wait_ge(sem("e_used"), g * H0 + u - 1)
                    if g == len(G0) - 1 and u == H0:
                        norm_sqrt(1, 0)
                    if g == 0 and u == 0:
                        act.wait_ge(sem("mov"), NT)
                    for k in range(nb):
                        act.wait_ge(sem("bank_full"), banks_before[(g, u)] + k + 1)
                        act.activation((DA if u == 0 else E)[:, k, :], PS[:, k, 0:4 * C0], ACT.Copy
                                       ).then_inc(sem("bank_free"), 1)
            def turn_mask(g, j):
                blk = AT[:, j, G0[g][0] * P:(G0[g][0] + G0[g][1]) * P]
                act.activation(blk, blk, ACT.Copy, scale=-MASKED, bias=MASKED, saturate=False).then_inc(sem("ab"), 1)

            norm_ready(1, 0)
            for t in range(NT + 1):
                if t == 3:
                    norm_sqrt(1, 1)
                if t == NORM1[1][0]:
                    norm_ready(1, 1)
                if t < NT:
                    norm_block(1, t, H32)
                t -= 1
                if t < 0:
                    continue
                act.wait_ge(sem("h1_tr"), t + 1)
                if t >= 2:
                    act.wait_ge(sem("hu_mm"), t - 1)
                act.activation(HT1[:, t % 2, :], PS[:, t % 2, 0:D], ACT.Copy
                               ).then_inc(sem("h1T"), 1)
            act.wait_ge(sem("hu_mm"), NT)
            act.wait_ge(sem("fr_arg"), 1)
            act.activation(FR, FR, ACT.Exp).then_inc(sem("fr"), 1)
            act.wait_ge(sem("bias_e"), 1)

            for t in range(NT + 2):
                if t == 2:
                    act.wait_ge(sem("fr"), 1)
                if t >= 2:
                    act.wait_ge(sem("rz_mm"), t - 1)
                    if t >= 3:
                        act.wait_ge(sem("gru_x"), t - 2)
                    act.activation(TRZ, PS[:, 1 + t % 2, :], ACT.Tanh, scale=0.5).then_inc(sem("trz"), 1)
                    act.wait_ge(sem("hw_mm"), t - 1)
                    if t >= 3:
                        act.wait_ge(sem("hw_dma"), 16 * (t - 2))
                    for h in range(H1):
                        act.activation(HWS[:, h, 0, 0:D], PS[:, 6 + h // 2, (h % 2) * D:(h % 2 + 1) * D], ACT.Copy,
                                       scale=FR[:, (t - 2) * H1 + h:(t - 2) * H1 + h + 1]).then_inc(sem("hw_hi"), 1)
                if 1 <= t <= NT:
                    act.wait_ge(sem("tb"), t)
                    act.activation(SH, PS[:, 0, :], ACT.Copy).then_inc(sem("sh"), 1)
                if t >= 2:
                    act.wait_ge(sem("u"), t - 1)
                    act.activation(GN, GT, ACT.Tanh).then_inc(sem("n"), 1)
                if t < NT:
                    act.wait_ge(sem("ns"), t + 1)
                    act.activation(NSS, PS[:, 5, 0:D], ACT.Copy).then_inc(sem("ns_sb"), 1)
                for g in range(len(G0) - 1):
                    last = G0[g][0] + G0[g][1]
                    for j in range(4 * (t - last), min(4 * (t - last + 1), NT)):
                        if j >= 0:
                            turn_mask(g, j)
            act.wait_ge(sem("gru_x"), NT)

            m = 0
            for h in range(H1):
                for g, (b0, nb) in enumerate(G0):
                    for j in range(NT):
                        act.wait_ge(sem("t_built"), m + 1)
                        if m >= NRING:
                            act.wait_ge(sem("p_used"), m - NRING + 1)
                        act.activation(PW[:, m % NRING, 0:nb * P], T[:, m % NRING, 0:nb * P], ACT.Exp, scale=LN2
                                       ).then_inc(sem("p_exp"), 1)
                        if h == 0 and g < 2 and j % 2 == 1:
                            turn_mask(2, g * NT // 2 + j // 2)
                        m += 1
            for t in range(NT + 1):
                if t < NT:
                    act.wait_ge(sem("tb"), NT + t + 1)
                    if t >= 2:
                        act.wait_ge(sem("rz_mm"), NT + t - 1)
                    act.activation((SH2 if t % 2 == 0 else SH2B)[:, 0, :], PS[:, 0 if t % 2 == 0 else 5, :], ACT.Copy
                                   ).then_inc(sem("sh_hi"), 1)
                if t >= 1:
                    act.wait_ge(sem("rz_mm"), NT + t)
                    if t >= 3:
                        act.wait_ge(sem("gru_x"), NT + t - 2)
                    act.activation(TRZ2[:, (t - 1) % 2, :], PS[:, 1 + (t - 1) % 2, :], ACT.Tanh, scale=0.5 / WSCALE).then_inc(sem("trz"), 1)
                    act.wait_ge(sem("u"), NT + t)
                    act.activation(GN2[:, (t - 1) % 2, :], GT2[:, (t - 1) % 2, :], ACT.Tanh, scale=1.0 / WSCALE).then_inc(sem("n"), 1)
                for part, (t0, t1) in enumerate(NORM2[:-1]):
                    if t == t1 + NORM_LAG:
                        norm_sqrt(2, part)
                    if t == t1 + NORM_LAG + 1:
                        norm_ready(2, part)
                for b in norm2_blocks(t):
                    norm_block(2, b, H2, HHL2)
            norm_sqrt(2, len(NORM2) - 1)
            norm_ready(2, len(NORM2) - 1)
            for b in range(NORM2[-1][0], NT):
                norm_block(2, b, H2, HHL2)
            for t in range(NT + 1):
                if t >= 1:
                    act.wait_ge(sem("tb2"), t)
                    act.activation(SH3, PS[:, 0, :], ACT.Copy).then_inc(sem("sh3"), 1)
                if t < NT:
                    act.wait_ge(sem("rdeg"), t + 1)
                    act.activation(NEI, PS[:, AGG_BANK[t % 4], 0:D], ACT.Copy, scale=ln[:, 3, t:t + 1]).then_inc(sem("nei"), 1)
            with act.If(layer3_needed(act) == 1):
                act.wait_ge(sem("x_l2"), NT)
                norm_sqrt(3)
                norm_ready(3)
                for t in range(NT):
                    norm_block(3, t, H3)
                for t in range(NT):
                    act.wait_ge(sem("h3_tr"), t + 1)
                    if t >= 2:
                        act.wait_ge(sem("msg_mm"), t - 1)
                    act.activation(SH4[:, t % 2, :], PS[:, t % 2, 0:D], ACT.Copy).then_inc(sem("h3T"), 1)
                m = 0
                for g, (b0, nb) in enumerate(G0):
                    for j in range(NT):
                        act.wait_ge(sem("rcp"), m + 1)
                        v = RCP[:, m % 2, 0:nb * P]
                        act.activation(v, v, ACT.Square, bias=small[:, 17:18]).then_inc(sem("sq"), 1)
                        act.wait_ge(sem("sq"), m + 1)
                        act.activation(v, v, ACT.Exp, scale=-2.0).then_inc(sem("sens"), 1)
                        m += 1
            with act.Else():
                act.nop()

        @block.vector
        def _(dve):
            link = link_on(dve, "dve_chain")
            dve.memset(small[:, 18:19], -0.5).then_inc(sem("halves"), 1)
            dve.memset(small[:, 19:20], -0.25).then_inc(sem("halves"), 1)

            def norm_stats(q, t):
                dve.bn_stats(stats[:, t, :], X[:, t, :]).then_inc(sem("st"), 1)
                dve.wait_ge(sem("st"), q * NT + t + 1)
                dve.bn_aggr(mv[:, t, :], stats[:, t, :]).then_inc(sem("ag"), 1)

            def norm_var(q, part=0):
                t0, t1 = norm_parts[q][part]
                dve.wait_ge(sem("ag"), q * NT + t1)
                dve.tensor_scalar(ln[:, 0, t0:t1], mv[:, t0:t1, 1], EPS, None, ALU.add).then_inc(sem("var"), 1)

            def norm_scales(q, part=0):
                t0, t1 = norm_parts[q][part]
                count = parts_before(q) + part + 1
                row = [ln[:, i, t0:t1] for i in range(6)]
                dve.wait_ge(sem("sqrt"), count)
                dve.wait_ge(sem("var"), count)
                link(dve.reciprocal(row[3], row[1]))
                link(dve.tensor_tensor(row[4], row[3], row[3], ALU.mult))
                link(dve.tensor_tensor(row[4], row[4], row[0], ALU.mult))
                link(dve.tensor_scalar(row[4], row[4], -0.5, 1.5, ALU.mult, ALU.add))
                link(dve.tensor_tensor(row[2], row[3], row[4], ALU.mult))
                dve.scalar_tensor_tensor(out=row[5], in0=mv[:, t0:t1, 0], scalar=-1.0, in1=row[2],
                                         op0=ALU.mult, op1=ALU.mult).then_inc(sem("rstd"), 1)

            for t in range(NT):
                if t == 0:
                    dve.wait_ge(sem("x_in"), 32)
                norm_stats(0, t)
            norm_var(0)
            norm_scales(0)

            def count_sensitive(n):
                nb = G0[chunk0[n][0]][1]
                if n >= 1:
                    dve.wait_ge(sem("checked"), n)
                dve.scalar_tensor_tensor(out=junk[:, 0:nb * P], in0=STG[:, n % 4, 0:nb * P], scalar=1.0,
                                         in1=STG[:, n % 4, 0:nb * P], op0=ALU.is_lt, op1=ALU.logical_and,
                                         accum_out=sens_count[:, n:n + 1]).then_inc(sem("checked"), 1)

            dve.wait_ge(sem("wal_mm"), 1)
            dve.tensor_copy(WAL, PS[:, 4, 0:2 * DC * H0].rearrange("p (c n) -> p c n", c=DC)).then_inc(sem("wal"), 1)
            for t in range(NT):
                nb = G0[0][1]
                dve.wait_ge(sem(f"stg{t % 4}"), 16 * (t // 4 + 1))
                if t % 2 == 0:
                    dve.tensor_copy(AT[:, t, 0:nb * P], STG[:, t % 4, 0:nb * P], saturate=False).then_inc(sem("stg_cast"), 1)
                count_sensitive(t)
            dve.wait_ge(sem("ht_mm"), NT)
            link(dve.tensor_copy(ELR, PS[:, 5, 0:NT * 2 * H0].rearrange("p (t n) -> p t n", n=2 * H0)))
            dve.tensor_copy(ELC.rearrange("p (t h) -> p t h", h=H0), ELR[:, :, 0:H0]).then_inc(sem("elc"), 1)
            dve.tensor_reduce(small[:, 0:4], ELR[:, :, H0:2 * H0].rearrange("p t h -> p h t"), AX.X, ALU.max
                              ).then_inc(sem("er_max"), 1)
            link(dve.tensor_scalar(NER, ELR[:, :, H0:2 * H0], -1.0, None, ALU.mult))
            dve.wait_ge(sem("er_gmax"), 1)
            Gb = small[:, 4:8].unsqueeze(1).to_broadcast([P, NT, H0])
            CO = [COEF[:, q, :].rearrange("p (t h) -> p t h", h=H0) for q in range(4)]
            MXv = MX.rearrange("p (t h) -> p t h", h=H0)
            link(dve.tensor_tensor(CO[0], ELR[:, :, 0:H0], Gb, ALU.add))
            link(dve.scalar_tensor_tensor(out=MXv, in0=CO[0], scalar=SLOPE, in1=CO[0], op0=ALU.mult, op1=ALU.max))
            link(dve.scalar_tensor_tensor(out=CO[1], in0=CO[0], scalar=SLOPE, in1=MXv, op0=ALU.mult, op1=ALU.subtract))
            link(dve.tensor_tensor(CO[0], CO[0], MXv, ALU.subtract))
            link(dve.tensor_tensor(CO[2], ELR[:, :, H0:2 * H0], Gb, ALU.subtract))
            dve.tensor_scalar(CO[3], CO[2], SLOPE, None, ALU.mult).then_inc(sem("arg"), 1)
            dve.wait_ge(sem("elT_mm"), 1)
            dve.tensor_copy(ELT[0:NT * H0, :], PS[0:NT * H0, 6, 0:P]).then_inc(sem("el_t"), 1)
            dve.wait_ge(sem("coef"), 1)

            def low_part(t):
                dve.wait_ge(sem("mov_hi"), t + 1)
                dve.tensor_tensor(MOV[:, t, :, 1, :], TS[:, t % 3, :].rearrange("p (h c) -> p h c", h=H0),
                                  MOV[:, t, :, 0, :], ALU.subtract).then_inc(sem("mov"), 1)

            for t in range(NT):
                if t >= 3:
                    dve.wait_ge(sem("mov"), t - 2)
                dve.wait_ge(sem("htf"), t + 1)
                dve.tensor_tensor(TS[:, t % 3, :].rearrange("p (h b c) -> p h b c", h=H0, b=2)[:, :, 0, :],
                                  HTF[:, t, :].rearrange("p (h c) -> p h c", c=C0),
                                  COEF[:, 2, t * H0:(t + 1) * H0].unsqueeze(2).to_broadcast([P, H0, C0]),
                                  ALU.mult).then_inc(sem("t_b"), 1)
                if t >= 1:
                    low_part(t - 1)
            low_part(NT - 1)
            dve.wait_ge(sem("mov"), NT)
            dve.wait_ge(sem("t_d"), NT)

            def reciprocals(g, heads):
                dve.wait_ge(sem("e_used"), g * H0 + heads)
                RDg = RD[:, 0:G0[g][1], 0:heads]
                link(dve.tensor_scalar(RDg, DA[:, 0:G0[g][1], :].rearrange("p k (h c) -> p k h c", c=C0)
                                       [:, :, 0:heads, F0], TINY, None, ALU.max))
                dve.reciprocal(RDg, RDg).then_inc(sem("rden0"), 1)

            for n, (g, h) in enumerate(units0):
                b0, nb = G0[g]
                dve.wait_ge(sem(f"elb{n % 2}"), 16 * (n // 2 + 1))
                for j in range(NT):
                    m = n * NT + j
                    if g >= 1 and h == 0:
                        dve.wait_ge(sem("stg_used"), (g - 1) * NT + j + 1)
                    if g == 0 and h == 0 and j == 0:
                        dve.wait_ge(sem("stg_cast"), NT // 2)
                        dve.wait_ge(sem("stg_cast_pool"), NT // 2)
                    if m >= NMASK:
                        n_old, j_old = divmod(m - NMASK, NT)
                        g_old, h_old = units0[n_old]
                        if j_old < NT - 1:
                            dve.wait_ge(sem("mask_used"), n_old * (NT - 1) + j_old + 1)
                        else:
                            dve.wait_ge(sem("bank_full"), banks_before[(g_old, h_old + 1)] + G0[g_old][1])
                    dve.scalar_tensor_tensor(out=MASK[:, m % NMASK, 0:nb * P], in0=ELB[:, n % 2, 0:nb * P],
                                             scalar=NER[:, j, h:h + 1], in1=AT[:, j, b0 * P:(b0 + nb) * P],
                                             op0=ALU.is_gt, op1=ALU.mult, saturate=False).then_inc(sem("masks_built"), 1)
                    if n == len(units0) - 1 and 3 <= j < 3 + NORM1[0][1]:
                        if j == 3:
                            dve.wait_ge(sem("da_used"), len(G0) - 1)
                        norm_stats(1, j - 3)
                if n == 2 * H0 + 1:
                    dve.wait_ge(sem("checked"), NT)
                    dve.wait_ge(sem("summed"), len(chunk0) - NT)
                    dve.tensor_reduce(small[:, 20:21], sens_count[:], AX.X, ALU.max).then_inc(sem("sens_max"), 1)
                if n == len(units0) - 1:
                    dve.wait_ge(sem("sens_gmax"), 1)
                    dve.tensor_scalar(sens_any[:], small[:, 21:22], 0.0, None, ALU.is_gt).then_inc(sem("flag"), 1)
                if h == 0 and g >= 1:
                    reciprocals(g - 1, H0)
            norm_var(1, 0)
            norm_scales(1, 0)
            dve.wait_ge(sem("u_mm"), 1)
            dve.tensor_copy(U1[:], PS[:, 7, 0:DC * H1].rearrange("p (c h) -> p c h", c=DC)).then_inc(sem("u1"), 1)
            reciprocals(len(G0) - 1, H0 - 1)
            dve.wait_ge(sem("bank_full"), banks_before[(len(G0) - 1, 1)])
            for t in range(NT):
                blk = AT[:, t, t * P:(t + 1) * P]
                dve.tensor_tensor(blk, blk, NOTI[:], ALU.mult, saturate=False).then_inc(sem("diag0"), 1)
            g, h = units0[-1]
            b0, nb = G0[g]
            Ev, Dv = E[:, 0:nb, :], DA[:, 0:nb, h * C0:(h + 1) * C0]
            co = [COEF[:, q, :].rearrange("p (t h) -> p t h", h=H0)[:, b0:b0 + nb, h:h + 1].to_broadcast([P, nb, C0])
                  for q in range(2)]
            dve.wait_ge(sem("bank_free"), banks_before[(g, h + 1)] + nb)
            link(dve.tensor_tensor(Ev[:, :, 0:2 * C0], Ev[:, :, 0:2 * C0], Ev[:, :, 2 * C0:4 * C0], ALU.add))
            link(dve.tensor_tensor(Ev[:, :, C0:2 * C0], Dv, Ev[:, :, C0:2 * C0], ALU.subtract))
            link(dve.tensor_tensor(Ev[:, :, 0:C0], Ev[:, :, 0:C0], co[0], ALU.mult))
            link(dve.tensor_tensor(Ev[:, :, C0:2 * C0], Ev[:, :, C0:2 * C0], co[1], ALU.mult))
            link(dve.tensor_tensor(Dv, Ev[:, :, 0:C0], Ev[:, :, C0:2 * C0], ALU.add))
            link(dve.tensor_scalar(RD[:, 0:nb, h:h + 1], Dv[:, :, F0:C0], TINY, None, ALU.max))
            link(dve.reciprocal(RD[:, 0:nb, h:h + 1], RD[:, 0:nb, h:h + 1]))
            link(dve.tensor_tensor(Dv[:, :, 0:F0], Dv[:, :, 0:F0], RD[:, 0:nb, h:h + 1].to_broadcast([P, nb, F0]), ALU.mult))
            Xh = X[:, b0:b0 + nb, h * F0:(h + 1) * F0]
            link(dve.tensor_tensor(Xh, Xh, Dv[:, :, 0:F0], ALU.add))
            dve.wait_ge(sem("da_used"), len(G0))
            dve.sem_inc(sem("x_l0"), 1)
            for t in range(*NORM1[1]):
                norm_stats(1, t)
            norm_var(1, 1)
            norm_scales(1, 1)
            dve.memset(small[:, 17:18], -1.0).then_inc(sem("minus1"), 1)
            for t in range(NT):
                dve.wait_ge(sem("hi1"), t + 1)
                dve.tensor_tensor(HHL[:, t, 1, 0:D], H32[:, t, :], HHL[:, t, 0, 0:D], ALU.subtract
                                  ).then_inc(sem("lo1"), 1)

            def bias_sum(br, brb, loaded, count):
                dve.wait_ge(sem(loaded), count)
                link(dve.tensor_tensor(br[0:3, 0:2 * D], br[0:3, 0:2 * D], brb[0:3, :], ALU.add))

            def bias_part(k, br, bp, bias):
                link(dve.tensor_copy(bp[0:3, :], br[0:3, :]))
                if k < 2:
                    link(dve.tensor_tensor(br[0:3, :], br[0:3, :], bp[0:3, :], ALU.subtract))
                if k == 0:
                    ins = dve.tensor_scalar(bias[0:3, :], bp[0:3, :], ident[0:3, 0:1], None, ALU.mult)
                else:
                    ins = dve.scalar_tensor_tensor(out=bias[0:3, :], in0=bp[0:3, :], scalar=ident[0:3, k:k + 1],
                                                   in1=bias[0:3, :], op0=ALU.mult, op1=ALU.add)
                link(ins)

            dve.wait_ge(sem("hu_mm"), NT)
            link(dve.tensor_copy(E1[:], PS[:, 2, 0:NT * H1].rearrange("p (t h) -> p t h", h=H1)))
            for k in range(3):
                part = UP[:, :, k * H1:(k + 1) * H1]
                link(dve.tensor_copy(part, E1[:]))
                if k < 2:
                    link(dve.tensor_tensor(E1[:], E1[:], part, ALU.subtract))
            dve.sem_inc(sem("up"), 1)
            bias_sum(BR, BRB, "be", 48)
            for k in range(3):
                bias_part(k, BR, BP, BIAS)
            dve.sem_inc(sem("bias_e"), 1)
            for h in range(H1):
                dve.memset(HWS[:, h, :, D:D + 2], 1.0).then_inc(sem("hws_pad"), 1)
            dve.wait_ge(sem("e_mm"), 1)
            link(dve.tensor_copy(E3, PS[:, 4, 0:NT * 3 * H1].rearrange("p (t c) -> p t c", t=NT)))
            link(dve.tensor_tensor(E1[:], E3[:, :, H1:2 * H1], E3[:, :, 2 * H1:3 * H1], ALU.add))
            link(dve.tensor_tensor(E1[:], E3[:, :, 0:H1], E1[:], ALU.add))
            link(dve.scalar_tensor_tensor(out=E1[:], in0=E1[:], scalar=SLOPE, in1=E1[:], op0=ALU.mult, op1=ALU.max))
            E2v = E2[:].rearrange("p (t h) -> p t h", h=H1)
            FRv = FR.rearrange("p (t h) -> p t h", h=H1)
            link(dve.tensor_scalar(E2v, E1[:], LOG2E, ROUND, ALU.mult, ALU.add))
            link(dve.tensor_scalar(E2v, E2v, -ROUND, None, ALU.add))
            link(dve.tensor_reduce(small[:, 8:11], E2v.rearrange("p t h -> p h t"), AX.X, ALU.min))
            dve.tensor_scalar(small[:, 8:11], small[:, 8:11], -1.0, None, ALU.mult).then_inc(sem("e_min"), 1)
            link(dve.scalar_tensor_tensor(out=FRv, in0=E2v, scalar=-LN2_HIGH, in1=E1[:], op0=ALU.mult, op1=ALU.add))
            dve.scalar_tensor_tensor(out=FRv, in0=E2v, scalar=-LN2_LOW, in1=FRv, op0=ALU.mult, op1=ALU.add
                                     ).then_inc(sem("fr_arg"), 1)
            dve.wait_ge(sem("shift"), 1)
            shift = small[:, 12:15].unsqueeze(1).to_broadcast([P, NT, H1])
            dve.tensor_tensor(E1[:], E2v, shift, ALU.add).then_inc(sem("e2"), 1)
            dve.wait_ge(sem("eT_mm"), 1)
            dve.tensor_copy(ET[0:NT * H1, :], PS[0:NT * H1, 7, 0:P]).then_inc(sem("et"), 1)

            def row_max(t, c):
                dve.wait_ge(sem(f"arow{c}"), 16 * (t + 1))
                if t // (NT // 2) == c:
                    dve.wait_ge(sem("row_diag"), t + 1)
                for h in range(H1):
                    dve.wait_ge(sem(f"eb{h}"), 16)
                    if t + c + h > 0:
                        dve.wait_ge(sem("rmax"), H1 * (2 * t + c) + h)
                    dve.tensor_tensor_reduce(junk, AROW[:, c, :],
                                             EB[:, h, c * QUARTER:(c + 1) * QUARTER], 1.0, 0.0, ALU.mult, ALU.max,
                                             M2[:, t, c, h:h + 1]).then_inc(sem("rmax"), 1)

            def gru_new(count, t, trz, gt):
                dve.wait_ge(sem("trz"), count)
                dve.wait_ge(sem("nb_mm"), count)
                if count >= 2:
                    dve.wait_ge(sem("n"), count - 1)
                nb_bank = PS[:, 3 + t % 2, :]
                link(dve.scalar_tensor_tensor(out=gt, in0=trz[:, 0:D], scalar=1.0, in1=nb_bank[:, D:2 * D],
                                              op0=ALU.add, op1=ALU.mult))
                dve.scalar_tensor_tensor(out=gt, in0=gt, scalar=0.5, in1=nb_bank[:, 0:D],
                                         op0=ALU.mult, op1=ALU.add).then_inc(sem("u"), 1)

            for t in range(NT + 2):
                if t >= 2:
                    gru_new(t - 1, t - 2, TRZ, GT)
                if t >= 2:
                    for h in range(H1):
                        dve.wait_ge(sem("hw_hi"), H1 * (t - 1))
                        dve.scalar_tensor_tensor(out=HWS[:, h, 1, 0:D], in0=PS[:, 6 + h // 2, (h % 2) * D:(h % 2 + 1) * D],
                                                 scalar=FR[:, (t - 2) * H1 + h:(t - 2) * H1 + h + 1],
                                                 in1=HWS[:, h, 0, 0:D], op0=ALU.mult, op1=ALU.subtract).then_inc(sem("hw_lo"), 1)
                for r, c in row_items(t):
                    row_max(r, c)
                if t == NT - 1:
                    dve.wait_ge(sem("rmax"), 2 * NT * H1)
                    link(dve.tensor_tensor(E2v, M2[:, :, 0, :], M2[:, :, 1, :], ALU.max))
                    dve.tensor_scalar(E2v, E2v, -1.0, None, ALU.mult).then_inc(sem("e2"), 1)
                if t == NT:
                    dve.wait_ge(sem("eT_mm"), 2)
                    dve.wait_ge(sem("ep"), 16)
                    dve.tensor_copy(ET[0:NT * H1, :], PS[0:NT * H1, 5, 0:P]).then_inc(sem("mt"), 1)

            def denominators(h, t0, t1, loads):
                dve.wait_ge(sem(f"hwb{h % 2}"), 16 * loads)
                w = HW[:, h % 2, t0:t1, :]
                f = FRv[:, t0:t1, h:h + 1]
                link(dve.tensor_copy(w[:, :, D:D + 1], f))
                dve.tensor_tensor(w[:, :, 2 * D + 2:2 * D + 3], f, w[:, :, D:D + 1], ALU.subtract
                                  ).then_inc(sem("hw_f"), 1)

            def attention_out(n):
                h, g = units1[n]
                b0, nb = G0[g]
                for k0 in range(0, nb, 2):
                    k1 = min(k0 + 2, nb)
                    dve.wait_ge(sem("bank_full1"), h * NT + b0 + k1)
                    link(dve.tensor_scalar(ln[:, 3, k0:k1], PS[:, k0:k1, D], TINY, float(H1), ALU.max, ALU.mult))
                    link(dve.reciprocal(ln[:, 4, k0:k1], ln[:, 3, k0:k1]))
                    for k in range(k0, k1):
                        if h == 0:
                            ins = dve.tensor_scalar(ES[:, b0 + k, :], PS[:, k, 0:D], ln[:, 4, k:k + 1], None, ALU.mult)
                        else:
                            ins = dve.scalar_tensor_tensor(out=ES[:, b0 + k, :], in0=PS[:, k, 0:D],
                                                           scalar=ln[:, 4, k:k + 1], in1=ES[:, b0 + k, :],
                                                           op0=ALU.mult, op1=ALU.add)
                        ins.then_inc(sem("es_done"), 1)

            m = 0
            for n, (h, g) in enumerate(units1):
                b0, nb = G0[g]
                if (h, g) == (0, 1):
                    dve.wait_ge(sem("mb0"), 32)
                if g == 0:
                    dve.wait_ge(sem(f"mb{h % 2}"), [16, 16, 48][h])
                    denominators(h, 0, HW_EARLY if h == 0 else NT, [1, 1, 3][h])
                if h == 0:
                    dve.wait_ge(sem("ab"), (g + 1) * NT)
                for j in range(NT):
                    if m >= NRING:
                        dve.wait_ge(sem("p_exp"), m - NRING + 1)
                    dve.scalar_tensor_tensor(out=T[:, m % NRING, 0:nb * P], in0=MB[:, h % 2, b0 * P:(b0 + nb) * P],
                                             scalar=E1[:, j, h:h + 1], in1=AT[:, j, b0 * P:(b0 + nb) * P],
                                             op0=ALU.add, op1=ALU.min).then_inc(sem("t_built"), 1)
                    if n == 0 and j == 8:
                        denominators(0, HW_EARLY, NT, 2)
                    if n == 1 and j == 2:
                        dve.wait_ge(sem("gru_x"), NT)
                    if n == 7 and j == 5:
                        bias_sum(BR2, BRB2, "bn", 48)
                        link(dve.tensor_scalar(BR2[0:3, :], BR2[0:3, :], WSCALE, None, ALU.mult))
                    if n == 7 and j in (7, 11, 15):
                        bias_part((j - 7) // 4, BR2, BP2, BIAS2)
                    if j == 4 and n >= 1:
                        attention_out(n - 1)
                    m += 1
            attention_out(len(units1) - 1)
            dve.sem_inc(sem("bias_n"), 1)
            dve.wait_ge(sem("p_used"), H1 * len(G0) * NT)

            def low_half(t):
                dve.wait_ge(sem("h2"), t + 1)
                dve.wait_ge(sem("hi2"), t + 1)
                dve.tensor_tensor(HHL2[:, t, 1, 0:D], H2[:, t, :], HHL2[:, t, 0, 0:D], ALU.subtract
                                  ).then_inc(sem("lo2"), 1)

            for t in range(NT + 1):
                if t < NT:
                    dve.wait_ge(sem("sh_hi"), t + 1)
                    sh = SH2 if t % 2 == 0 else SH2B
                    dve.tensor_tensor(sh[:, 1, :], PS[:, 0 if t % 2 == 0 else 5, :], sh[:, 0, :], ALU.subtract
                                      ).then_inc(sem("sh"), 1)
                if t < NT:
                    link(dve.tensor_scalar(AT[:, t, :], AT[:, t, :], 0.0, None, ALU.is_equal, saturate=False))
                    blk = AT[:, t, t * P:(t + 1) * P]
                    dve.scalar_tensor_tensor(out=blk, in0=ident[:], scalar=DN[:, t:t + 1], in1=blk, op0=ALU.mult,
                                             op1=ALU.add, saturate=False).then_inc(sem("at_back"), 1)
                if t >= 1:
                    gru_new(NT + t, t - 1, TRZ2[:, (t - 1) % 2, :], GT2[:, (t - 1) % 2, :])
                if t >= NORM_LAG:
                    dve.wait_ge(sem("gru_x"), NT + t - NORM_LAG + 1)
                    norm_stats(2, t - NORM_LAG)
                for part, (t0, t1) in enumerate(NORM2[:-1]):
                    if t == t1 + NORM_LAG:
                        norm_var(2, part)
                    if t == t1 + NORM_LAG + 1:
                        norm_scales(2, part)
                for b in norm2_blocks(t - 1):
                    low_half(b)
            for b in norm2_blocks(NT):
                low_half(b)
            for t in range(NT - NORM_LAG + 1, NT):
                dve.wait_ge(sem("gru_x"), NT + t + 1)
                norm_stats(2, t)
            norm_var(2, len(NORM2) - 1)
            norm_scales(2, len(NORM2) - 1)
            for b in range(NORM2[-1][0], NT):
                low_half(b)
            for t in range(NT + 1):
                if t < NT:
                    dve.wait_ge(sem("agg"), t + 1)
                    link(dve.tensor_scalar(ln[:, 4, t:t + 1], PS[:, AGG_BANK[t % 4], D:D + 1], 1.0, None, ALU.add))
                    dve.reciprocal(ln[:, 3, t:t + 1], ln[:, 4, t:t + 1]).then_inc(sem("rdeg"), 1)
                if t >= 1:
                    dve.wait_ge(sem("lin"), t)
                    dve.tensor_tensor(X[:, t - 1, :], X[:, t - 1, :], PS[:, 3 + (t - 1) % 2, 0:D], ALU.add
                                      ).then_inc(sem("x_l2"), 1)
            with dve.If(layer3_needed(dve) == 1):
                dve.wait_ge(sem("x_l2"), NT)
                for t in range(NT):
                    norm_stats(3, t)
                norm_var(3)
                norm_scales(3)
                dve.wait_ge(sem("w3"), 32)
                for t in range(NT):
                    dve.wait_ge(sem("msg_mm"), t + 1)
                    dve.tensor_tensor(MSG[:, t, :], PS[:, 2 + t % 2, 0:D], B3, ALU.add).then_inc(sem("msg"), 1)

                def weights(m, nb):
                    dve.wait_ge(sem("sens"), m + 1)
                    if m >= 3:
                        dve.wait_ge(sem("w_used"), m - 2)
                    dve.scalar_tensor_tensor(out=WT[:, m % 3, 0:nb * P], in0=DIST[:, m % 4, 0:nb * P], scalar=1.0,
                                             in1=RCP[:, m % 2, 0:nb * P], op0=ALU.is_lt, op1=ALU.mult
                                             ).then_inc(sem("w_built"), 1)

                m = 0
                for g, (b0, nb) in enumerate(G0):
                    for j in range(NT):
                        dve.wait_ge(sem(f"stg{m % 4}"), stg_before[m % 4] + 16 * (m // 4 + 1))
                        if m >= 2:
                            dve.wait_ge(sem("w_built"), m - 1)
                        dve.tensor_scalar(RCP[:, m % 2, 0:nb * P], DIST[:, m % 4, 0:nb * P], 0.0, NEAR_ZERO,
                                          ALU.is_equal, ALU.mult).then_inc(sem("near0"), 1)
                        dve.wait_ge(sem("no_zero"), m + 1)
                        dve.reciprocal(RCP[:, m % 2, 0:nb * P], RCP[:, m % 2, 0:nb * P]).then_inc(sem("rcp"), 1)
                        if j >= 1:
                            weights(m - 1, nb)
                        m += 1
                    weights(m - 1, nb)
                    for k in range(nb):
                        dve.wait_ge(sem("bank_full3"), b0 + k + 1)
                        dve.tensor_tensor(X[:, b0 + k, :], X[:, b0 + k, :], PS[:, k, 0:D], ALU.add).then_inc(sem("x_l3"), 1)
            with dve.Else():
                dve.nop()

        @block.tensor
        def _(pe):
            pe.wait_ge(sem("w0"), 160)
            for kc in range(DC):
                for c in range(DC):
                    ins = pe.matmul(PS[:, 4, kc * 8:kc * 8 + 8], WMT[:, c, kc * P:(kc + 1) * P], ALR[:, c, :],
                                    start=(c == 0), stop=(c == DC - 1))
            ins.then_inc(sem("wal_mm"), 1)
            pe.wait_ge(sem("consts"), 1)

            def transposes(t):
                pe.wait_ge(sem("h"), t + 1)
                if t >= 2:
                    pe.wait_ge(sem("hT"), t - 1)
                for c in range(DC):
                    ins = pe.transpose(PS[:, t % 2, c * P:(c + 1) * P], HS[:, t % 2, c * P:(c + 1) * P], ident[:])
                ins.then_inc(sem("h_tr"), 1)

            transposes(0)
            for t in range(NT):
                if t + 1 < NT:
                    transposes(t + 1)
                pe.wait_ge(sem("hT"), t + 1)
                if t == 0:
                    pe.wait_ge(sem("wal"), 1)
                if t >= 2:
                    pe.wait_ge(sem("htf"), t - 1)
                for c in range(DC):
                    pe.matmul(PS[:, 5, t * 8:t * 8 + 8], HTS[:, t % 2, c * P:(c + 1) * P], WAL[:, c, :],
                              start=(c == 0), stop=(c == DC - 1))
                for c in range(DC):
                    ins = pe.matmul(PS[:, 2 + t % 2, 0:D], HTS[:, t % 2, c * P:(c + 1) * P], WM[:, c, :],
                                    start=(c == 0), stop=(c == DC - 1))
                ins.then_inc(sem("ht_mm"), 1)
            pe.wait_ge(sem("elc"), 1)
            pe.transpose(PS[0:NT * H0, 6, 0:P], ELC, ident[:]).then_inc(sem("elT_mm"), 1)
            pe.wait_ge(sem("el_t"), 1)
            for g, (b0, nb) in enumerate(G0):
                for js in rounds(2):
                    if g == 0:
                        pe.wait_ge(sem("stg_cast"), js[-1] // 2 + 1)
                        if js[-1] > 0:
                            pe.wait_ge(sem("stg_cast_pool"), (js[-1] + 1) // 2)
                    else:
                        pe.wait_ge(sem("stg_used"), (g - 1) * NT + js[-1] + 1)
                    if g == 0:
                        pe.wait_ge(sem("mov"), js[-1] + 1)
                    for k in range(nb):
                        if js[0] == 0 and g >= 1:
                            pe.wait_ge(sem("bank_free"), min(banks_before[(g, 0)], banks_before[(g, 0)] - G0[g - 1][1] + k + 1))
                        for j in js:
                            for q in range(2):
                                ins = pe.matmul(PS[:, k, 0:4 * C0], AT[:, j, (b0 + k) * P:(b0 + k + 1) * P],
                                                MOV[:, j, :, q, C0:2 * C0], start=(j == 0 and q == 0),
                                                stop=(j == NT - 1 and q == 1))
                        if js[-1] == NT - 1:
                            ins.then_inc(sem("bank_full"), 1)
                for h in range(H0):
                    if (g, h) == (len(G0) - 1, H0 - 1):
                        pe.wait_ge(sem("w1"), 32)
                        for kc in range(DC):
                            for hh in range(H1):
                                for c in range(DC):
                                    ins = pe.matmul(PS[:, 7, kc * H1 + hh:kc * H1 + hh + 1],
                                                    GWT[:, hh * DC + c, kc * P:(kc + 1) * P],
                                                    A1[:, c, hh:hh + 1], start=(c == 0), stop=(c == DC - 1))
                        ins.then_inc(sem("u_mm"), 1)
                    m = (g * H0 + h) * NT
                    for js in rounds(4):
                        pe.wait_ge(sem("masks_built"), m + js[-1] + 1)
                        for k in range(nb):
                            if js[0] == 0:
                                pe.wait_ge(sem("bank_free"), banks_before[(g, h)] + k + 1)
                            for j in js:
                                ins = pe.matmul(PS[:, k, 0:4 * C0], MASK[:, (m + j) % NMASK, k * P:(k + 1) * P],
                                                MOV[:, j, h, :, :].rearrange("p q c -> p (q c)"), start=(j == 0), stop=(j == NT - 1))
                                if j == NT - 1:
                                    ins.then_inc(sem("bank_full"), 1)
                                elif k == nb - 1:
                                    ins.then_inc(sem("mask_used"), 1)
            pe.wait_ge(sem("bank_free"), banks_before[(len(G0) - 1, H0)] + G0[-1][1])

            def h1_transposes(t):
                pe.wait_ge(sem("h1"), t + 1)
                if t >= 2:
                    pe.wait_ge(sem("h1T"), t - 1)
                for c in range(DC):
                    ins = pe.transpose(PS[:, t % 2, c * P:(c + 1) * P], H32[:, t, c * P:(c + 1) * P], ident[:])
                ins.then_inc(sem("h1_tr"), 1)

            def support_mm(t, j):
                if t == 0:
                    pe.wait_ge(sem("lo1"), j + 1)
                if t == 0 and j == 0:
                    pe.wait_ge(sem("diag0"), NT)
                for q in range(2):
                    ins = pe.matmul(PS[:, 5, 0:D], AT[:, j, t * P:(t + 1) * P], HHL[:, j, q, 0:D],
                                    start=(j == 0 and q == 0), stop=(j == NT - 1 and q == 1))
                if j == NT - 1:
                    ins.then_inc(sem("ns"), 1)

            h1_transposes(0)
            pe.wait_ge(sem("u1"), 1)
            for t in range(NT):
                if t + 1 < NT:
                    h1_transposes(t + 1)
                pe.wait_ge(sem("h1T"), t + 1)
                for c in range(DC):
                    ins = pe.matmul(PS[:, 2, t * H1:(t + 1) * H1], HT1[:, t % 2, c * P:(c + 1) * P],
                                    U1[:, c, :], start=(c == 0), stop=(c == DC - 1))
                ins.then_inc(sem("hu_mm"), 1)
                if t >= 8:
                    support_mm(0, t - 8)
            for j in range(NT - 8, NT):
                support_mm(0, j)
            pe.wait_ge(sem("up"), 1)
            for t in range(NT):
                for j in range(NT):
                    ins = pe.matmul(PS[:, 4, t * 3 * H1:(t + 1) * 3 * H1], AT[:, j, t * P:(t + 1) * P], UP[:, j, 0:3 * H1],
                                    start=(j == 0), stop=(j == NT - 1))
            ins.then_inc(sem("e_mm"), 1)
            pe.wait_ge(sem("e2"), 1)
            pe.transpose(PS[0:NT * H1, 7, 0:P], E1[:].rearrange("p t h -> p (t h)"), ident[:]).then_inc(sem("eT_mm"), 1)
            pe.wait_ge(sem("et"), 1)
            pe.wait_ge(sem("lo1"), NT)
            pe.wait_ge(sem("we"), 48)
            pe.wait_ge(sem("bias_e"), 1)
            pe.wait_ge(sem("consts"), 5)

            def gru_mm(count, t, sh, wih, whh, bias, between=None):
                pe.wait_ge(sem("sh"), count)
                if count >= 3:
                    pe.wait_ge(sem("trz"), count - 2)
                    pe.wait_ge(sem("u"), count - 2)
                rz = PS[:, 1 + t % 2, :]
                for c in range(DC):
                    pe.matmul(rz, sh[:, c * P:(c + 1) * P], wih[:, c, 0:2 * D], start=(c == 0), stop=False)
                    pe.matmul(rz, sh[:, (DC + c) * P:(DC + c + 1) * P], whh[:, c, 0:2 * D], start=False, stop=False)
                pe.matmul(rz, ones3[0:3, :], bias[0:3, 0:2 * D], start=False, stop=True).then_inc(sem("rz_mm"), 1)
                if between:
                    between()
                for q, w in ((0, wih), (1, whh)):
                    o = PS[:, 3 + t % 2, q * D:(q + 1) * D]
                    for c in range(DC):
                        pe.matmul(o, sh[:, (DC * q + c) * P:(DC * q + c + 1) * P], w[:, c, 2 * D:3 * D],
                                  start=(c == 0), stop=False)
                    ins = pe.matmul(o, ones3[0:3, :], bias[0:3, (2 + q) * D:(3 + q) * D], start=False, stop=True)
                ins.then_inc(sem("nb_mm"), 1)

            def row_maxima():
                pe.wait_ge(sem("e2"), 2)
                pe.transpose(PS[0:NT * H1, 5, 0:P], E2[:], ident[:]).then_inc(sem("eT_mm"), 1)

            for t in range(NT + 1):
                if t >= 1:
                    pe.wait_ge(sem("ns_sb"), t)
                    if t >= 2:
                        pe.wait_ge(sem("sh"), t - 1)
                    for c in range(DC):
                        pe.transpose(PS[:, 0, c * P:(c + 1) * P], NSS[:, c * P:(c + 1) * P], ident[:])
                    for c in range(DC):
                        ins = pe.transpose(PS[:, 0, (DC + c) * P:(DC + c + 1) * P], H32[:, t - 1, c * P:(c + 1) * P], ident[:])
                    ins.then_inc(sem("tb"), 1)
                if 1 <= t < NT:
                    for j in range(NT):
                        support_mm(t, j)
                if t >= 1:
                    gru_mm(t, t - 1, SH, WIH, WHH, BIAS, row_maxima if t == NT else None)
                    if t >= 2:
                        pe.wait_ge(sem("hw_lo"), H1 * (t - 1))
                    for h in range(H1):
                        for c in range(DC):
                            ins = pe.matmul(PS[:, 6 + h // 2, (h % 2) * D:(h % 2 + 1) * D],
                                            SH[:, (DC + c) * P:(DC + c + 1) * P], GW[:, h * DC + c, :],
                                            start=(c == 0), stop=(c == DC - 1))
                    ins.then_inc(sem("hw_mm"), 1)
            pe.wait_ge(sem("mt"), 1)
            pe.wait_ge(sem("hw_lo"), H1 * NT)
            pe.wait_ge(sem("u"), NT)
            for h in range(H1):
                pe.wait_ge(sem("hw_f"), [1, 3, 4][h])
                for g, (b0, nb) in enumerate(G0):
                    m = (h * len(G0) + g) * NT
                    for js in rounds(2):
                        pe.wait_ge(sem("p_exp"), m + js[-1] + 1)
                        if m + js[-1] == HW_EARLY:
                            pe.wait_ge(sem("hw_f"), 2)
                        for k in range(nb):
                            if js[0] == 0 and (h, g) != (0, 0):
                                nb_old = G0[g - 1][1]
                                pe.wait_ge(sem("es_done"), h * NT + b0 - nb_old + min(k + 1, nb_old))
                            for j in js:
                                weights, w = PW[:, (m + j) % NRING, k * P:(k + 1) * P], HW[:, h % 2, j, :]
                                pe.matmul(PS[:, k, 0:D + 1], weights, w[:, 0:D + 1], start=(j == 0), stop=False)
                                ins = pe.matmul(PS[:, k, 0:D + 1], weights, w[:, D + 2:2 * D + 3], start=False,
                                                stop=(j == NT - 1))
                                if j == NT - 1:
                                    ins.then_inc(sem("bank_full1"), 1)
                                elif k == nb - 1:
                                    ins.then_inc(sem("p_used"), 1)
                        if js[-1] == NT - 1:
                            pe.wait_ge(sem("bank_full1"), h * NT + b0 + nb)
                            pe.sem_inc(sem("p_used"), 1)
            pe.wait_ge(sem("wn_split"), 2)
            pe.wait_ge(sem("h_back"), 16)

            def node_mm(t, sh):
                pe.wait_ge(sem("sh"), NT + t + 1)
                pe.wait_ge(sem("trz"), NT + t - 1)
                pe.wait_ge(sem("u"), NT + t - 1)
                rz = PS[:, 1 + t % 2, :]
                for q, w in enumerate((WIH2S, WHH2S)):
                    for c in range(DC):
                        for a, b in ((0, 0), (0, 1), (1, 0)):
                            pe.matmul(rz, sh[:, a, (DC * q + c) * P:(DC * q + c + 1) * P], w[:, c, 0:2, b, :],
                                      start=(q == 0 and c == 0 and a + b == 0), stop=False)
                pe.matmul(rz, ones3[0:3, :], BIAS2[0:3, 0:2 * D], start=False, stop=True).then_inc(sem("rz_mm"), 1)
                for q, w in enumerate((WIH2S, WHH2S)):
                    o = PS[:, 3 + t % 2, q * D:(q + 1) * D]
                    for c in range(DC):
                        for a, b in ((0, 0), (0, 1), (1, 0)):
                            pe.matmul(o, sh[:, a, (DC * q + c) * P:(DC * q + c + 1) * P], w[:, c, 2, b, :],
                                      start=(c == 0 and a + b == 0), stop=False)
                    ins = pe.matmul(o, ones3[0:3, :], BIAS2[0:3, (2 + q) * D:(3 + q) * D], start=False, stop=True)
                ins.then_inc(sem("nb_mm"), 1)

            def node_transposes(t):
                if t >= 2:
                    pe.wait_ge(sem("sh"), NT + t - 1)
                bank = 0 if t % 2 == 0 else 5
                for c in range(DC):
                    pe.transpose(PS[:, bank, c * P:(c + 1) * P], ES[:, t, c * P:(c + 1) * P], ident[:])
                for c in range(DC):
                    ins = pe.transpose(PS[:, bank, (DC + c) * P:(DC + c + 1) * P], H32B[:, t, c * P:(c + 1) * P], ident[:])
                ins.then_inc(sem("tb"), 1)

            pe.wait_ge(sem("es_done"), NT * (H1 - 1) + G0[-1][0] + 1)
            node_transposes(0)
            pe.wait_ge(sem("es_done"), NT * H1)
            pe.wait_ge(sem("bias_n"), 1)
            for t in range(NT):
                if t + 1 < NT:
                    node_transposes(t + 1)
                node_mm(t, SH2 if t % 2 == 0 else SH2B)
            pe.wait_ge(sem("at_back"), NT)
            pe.wait_ge(sem("hhl_pad"), 2)

            def sum_neighbours(t, j0, j1):
                o = PS[:, AGG_BANK[t % 4], :]
                for j in range(j0, j1):
                    if t < 4:
                        pe.wait_ge(sem("lo2"), j + 1)
                    pe.matmul(o[:, 0:D + 1], AT[:, j, t * P:(t + 1) * P], HHL2[:, j, 0, 0:D + 1], start=(j == 0), stop=False)
                    ins = pe.matmul(o[:, 0:D], AT[:, j, t * P:(t + 1) * P], HHL2[:, j, 1, 0:D], start=False,
                                    stop=(j == NT - 1))
                if j1 == NT:
                    ins.then_inc(sem("agg"), 1)

            pe.wait_ge(sem("sh"), 2 * NT)
            for t in range(4):
                if t == 3:
                    pe.wait_ge(sem("trz"), 2 * NT - 1)
                sum_neighbours(t, 0, NORM2[-1][0])
            for t in range(NT + 1):
                if t >= 1:
                    pe.wait_ge(sem("nei"), t)
                    if t >= 2:
                        pe.wait_ge(sem("sh3"), t - 1)
                    for c in range(DC):
                        pe.transpose(PS[:, 0, c * P:(c + 1) * P], H2[:, t - 1, c * P:(c + 1) * P], ident[:])
                    for c in range(DC):
                        ins = pe.transpose(PS[:, 0, (DC + c) * P:(DC + c + 1) * P], NEI[:, c * P:(c + 1) * P], ident[:])
                    ins.then_inc(sem("tb2"), 1)
                if t < 4:
                    sum_neighbours(t, NORM2[-1][0], NT)
                elif t < NT:
                    sum_neighbours(t, 0, NT)
                if t >= 1:
                    pe.wait_ge(sem("sh3"), t)
                    if t == 1:
                        pe.wait_ge(sem("w2"), 16)
                    if t >= 3:
                        pe.wait_ge(sem("x_l2"), t - 2)
                    for c in range(2 * DC):
                        ins = pe.matmul(PS[:, 3 + (t - 1) % 2, 0:D], SH3[:, c * P:(c + 1) * P], W2[:, c, :],
                                        start=(c == 0), stop=(c == 2 * DC - 1))
                    ins.then_inc(sem("lin"), 1)
            with pe.If(layer3_needed(pe) == 1):
                pe.wait_ge(sem("w3"), 32)

                def h3_transposes(t):
                    pe.wait_ge(sem("h3"), t + 1)
                    if t >= 2:
                        pe.wait_ge(sem("h3T"), t - 1)
                    for c in range(DC):
                        ins = pe.transpose(PS[:, t % 2, c * P:(c + 1) * P], H3[:, t, c * P:(c + 1) * P], ident[:])
                    ins.then_inc(sem("h3_tr"), 1)

                h3_transposes(0)
                for t in range(NT):
                    if t + 1 < NT:
                        h3_transposes(t + 1)
                    pe.wait_ge(sem("h3T"), t + 1)
                    if t >= 2:
                        pe.wait_ge(sem("msg"), t - 1)
                    for c in range(DC):
                        ins = pe.matmul(PS[:, 2 + t % 2, 0:D], SH4[:, t % 2, c * P:(c + 1) * P], W3[:, c, :],
                                        start=(c == 0), stop=(c == DC - 1))
                    ins.then_inc(sem("msg_mm"), 1)
                pe.wait_ge(sem("msg"), NT)
                m = 0
                for g, (b0, nb) in enumerate(G0):
                    for j in range(NT):
                        pe.wait_ge(sem("w_built"), m + 1)
                        for k in range(nb):
                            if j == 0 and g >= 1:
                                nb_old = G0[g - 1][1]
                                pe.wait_ge(sem("x_l3"), b0 - nb_old + min(k + 1, nb_old))
                            ins = pe.matmul(PS[:, k, 0:D], WT[:, m % 3, k * P:(k + 1) * P], MSG[:, j, :],
                                            start=(j == 0), stop=(j == NT - 1))
                            if j == NT - 1:
                                ins.then_inc(sem("bank_full3"), 1)
                            elif k == nb - 1:
                                ins.then_inc(sem("w_used"), 1)
                        if j == NT - 1:
                            pe.wait_ge(sem("bank_full3"), b0 + nb)
                            pe.sem_inc(sem("w_used"), 1)
                        m += 1
            with pe.Else():
                pe.nop()


def kernel(**inputs):
    import numpy as _np
    import concourse.bacc as _bacc
    from concourse import mybir as _mybir
    from concourse.bass_utils import run_bass_kernel_spmd as _run

    n = inputs["x"].shape[0]
    padded = -(-n // 128) * 128

    def padded_to(a, rows, cols):
        out = _np.zeros((rows, cols), a.dtype)
        out[:a.shape[0], :a.shape[1]] = a
        return out

    a = {k: _np.asarray(v) for k, v in inputs.items()}
    arrays = {
        "x": padded_to(a["x"], padded, a["x"].shape[1]),
        "adjT": padded_to(a["adj"].T, padded, padded),
        "Wm": a["L0_gnn_Wm"],
        "WmT": a["L0_gnn_Wm"].T,
        "al": a["L0_gnn_al"],
        "ar": a["L0_gnn_ar"],
        "adj": padded_to(a["adj"], padded, padded),
        "diag": padded_to(_np.diagonal(a["adj"])[None], 1, padded).reshape(padded // 128, 128).T,
        "gatW": a["L1_gnn_gat_W"],
        "gatWT": a["L1_gnn_gat_W"].transpose(0, 2, 1),
        "gat_a": a["L1_gnn_gat_a"][:, :256, 0].reshape(3, 2, 128).transpose(2, 1, 0),
        "edge_WihT": a["L1_gnn_edge_Wih"].T,
        "edge_WhhT": a["L1_gnn_edge_Whh"].T,
        "edge_bih": a["L1_gnn_edge_bih"],
        "edge_bhh": a["L1_gnn_edge_bhh"],
        "node_WihT": a["L1_gnn_node_Wih"].T,
        "node_WhhT": a["L1_gnn_node_Whh"].T,
        "node_bih": a["L1_gnn_node_bih"],
        "node_bhh": a["L1_gnn_node_bhh"],
        "W2T": a["L2_gnn_W"].T,
        "W3": a["L3_gnn_W"],
        "B3": a["L3_gnn_B"],
    }
    arrays = {k: _np.ascontiguousarray(v) for k, v in arrays.items()}
    nc = _bacc.Bacc("TRN2", target_bir_lowering=False, num_devices=1)
    t_in = {k: nc.dram_tensor(f"in_{k}", v.shape, _mybir.dt.from_np(v.dtype), kind="ExternalInput").ap()
            for k, v in arrays.items()}
    out = nc.dram_tensor("out", (n, a["x"].shape[1]), _mybir.dt.float32, kind="ExternalOutput").ap()
    gnn_stack_kernel(nc, t_in, out)
    r = _run(nc, [{f"in_{k}": v for k, v in arrays.items()}], core_ids=[0])
    return r.results[0]["out"]
```
